# Optimizing a Trainium2 kernel written in Bass

```python
import numpy as np
import jax
import jax.numpy as jnp

def _softmax(x, axis=-1):
    return jax.nn.softmax(x, axis=axis)

def _gelu(x):
    return jax.nn.gelu(x, approximate=True)

def _silu(x):
    return jax.nn.silu(x)

def _sigmoid(x):
    return jax.nn.sigmoid(x)

def _layernorm(x, axis=-1, eps=1e-05):
    m = jnp.mean(x, axis=axis, keepdims=True)
    v = jnp.var(x, axis=axis, keepdims=True)
    return (x - m) / jnp.sqrt(v + eps)

def _scatter_add(tgt, idx, src, axis=0):
    return tgt.at[idx].add(src)

def _segment_sum(src, seg, n):
    return jax.ops.segment_sum(src, seg, n)
kernel_name = 'mk_xattn_ffn_d2_seqx_r8_e0443e'

def setup_inputs(seed: int=0):
    np.random.seed(seed)
    _w = jnp.asarray

    def _rec_inputs():
        import jax
        import jax.numpy as jnp
        _rk = jax.random.key(seed)
        x = -0.0002928 + 1 * jax.random.normal(jax.random.fold_in(_rk, 1), (4, 512, 128), jnp.float32)
        _lenS = 512 - jax.random.randint(jax.random.fold_in(_rk, 7), (4,), 0, max(1, 512 // 4) + 1, jnp.int32)
        _lenS2 = 32 - jax.random.randint(jax.random.fold_in(_rk, 8), (4,), 0, max(1, 32 // 4) + 1, jnp.int32)
        _ctx_1024P = jax.random.normal(jax.random.fold_in(_rk, 11), (4, 16, 128), jnp.float32)
        _ctx_1024c = jax.random.dirichlet(jax.random.fold_in(_rk, 511), 0.3 * jnp.ones((16,), jnp.float32), (4, 32))
        _ctx_1024t = jnp.einsum('bsk,bkd->bsd', _ctx_1024c, _ctx_1024P)
        _ctx_1024t = _ctx_1024t * jax.lax.rsqrt(jnp.mean(jnp.square(_ctx_1024t)) + 1e-12) * 0.953939
        ctx_1024 = -1.39393e-06 + 0.999914 * (_ctx_1024t + 0.3 * jax.random.normal(jax.random.fold_in(_rk, 611), (4, 32, 128), jnp.float32))
        return (x, ctx_1024)
    x, ctx_1024 = _rec_inputs()

    def _L0_xattn_setup():
        import jax, jax.numpy as jnp
        import numpy as np
        B, SQ, SKV, D, H = (2, 256, 256, 128, 16)
        HD = D // H
        ROPE_BASE = 10000.0

        def _rope_interleaved(x):
            s, hd = (x.shape[1], x.shape[-1])
            dim = hd // 2
            freqs = jnp.exp(-jnp.arange(dim, dtype=x.dtype) * jnp.log(jnp.asarray(ROPE_BASE, x.dtype)) / dim)
            ang = jnp.arange(s, dtype=x.dtype)[:, None] * freqs[None, :]
            cos = jnp.cos(ang)[None, :, None, :]
            sin = jnp.sin(ang)[None, :, None, :]
            xe, xo = (x[..., ::2], x[..., 1::2])
            re = xe * cos - xo * sin
            ro = xe * sin + xo * cos
            return jnp.stack([re, ro], axis=-1).reshape(x.shape)
        key = jax.random.key(seed)
        ks = jax.random.split(key, 6)
        s = 1.0 / np.sqrt(D)
        return {'x_q': jax.random.normal(ks[0], (B, SQ, D), jnp.float32), 'x_kv': jax.random.normal(ks[1], (B, SKV, D), jnp.float32), 'wq': jax.random.normal(ks[2], (D, D), jnp.float32) * s, 'bq': jnp.zeros((D,), jnp.float32), 'wk': jax.random.normal(ks[3], (D, D), jnp.float32) * s, 'bk': jnp.zeros((D,), jnp.float32), 'wv': jax.random.normal(ks[4], (D, D), jnp.float32) * s, 'bv': jnp.zeros((D,), jnp.float32), 'wo': jax.random.normal(ks[5], (D, D), jnp.float32) * s, 'bo': jnp.zeros((D,), jnp.float32)}
    _L0_xattn_all = _L0_xattn_setup()
    _L0_xattn_in = {k: v for k, v in _L0_xattn_all.items() if k in ('wq', 'bq', 'wk', 'bk', 'wv', 'bv', 'wo', 'bo')}
    del _L0_xattn_all

    def _L0_ffn_setup():
        import jax, jax.numpy as jnp
        import numpy as np
        B, S, H = (4, 256, 128)
        E = 8
        GS = 2
        NG = E // GS
        F = int(H * 4 * (2.0 / 3.0))
        key = jax.random.key(seed)
        ks = jax.random.split(key, 7)
        sc_h = 1.0 / np.sqrt(H)
        sc_f = 1.0 / np.sqrt(F)
        return {'x': jax.random.normal(ks[0], (B, S, H), dtype=jnp.float32), 'Wr': jax.random.normal(ks[1], (H, E), dtype=jnp.float32) * sc_h, 'br': jnp.zeros((E,), dtype=jnp.float32), 'W_up': jax.random.normal(ks[2], (NG, H, F), dtype=jnp.float32) * sc_h, 'b_up': jax.random.normal(ks[3], (NG, F), dtype=jnp.float32) * 0.01, 'W_down': jax.random.normal(ks[4], (E, F, H), dtype=jnp.float32) * sc_f, 'b_down': jax.random.normal(ks[5], (E, H), dtype=jnp.float32) * 0.01}
    _L0_ffn_all = _L0_ffn_setup()
    _L0_ffn_in = {k: v for k, v in _L0_ffn_all.items() if k in ('Wr', 'br', 'W_up', 'b_up', 'W_down', 'b_down')}
    del _L0_ffn_all

    def _L1_xattn_setup():
        import jax, jax.numpy as jnp
        import numpy as np
        DIM = 128
        NHEADS = 8
        HEAD_DIM = DIM // NHEADS
        ROPE_BASE = 10000.0

        def _rope(t, positions):
            d = t.shape[-1]
            inv_freq = 1.0 / ROPE_BASE ** (jnp.arange(0, d, 2, dtype=jnp.float32) / d)
            freqs = positions[:, None].astype(jnp.float32) * inv_freq
            emb = jnp.concatenate([freqs, freqs], axis=-1)
            cos = jnp.cos(emb)[None, :, None, :].astype(t.dtype)
            sin = jnp.sin(emb)[None, :, None, :].astype(t.dtype)
            t1, t2 = jnp.split(t, 2, axis=-1)
            rot = jnp.concatenate([-t2, t1], axis=-1)
            return t * cos + rot * sin
        key = jax.random.key(seed)
        k1, k2, k3, k4, k5 = jax.random.split(key, 5)
        B, T, S = (2, 256, 375)
        w_std = 1.0 / np.sqrt(DIM)
        return {'x': jax.random.normal(k1, (B, T, DIM), dtype=jnp.float32), 'xmel': jax.random.normal(k2, (B, S, DIM), dtype=jnp.float32), 'Wq': jax.random.normal(k3, (DIM, DIM), dtype=jnp.float32) * w_std, 'Wkv': jax.random.normal(k4, (2 * DIM, DIM), dtype=jnp.float32) * w_std, 'Wout': jax.random.normal(k5, (DIM, DIM), dtype=jnp.float32) * w_std}
    _L1_xattn_all = _L1_xattn_setup()
    _L1_xattn_in = {k: v for k, v in _L1_xattn_all.items() if k in ('Wq', 'Wkv', 'Wout')}
    del _L1_xattn_all

    def _L1_ffn_setup():
        import jax, jax.numpy as jnp
        import numpy as np
        NUM_GEMMS = 8
        HIDDEN = 128
        INTER = 512
        key = jax.random.key(seed)
        k_x, k_w1, k_b1, k_w2, k_b2 = jax.random.split(key, 5)
        x = jax.random.normal(k_x, (8, 256, HIDDEN), dtype=jnp.float32)
        s1 = 1.0 / np.sqrt(HIDDEN)
        s2 = 1.0 / np.sqrt(INTER)
        W1 = jax.random.uniform(k_w1, (NUM_GEMMS, INTER, HIDDEN), jnp.float32, -s1, s1)
        b1 = jax.random.uniform(k_b1, (NUM_GEMMS, INTER), jnp.float32, -s1, s1)
        W2 = jax.random.uniform(k_w2, (NUM_GEMMS, HIDDEN, INTER), jnp.float32, -s2, s2)
        b2 = jax.random.uniform(k_b2, (NUM_GEMMS, HIDDEN), jnp.float32, -s2, s2)
        return {'x': x, 'W1': W1, 'b1': b1, 'W2': W2, 'b2': b2}
    _L1_ffn_all = _L1_ffn_setup()
    _L1_ffn_in = {k: v for k, v in _L1_ffn_all.items() if k in ('W1', 'b1', 'W2', 'b2')}
    del _L1_ffn_all
    return {'x': x, 'ctx_1024': ctx_1024, 'L0_xattn_wq': _L0_xattn_in['wq'], 'L0_xattn_bq': _L0_xattn_in['bq'], 'L0_xattn_wk': _L0_xattn_in['wk'], 'L0_xattn_bk': _L0_xattn_in['bk'], 'L0_xattn_wv': _L0_xattn_in['wv'], 'L0_xattn_bv': _L0_xattn_in['bv'], 'L0_xattn_wo': _L0_xattn_in['wo'], 'L0_xattn_bo': _L0_xattn_in['bo'], 'L0_ffn_Wr': _L0_ffn_in['Wr'], 'L0_ffn_br': _L0_ffn_in['br'], 'L0_ffn_W_up': _L0_ffn_in['W_up'], 'L0_ffn_b_up': _L0_ffn_in['b_up'], 'L0_ffn_W_down': _L0_ffn_in['W_down'], 'L0_ffn_b_down': _L0_ffn_in['b_down'], 'L1_xattn_Wq': _L1_xattn_in['Wq'], 'L1_xattn_Wkv': _L1_xattn_in['Wkv'], 'L1_xattn_Wout': _L1_xattn_in['Wout'], 'L1_ffn_W1': _L1_ffn_in['W1'], 'L1_ffn_b1': _L1_ffn_in['b1'], 'L1_ffn_W2': _L1_ffn_in['W2'], 'L1_ffn_b2': _L1_ffn_in['b2']}

def reference(x, ctx_1024, L0_xattn_wq, L0_xattn_bq, L0_xattn_wk, L0_xattn_bk, L0_xattn_wv, L0_xattn_bv, L0_xattn_wo, L0_xattn_bo, L0_ffn_Wr, L0_ffn_br, L0_ffn_W_up, L0_ffn_b_up, L0_ffn_W_down, L0_ffn_b_down, L1_xattn_Wq, L1_xattn_Wkv, L1_xattn_Wout, L1_ffn_W1, L1_ffn_b1, L1_ffn_W2, L1_ffn_b2):
    import jax
    import jax.numpy as jnp

    def _L0_xattn_ref(x_q, x_kv, wq, bq, wk, bk, wv, bv, wo, bo):
        import jax, jax.numpy as jnp
        import numpy as np
        B, SQ, SKV, D, H = (2, 256, 256, 128, 16)
        HD = D // H
        ROPE_BASE = 10000.0

        def _rope_interleaved(x):
            s, hd = (x.shape[1], x.shape[-1])
            dim = hd // 2
            freqs = jnp.exp(-jnp.arange(dim, dtype=x.dtype) * jnp.log(jnp.asarray(ROPE_BASE, x.dtype)) / dim)
            ang = jnp.arange(s, dtype=x.dtype)[:, None] * freqs[None, :]
            cos = jnp.cos(ang)[None, :, None, :]
            sin = jnp.sin(ang)[None, :, None, :]
            xe, xo = (x[..., ::2], x[..., 1::2])
            re = xe * cos - xo * sin
            ro = xe * sin + xo * cos
            return jnp.stack([re, ro], axis=-1).reshape(x.shape)
        b, sq, _ = x_q.shape
        skv = x_kv.shape[1]
        q = (jnp.einsum('bsd,ed->bse', x_q, wq) + bq).reshape(b, sq, H, HD)
        k = (jnp.einsum('bsd,ed->bse', x_kv, wk) + bk).reshape(b, skv, H, HD)
        v = (jnp.einsum('bsd,ed->bse', x_kv, wv) + bv).reshape(b, skv, H, HD)
        q = _rope_interleaved(q)
        k = _rope_interleaved(k)
        scores = jnp.einsum('bqhd,bkhd->bhqk', q, k) / jnp.sqrt(jnp.asarray(HD, q.dtype))
        attn = jax.nn.softmax(scores, axis=-1)
        ctx = jnp.einsum('bhqk,bkhd->bqhd', attn, v).reshape(b, sq, D)
        return jnp.einsum('bsd,ed->bse', ctx, wo) + bo

    def _L0_ffn_ref(x, Wr, br, W_up, b_up, W_down, b_down):
        import jax, jax.numpy as jnp
        import numpy as np
        B, S, H = (4, 256, 128)
        E = 8
        GS = 2
        NG = E // GS
        F = int(H * 4 * (2.0 / 3.0))
        b, s, h = x.shape
        n_tok = b * s
        k = n_tok // E
        xf = x.reshape(n_tok, h)
        logits = xf @ Wr + br
        Sm = jax.nn.softmax(logits, axis=-1)
        G_t, idx_t = jax.lax.top_k(Sm.T, k)
        G = G_t.T
        idx = idx_t.T
        tokens = xf[idx]
        group = jnp.arange(E) // GS
        Wu = W_up[group]
        bu = b_up[group]
        mid = jax.nn.silu(jnp.einsum('keh,ehf->kef', tokens, Wu) + bu)
        out = jnp.einsum('kef,efh->keh', mid, W_down) + b_down
        y = jnp.zeros_like(xf).at[idx].add(G[..., None] * out)
        return y.reshape(b, s, h)

    def _L1_xattn_ref(x, xmel, Wq, Wkv, Wout):
        import jax, jax.numpy as jnp
        import numpy as np
        DIM = 128
        NHEADS = 8
        HEAD_DIM = DIM // NHEADS
        ROPE_BASE = 10000.0

        def _rope(t, positions):
            d = t.shape[-1]
            inv_freq = 1.0 / ROPE_BASE ** (jnp.arange(0, d, 2, dtype=jnp.float32) / d)
            freqs = positions[:, None].astype(jnp.float32) * inv_freq
            emb = jnp.concatenate([freqs, freqs], axis=-1)
            cos = jnp.cos(emb)[None, :, None, :].astype(t.dtype)
            sin = jnp.sin(emb)[None, :, None, :].astype(t.dtype)
            t1, t2 = jnp.split(t, 2, axis=-1)
            rot = jnp.concatenate([-t2, t1], axis=-1)
            return t * cos + rot * sin
        B, T, C = x.shape
        S = xmel.shape[1]
        H, D = (NHEADS, C // NHEADS)
        q = (x @ Wq.T).reshape(B, T, H, D)
        kv = (xmel @ Wkv.T).reshape(B, S, 2, H, D)
        q = _rope(q, jnp.arange(T))
        k = _rope(kv[:, :, 0], jnp.arange(S))
        v = kv[:, :, 1]
        scale = (C // H) ** (-0.25)
        q = q * scale
        k = k * scale
        scores = jnp.einsum('bthd,bshd->bhts', q, k)
        attn = jax.nn.softmax(scores, axis=-1)
        out = jnp.einsum('bhts,bshd->bthd', attn, v)
        out = out.reshape(B, T, C)
        return out @ Wout.T

    def _L1_ffn_ref(x, W1, b1, W2, b2):
        import jax, jax.numpy as jnp
        import numpy as np
        NUM_GEMMS = 8
        HIDDEN = 128
        INTER = 512
        orig_shape = x.shape
        token_num = int(np.prod(orig_shape[:-1]))
        m = token_num // NUM_GEMMS
        xg = x.reshape(NUM_GEMMS, m, HIDDEN)
        h1 = jnp.einsum('gmh,goh->gmo', xg, W1) + b1[:, None, :]
        h2 = jnp.einsum('gmo,gho->gmh', h1, W2) + b2[:, None, :]
        return h2.reshape(orig_shape)
    x = x + _L0_xattn_ref(_layernorm(x, axis=-1), ctx_1024, L0_xattn_wq, L0_xattn_bq, L0_xattn_wk, L0_xattn_bk, L0_xattn_wv, L0_xattn_bv, L0_xattn_wo, L0_xattn_bo)
    x = x + _L0_ffn_ref(_layernorm(x, axis=-1), L0_ffn_Wr, L0_ffn_br, L0_ffn_W_up, L0_ffn_b_up, L0_ffn_W_down, L0_ffn_b_down)
    x = x + _L1_xattn_ref(_layernorm(x, axis=-1), ctx_1024, L1_xattn_Wq, L1_xattn_Wkv, L1_xattn_Wout)
    x = x + _L1_ffn_ref(_layernorm(x, axis=-1), L1_ffn_W1, L1_ffn_b1, L1_ffn_W2, L1_ffn_b2)
    return x

_drawn_inputs = setup_inputs


def setup_inputs(seed=0):
    import zlib

    import numpy as np

    out = dict(_drawn_inputs(seed))
    spreads = {'L0_xattn_bq': (0.0, 0.1),
     'L0_xattn_bk': (0.0, 0.444),
     'L0_xattn_bv': (0.0, 0.1),
     'L0_xattn_bo': (0.0, 0.1),
     'L0_ffn_br': (0.0, 0.1)}
    factors = {'L0_ffn_b_up': 31.069, 'L0_ffn_b_down': 8.0, 'L1_ffn_b1': 2.723, 'L1_ffn_b2': 3.125}
    for name, (base, spread) in spreads.items():
        noise = np.random.default_rng([zlib.crc32(name.encode()), seed]).standard_normal(out[name].shape)
        drawn = base * np.exp(spread * noise) if base else spread * noise
        out[name] = jnp.asarray(drawn.astype(out[name].dtype))
    for name, factor in factors.items():
        out[name] = (out[name] * factor).astype(out[name].dtype)
    return out
```

```python
from contextlib import ExitStack

import numpy as np

import concourse.bass as bass
from concourse import mybir

B, SEQ, D = 4, 512, 128
KV = 32
P = 128
N_TOK = B * SEQ
TILES = N_TOK // P
TPB = SEQ // P
HEADS = (16, 8)
EXPERTS, GROUPS = 8, 4
CAP = N_TOK // EXPERTS
HALVES = CAP // P
F = int(D * 4 * (2.0 / 3.0))
FT = (F + P - 1) // P
BIAS_ROW = 96
F_LAST = BIAS_ROW
GEMMS, INTER = 8, 512
OT = INTER // P
TPG = TILES // GEMMS
BITS = 3
STEPS = 10
CANDS = (1 << BITS) - 1
ROW = D + EXPERTS
SLOT_B = 16
EPS = 1e-5
RSQRT_MAGIC = float(0x5F3759DF)

F32, F32R = mybir.dt.float32, mybir.dt.float32r
BF16, F16 = mybir.dt.bfloat16, mybir.dt.float16
I32, U32 = mybir.dt.int32, mybir.dt.uint32
ALU = mybir.AluOpType
ACT = mybir.ActivationFunctionType
X_AXIS = mybir.AxisListType.X


def columns(**widths):
    at, out = 0, {}
    for name, width in widths.items():
        out[name] = (at, at + width)
        at += width
    return out, at


C32, C32_W = columns(ident=P, head0=16, head1=8, vmask0=P, vmask1=P, expert=P, crow=8, ones=P)
CSM, CSM_W = columns(tri=P, ones=P, neg0=4 * P, neg1=2 * P)
C16, C16_W = columns(iota=P, token=TILES * P, place=8 * P)
W_Q, W_QS, W_K, W_KS, W_V, W_O = range(6)


class Chain:

    def __init__(self, engine, semaphore):
        self.engine, self.semaphore, self.count = engine, semaphore, 0

    def step(self, instruction):
        instruction.then_inc(self.semaphore, 1)
        self.count += 1

    def settle(self):
        self.engine.wait_ge(self.semaphore, self.count)


def build(nc, ins, out):
    with ExitStack() as ctx:
        def sb(name, shape, dt=F32):
            return ctx.enter_context(nc.sbuf_tensor(name, shape, dt))

        def sem(name):
            return ctx.enter_context(nc.semaphore(name))

        bank = [ctx.enter_context(nc.psum_tensor(f"bank{i}", [P, 512], F32)) for i in range(8)]
        TX = bank[0]
        ring = bank[1:4]
        score_bank = bank[4:6]
        ctx_bank, sum_bank = bank[6], bank[7]

        dispatch = nc.dram_tensor("dispatch_rows", [N_TOK, ROW], F32).ap()
        y_even = nc.dram_tensor("y_even", [N_TOK, D], F32).ap()
        y_odd = nc.dram_tensor("y_odd", [N_TOK, D], F32).ap()

        c32 = sb("c32", [P, C32_W])
        csm = sb("csm", [P, CSM_W], F16)
        ident_bf = sb("ident_bf", [P, P], BF16)
        c16 = sb("c16", [P, C16_W], F16)
        kbits = sb("kbits", [P, STEPS * 8], I32)

        def k32(name):
            return c32[:, C32[name][0]:C32[name][1]]

        def ksm(name):
            return csm[:, CSM[name][0]:CSM[name][1]]

        def k16(name):
            return c16[:, C16[name][0]:C16[name][1]]

        w_att = [sb(f"w_att{a}", [P, 6, D]) for a in range(2)]
        b_col = sb("b_col", [P, 4])
        b_row = sb("b_row", [P, 2, D])
        rope = [sb(f"rope{a}", [P, 2, SEQ]) for a in range(2)]
        ctx_rows = sb("ctx_rows", [P, D])
        ctx_t = sb("ctx_t", [P, B, 4, KV])
        wr = sb("wr", [P, 32])
        br = sb("br", [P, 1])
        w_up = sb("w_up", [P, GROUPS, FT, P])
        b_up = sb("b_up", [P, GROUPS, FT])
        w_down = sb("w_down", [P, EXPERTS, FT, D])
        w1 = sb("w1", [P, GEMMS, OT, D])
        w2t = sb("w2t", [P, GEMMS, OT, D])
        b1c = sb("b1c", [P, OT, 32])
        b2b = sb("b2b", [P, GEMMS, D])
        w21 = sb("w21", [P, GEMMS, D])
        c21 = sb("c21", [P, GEMMS, D])
        c_raw = sb("c_raw", [P, 2 * D])
        c_one = sb("c_one", [P, GEMMS, D])

        x_in = sb("x_in", [P, TILES, D])
        x_mid = sb("x_mid", [P, TILES, D])
        x_add = sb("x_add", [P, TILES, D])
        xn = sb("xn", [P, TILES, D])
        xn_t = sb("xn_t", [P, TILES, P])
        stats = sb("stats", [P, TILES, 6])
        mean = sb("mean", [P, TILES])
        rstd = sb("rstd", [P, TILES])
        ln_a = sb("ln_a", [P, TILES])
        ln_v = sb("ln_v", [P, TILES])

        k_rot = sb("k_rot", [P, B, KV])
        k_a = sb("k_a", [P, B, KV])
        k_b = sb("k_b", [P, B, KV])
        k_bd = sb("k_bd", [P, B, 512])
        k_bdr = sb("k_bdr", [P, B, 512], F32R)
        v_raw = sb("v_raw", [P, B, D])
        v_bd = sb("v_bd", [P, B, D])
        q_a = sb("q_a", [P, SEQ])
        q_b = sb("q_b", [P, SEQ])
        q_t = [sb(f"q_t{i}", [P, SEQ]) for i in range(2)]
        q_tr = [sb(f"q_tr{i}", [P, SEQ], F32R) for i in range(2)]
        m_max = sb("m_max", [P, TPB, 16])
        m_hl = [sb(f"m_hl{i}", [P, TPB, 32], BF16) for i in range(2)]
        m_t = [sb(f"m_t{i}", [P, SEQ], BF16) for i in range(2)]
        probs_all = sb("probs", [P, 4, SEQ])
        probs = [probs_all[:, i, :] for i in range(4)]
        recip = sb("recip", [P, SEQ])
        att_t = [sb(f"att_t{i}", [P, SEQ]) for i in range(2)]

        logit_t = sb("logit_t", [P, SEQ])
        logit = sb("logit", [P, TILES, EXPERTS])
        l_max = sb("l_max", [P, TILES])
        l_exp = sb("l_exp", [P, TILES, EXPERTS])
        l_sum = sb("l_sum", [P, TILES])
        weight = sb("weight", [P, TILES, EXPERTS])
        cand = sb("cand", [P, EXPERTS, 8], I32)
        hit = [sb(f"hit{i}", [P, EXPERTS, 8]) for i in range(2)]
        above = sb("above", [P, CANDS, TILES, EXPERTS], BF16)
        picks = sb("picks", [P, 2, TILES, EXPERTS], BF16)
        n_above = sb("n_above", [P, TILES])
        pos_a = sb("pos_a", [P, TILES, EXPERTS])
        pos_b = sb("pos_b", [P, TILES, EXPERTS])
        pos_i = sb("pos_i", [P, TILES, EXPERTS], I32)
        pos_d = sb("pos_d", [P, 2, TILES, EXPERTS], I32)
        pos_h = sb("pos_h", [P, 2, TILES, EXPERTS], F16)
        onehot_a, onehot_b = (probs_all[:, 2 * i:2 * i + 2, :].rearrange("p a n -> p (a n)").bitcast(F16)
                              .rearrange("p (t a e) -> p t a e", t=TILES, a=16) for i in range(2))
        ids = sb("ids", [P, P], F16)
        slot_token = sb("slot_token", [P, HALVES * EXPERTS], I32)
        rows = (w1[:, :, :, :].rearrange("p g k d -> p (g k d)")[:, 0:EXPERTS * HALVES * ROW]
                .rearrange("p (c r) -> p c r", r=ROW))
        rows_t = [sb(f"rows_t{i}", [P, CAP]) for i in range(2)]
        hidden = [sb(f"hidden{i}", [P, FT, CAP]) for i in range(2)]
        expert_out = xn_t[:, :, :].rearrange("p (e h) d -> p e h d", h=HALVES)
        zero = sb("zero", [P, D])

        load = {n: sem(f"load_{n}") for n in (
            "x0", "x1", "x2", "x3", "c32", "csm", "c16", "kbits", "w_att0", "w_att1", "b_col", "b_row",
            "rope0", "rope1", "ctx", "router", "w_up", "w_down", "w1", "w2t", "b1c", "b2b")}
        dve_step = sem("dve_step")
        pool_step = sem("pool_step")
        zeroed = sem("zeroed")
        stats_ready = [sem(f"stats_ready{n}") for n in range(4)]
        xn_dve = [sem(f"xn_dve{n}") for n in range(4)]
        xn_pool = [sem(f"xn_pool{n}") for n in range(4)]
        xn_psum = [sem(f"xn_psum{n}") for n in range(4)]
        xn_t_ready = [sem(f"xn_t_ready{n}") for n in range(4)]

        class Attention:

            def __init__(self, a):
                self.a, self.heads = a, HEADS[a]
                self.hg = self.heads // 4
                self.cols = 4 * D // self.heads
                self.scale = float(D // self.heads) ** -0.5
                self.ctx_psum = sem(f"ctx_psum_{a}")
                self.ctx_t_ready = sem(f"ctx_t_ready_{a}")
                self.k_psum = sem(f"k_psum_{a}")
                self.k_rot_ready = sem(f"k_rot_ready_{a}")
                self.k_bd_dve = sem(f"k_bd_dve_{a}")
                self.k_bd_pool = sem(f"k_bd_pool_{a}")
                self.v_psum = sem(f"v_psum_{a}")
                self.v_raw_ready = sem(f"v_raw_ready_{a}")
                self.v_bd_ready = sem(f"v_bd_ready_{a}")
                self.ring_filled = sem(f"ring_filled_{a}")
                self.ring_read = sem(f"ring_read_{a}")
                self.q_ready = sem(f"q_ready_{a}")
                self.qr_ready = sem(f"qr_ready_{a}")
                self.m_ready = sem(f"m_ready_{a}")
                self.m_psum = sem(f"m_psum_{a}")
                self.m_t_ready = sem(f"m_t_ready_{a}")
                self.scores_ready = sem(f"scores_ready_{a}")
                self.probs_ready = sem(f"probs_ready_{a}")
                self.sum_ready = sem(f"sum_ready_{a}")
                self.ctx_ready = sem(f"ctx_ready_{a}")
                self.recip_ready = sem(f"recip_ready_{a}")
                self.att_ready = sem(f"att_ready_{a}")
                self.out_psum = sem(f"out_psum_{a}")
                self.resid_done = sem(f"resid_done_{a}")

        att = [Attention(0), Attention(1)]
        bo_added = sem("bo_added")
        ident_ready = sem("ident_ready")
        router_psum, logit_t_ready = sem("router_psum"), sem("logit_t_ready")
        logit_psum, logit_ready, l_exp_ready = sem("logit_psum"), sem("logit_ready"), sem("l_exp_ready")
        weight_ready = sem("weight_ready")
        above_ready, counted = sem("above_ready"), sem("counted")
        picks_ready, prefix_ready = sem("picks_ready"), sem("prefix_ready")
        onehot_ready, ids_psum, ids_ready, place_psum, slots_ready = (
            sem("onehot_ready"), sem("ids_psum"), sem("ids_ready"), sem("place_psum"), sem("slots_ready"))
        dispatched = [sem(f"dispatched{i}") for i in range(3)]
        y_init = sem("y_init")
        gathered = [sem(f"gathered{i}") for i in range(EXPERTS)]
        rows_psum, rows_t_ready = sem("rows_psum"), sem("rows_t_ready")
        up_psum, hidden_ready = sem("up_psum"), sem("hidden_ready")
        down_psum, expert_ready = sem("down_psum"), sem("expert_ready")
        added = [sem(f"added{i}") for i in range(2)]
        y_loaded = [sem(f"y_loaded{b}") for b in range(B)]
        x2_ready = sem("x2_ready")
        c_psum, c_raw_ready, c_one_ready, cb_psum, c21_ready = (
            sem("c_psum"), sem("c_raw_ready"), sem("c_one_ready"), sem("cb_psum"), sem("c21_ready"))
        w21_psum, w21_ready = sem("w21_psum"), sem("w21_ready")
        x3c_ready = sem("x3c_ready")
        fin_psum, fin_ready = sem("fin_psum"), sem("fin_ready")
        stored = sem("stored")

        def tok(ap):
            return ap.rearrange("(t p) d -> p t d", p=P)

        block = ctx.enter_context(nc.Block())

        @block.sync
        def _(sp):
            def get(dst, src, name):
                sp.dma_start(dst, src).then_inc(load[name], 16)

            def get_x(b):
                get(x_in[:, TPB * b:TPB * (b + 1), :], tok(ins["x"])[:, TPB * b:TPB * (b + 1), :], f"x{b}")

            get_x(0)
            get(c32[:, :], ins["c32"], "c32")
            get(w_att[0][:, :, :], ins["w_att0"], "w_att0")
            for b in range(1, B):
                get_x(b)
            get(csm[:, :], ins["csm"], "csm")
            get(b_row[:, :, :], ins["b_row"][None, :, :].to_broadcast([P, 2, D]), "b_row")
            get(wr[:, :], ins["wr"], "router")
            get(br[:, :], ins["br"], "router")
            get(rope[1][:, :, :], ins["rope1"], "rope1")
            get(w_att[1][:, :, :], ins["w_att1"], "w_att1")
            get(kbits[:, :], ins["kbits"], "kbits")
            get(b1c[:, :, :], ins["b1c"], "b1c")
            get(w2t[:, :, :, :], ins["w2t"], "w2t")
            get(w1[:, :, :, :], ins["w1"], "w1")
            get(b2b[:, :, :], ins["b2"][None, :, :].to_broadcast([P, GEMMS, D]), "b2b")
            get(c16[:, :], ins["c16"], "c16")
            get(w_up[:, :, :, :], ins["w_up"], "w_up")
            get(b_up[:, :, :], ins["b_up"], "w_up")
            get(w_down[:, :, :, :], ins["w_down"], "w_down")

            for h in range(2):
                sp.wait_ge((xn_dve if h == 0 else xn_pool)[1], TILES // 2)
                sp.dma_start(tok(dispatch)[:, 8 * h:8 * h + 8, 0:D], xn[:, 8 * h:8 * h + 8, :]).then_inc(dispatched[h], 16)
            sp.wait_ge(att[0].resid_done, B)
            sp.dma_start(tok(y_even), x_mid[:, :, :]).then_inc(y_init, 16)
            sp.wait_ge(zeroed, 1)
            sp.dma_start(tok(y_odd), zero[:, None, :].to_broadcast([P, TILES, D])).then_inc(y_init, 16)
            sp.wait_ge(weight_ready, 1)
            sp.dma_start(tok(dispatch)[:, :, D:ROW], weight[:, :, :]).then_inc(dispatched[2], 16)
            sp.wait_ge(added[0], 16 * HALVES * EXPERTS // 2)
            sp.wait_ge(added[1], 16 * HALVES * EXPERTS // 2)
            for b in range(B):
                span = slice(TPB * b, TPB * (b + 1))
                sp.dma_start(x_in[:, span, :], tok(y_even)[:, span, :]).then_inc(y_loaded[b], 16)
                sp.dma_start(x_add[:, span, :], tok(y_odd)[:, span, :]).then_inc(y_loaded[b], 16)
            for b in range(B):
                sp.wait_ge(fin_ready, b + 1)
                sp.dma_start(tok(out)[:, TPB * b:TPB * (b + 1), :], xn[:, TPB * b:TPB * (b + 1), :]).then_inc(stored, 16)
            sp.wait_ge(stored, 16 * B)

        def pe_prepare_kv(pe, L, first):
            W = w_att[L.a]
            pe.wait_ge(load[f"w_att{L.a}"], 16)
            if first:
                pe.wait_ge(load["ctx"], 16)
                pe.wait_ge(load["c32"], 16)
                nc.tensor.transpose(score_bank[0][:, 0:P], ctx_rows[:, :], k32("ident")).then_inc(L.ctx_psum, 1)
                pe.wait_ge(L.ctx_t_ready, 1)
            keys = ctx_t[:, :, 0, :]
            nc.tensor.matmul(score_bank[1][:, 0:P], W[:, W_K, :], keys, start=True, stop=True)
            nc.tensor.matmul(score_bank[1][:, P:2 * P], W[:, W_KS, :], keys, start=True, stop=True).then_inc(L.k_psum, 1)
            for b in range(B):
                last = nc.tensor.matmul(ctx_bank[:, b * P:(b + 1) * P], ctx_t[:, b, :, :], W[:, W_V, :],
                                        start=True, stop=True)
            last.then_inc(L.v_psum, 1)

        def dve_rotate_keys(dve, chain, L):
            cos = rope[L.a][:, 0, 0:KV][:, None, :].to_broadcast([P, B, KV])
            sin = rope[L.a][:, 1, 0:KV][:, None, :].to_broadcast([P, B, KV])
            kp = score_bank[1][:, 0:P].rearrange("p (b k) -> p b k", b=B)
            ks = score_bank[1][:, P:2 * P].rearrange("p (b k) -> p b k", b=B)
            dve.wait_ge(load[f"rope{L.a}"], 16)
            if L.a == 0:
                dve.wait_ge(load["b_col"], 16)
            dve.wait_ge(L.k_psum, 1)
            if L.a == 0:
                chain.step(nc.vector.scalar_tensor_tensor(k_a[:, :, :], kp, b_col[:, 2:3], cos, ALU.add, ALU.mult))
                chain.step(nc.vector.scalar_tensor_tensor(k_b[:, :, :], ks, b_col[:, 3:4], sin, ALU.add, ALU.mult))
            else:
                chain.step(nc.vector.tensor_tensor(k_a[:, :, :], kp, cos, ALU.mult))
                chain.step(nc.vector.tensor_tensor(k_b[:, :, :], ks, sin, ALU.mult))
            chain.settle()
            nc.vector.tensor_tensor(k_rot[:, :, :], k_a[:, :, :], k_b[:, :, :], ALU.add).then_inc(L.k_rot_ready, 1)

        def dve_first_keys(dve, L):
            dve.wait_ge(L.k_rot_ready, 1)
            for dst in (k_bdr, k_bd):
                spread_keys(nc.vector, L, 0, dst).then_inc(L.k_bd_dve, 1)

        def dve_values(dve, L):
            dve.wait_ge(L.v_psum, 1)
            vp = ctx_bank[:, :].rearrange("p (b e) -> p b e", b=B)
            mask = k32(f"vmask{L.a}")[:, None, :].to_broadcast([P, B, D])
            if L.a == 0:
                dve.wait_ge(load["b_row"], 16)
                nc.vector.tensor_tensor(v_raw[:, :, :], vp, b_row[:, 0:1, :].to_broadcast([P, B, D]),
                                        ALU.add).then_inc(L.v_raw_ready, 1)
                dve.wait_ge(L.v_raw_ready, 1)
                nc.vector.tensor_tensor(v_bd[:, :, :], v_raw[:, :, :], mask, ALU.mult).then_inc(L.v_bd_ready, 1)
            else:
                nc.vector.tensor_tensor(v_bd[:, :, :], vp, mask, ALU.mult).then_inc(L.v_bd_ready, 1)

        def spread_keys(engine, L, b, dst):
            o = dst[:, b, 0:L.heads * KV].rearrange("p (h k) -> p h k", h=L.heads)
            return engine.tensor_tensor(o, k_rot[:, b:b + 1, :].to_broadcast([P, L.heads, KV]),
                                        k32(f"head{L.a}")[:, :, None].to_broadcast([P, L.heads, KV]), ALU.mult)

        def pe_transpose_tokens(pe, n, b, dst):
            for j in range(TPB):
                last = nc.tensor.transpose(dst[:, j * P:(j + 1) * P], xn[:, TPB * b + j, :], k32("ident"))
            last.then_inc(xn_psum[n], 1)

        def uses(L):
            return 2 + L.hg

        def pe_fill(pe, L, u):
            if u >= 3:
                pe.wait_ge(L.ring_read, u - 2)
            return ring[u % 3]

        def pe_project_q(pe, L, n, b):
            W = w_att[L.a]
            pe_transpose_tokens(pe, n, b, TX)
            pe.wait_ge(xn_t_ready[n], b + 1)
            rhs = xn_t[:, TPB * b:TPB * (b + 1), :].rearrange("p j t -> p (j t)")
            for i, w in enumerate((W_Q, W_QS)):
                dst = pe_fill(pe, L, uses(L) * b + i)
                nc.tensor.matmul(dst[:, :], W[:, w, :], rhs, start=True, stop=True).then_inc(L.ring_filled, 1)

        def pe_max_scores(pe, L, b, i):
            width = L.heads * KV
            per = 512 // width
            dst = pe_fill(pe, L, uses(L) * b + 2 + i)
            pe.wait_ge(L.qr_ready, b + 1)
            for k in range(per):
                j = i * per + k
                last = nc.tensor.matmul(dst[:, k * width:(k + 1) * width], q_tr[b % 2][:, j * P:(j + 1) * P],
                                        k_bdr[:, b, 0:width], start=True, stop=True)
            last.then_inc(L.ring_filled, 1)

        def pe_transpose_maxima(pe, L, b):
            rows_m = 2 * L.heads
            pe.wait_ge(L.m_ready, b + 1)
            mt = TX[:, :].bitcast(BF16)
            for j in range(TPB):
                last = nc.tensor.transpose(mt[0:rows_m, j * P:(j + 1) * P], m_hl[b % 2][:, j, 0:rows_m], ident_bf[:, :])
            last.then_inc(L.m_psum, 1)

        def pe_scores(pe, L, b, g):
            v = L.hg * b + g
            if g == 0:
                pe.wait_ge(L.q_ready, b + 1)
            if v >= 2:
                pe.wait_ge(L.probs_ready, v - 1)
            nc.tensor.matmul(score_bank[v % 2][:, :], k_bd[:, b, g * P:(g + 1) * P], q_t[b % 2][:, :],
                             start=True, stop=False)
            if g == 0:
                pe.wait_ge(L.m_t_ready, b + 1)
            nc.tensor.matmul(score_bank[v % 2][:, :], ksm(f"neg{L.a}")[:, g * P:(g + 1) * P], m_t[b % 2][:, :],
                             start=False, stop=True).then_inc(L.scores_ready, 1)

        def pe_values(pe, L, b):
            for dst in (ctx_bank, sum_bank):
                if b >= 1 and dst is ctx_bank:
                    pe.wait_ge(L.att_ready, b)
                if b >= 1 and dst is sum_bank:
                    pe.wait_ge(L.resid_done, b)
                for g in range(L.hg):
                    pe.wait_ge(L.probs_ready, L.hg * b + g + 1)
                    w = (k32(f"vmask{L.a}")[:, 0:L.cols] if dst is sum_bank
                         else v_bd[:, b, g * L.cols:(g + 1) * L.cols])
                    last = nc.tensor.matmul(dst[g * L.cols:(g + 1) * L.cols, :], w, probs[(L.hg * b + g) % 4][:, :],
                                            start=True, stop=True)
                last.then_inc(L.sum_ready if dst is sum_bank else L.ctx_ready, 1)

        def pe_project_out(pe, L, b):
            pe.wait_ge(L.att_ready, b + 1)
            for j in range(TPB):
                last = nc.tensor.matmul(sum_bank[:, j * P:(j + 1) * P], att_t[b % 2][:, j * P:(j + 1) * P],
                                        w_att[L.a][:, W_O, :], start=True, stop=True)
            last.then_inc(L.out_psum, 1)

        def pe_attention(pe, L, n, tokens_ready):
            def keys_ready(b):
                if b == 0:
                    pe.wait_ge(L.k_bd_dve, 2)
                else:
                    pe.wait_ge(L.k_bd_pool, 2 * b)

            tokens_ready(0)
            pe_project_q(pe, L, n, 0)
            tokens_ready(1)
            keys_ready(0)
            for i in range(L.hg):
                pe_max_scores(pe, L, 0, i)
            pe_project_q(pe, L, n, 1)
            for b in range(B):
                pe_transpose_maxima(pe, L, b)
                if b + 1 < B:
                    keys_ready(b + 1)
                for g in range(L.hg):
                    pe_scores(pe, L, b, g)
                    if b + 1 < B:
                        pe_max_scores(pe, L, b + 1, g)
                if b >= 1:
                    pe_project_out(pe, L, b - 1)
                if b + 2 < B:
                    tokens_ready(b + 2)
                    pe_project_q(pe, L, n, b + 2)
                if b == 0:
                    pe.wait_ge(L.v_bd_ready, 1)
                pe_values(pe, L, b)
            pe_project_out(pe, L, B - 1)

        def act_attention(act, L, n):
            def tokens(b):
                act.wait_ge(xn_psum[n], b + 1)
                nc.scalar.activation(xn_t[:, TPB * b:TPB * (b + 1), :].rearrange("p j t -> p (j t)"), TX[:, :],
                                     ACT.Copy).then_inc(xn_t_ready[n], 1)

            def rounded_q(b):
                act.wait_ge(L.q_ready, b + 1)
                nc.scalar.activation(q_tr[b % 2][:, :], q_t[b % 2][:, :], ACT.Copy).then_inc(L.qr_ready, 1)

            tokens(0)
            rounded_q(0)
            tokens(1)
            rounded_q(1)
            for b in range(B):
                rows_m = 2 * L.heads
                act.wait_ge(L.m_psum, b + 1)
                nc.scalar.activation(m_t[b % 2][0:rows_m, :], TX[:, :].bitcast(BF16)[0:rows_m, 0:SEQ],
                                     ACT.Copy).then_inc(L.m_t_ready, 1)
                for g in range(L.hg):
                    v = L.hg * b + g
                    act.wait_ge(L.scores_ready, v + 1)
                    if v >= 4:
                        act.wait_ge(L.sum_ready, (v - 4) // L.hg + 1)
                    nc.scalar.activation(probs[v % 4][:, :], score_bank[v % 2][:, :], ACT.Exp,
                                         scale=L.scale).then_inc(L.probs_ready, 1)
                if b + 2 < B:
                    tokens(b + 2)
                    rounded_q(b + 2)

        def dve_attention(dve, chain, L, resid, after=None):
            cos, sin = rope[L.a][:, 0, :], rope[L.a][:, 1, :]

            def query(b):
                u = uses(L) * b
                dve.wait_ge(L.ring_filled, u + 1)
                if L.a == 0:
                    nc.vector.scalar_tensor_tensor(q_a[:, :], ring[u % 3][:, :], b_col[:, 0:1], cos,
                                                   ALU.add, ALU.mult).then_inc(L.ring_read, 1)
                else:
                    nc.vector.tensor_tensor(q_a[:, :], ring[u % 3][:, :], cos, ALU.mult).then_inc(L.ring_read, 1)
                dve.wait_ge(L.ring_filled, u + 2)
                if L.a == 0:
                    nc.vector.scalar_tensor_tensor(q_b[:, :], ring[(u + 1) % 3][:, :], b_col[:, 1:2], sin,
                                                   ALU.add, ALU.mult).then_inc(L.ring_read, 1)
                else:
                    nc.vector.tensor_tensor(q_b[:, :], ring[(u + 1) % 3][:, :], sin, ALU.mult).then_inc(L.ring_read, 1)
                dve.wait_ge(L.ring_read, u + 2)
                nc.vector.tensor_tensor(q_t[b % 2][:, :], q_a[:, :], q_b[:, :], ALU.add).then_inc(L.q_ready, 1)

            def maximum(b):
                per = TPB // L.hg
                for i in range(L.hg):
                    u = uses(L) * b + 2 + i
                    dve.wait_ge(L.ring_filled, u + 1)
                    nc.vector.tensor_reduce(m_max[:, i * per:(i + 1) * per, 0:L.heads],
                                            ring[u % 3][:, :].rearrange("p (j h k) -> p j h k", j=per, h=L.heads),
                                            X_AXIS, ALU.max).then_inc(L.ring_read, 1)
                dve.wait_ge(L.ring_read, uses(L) * (b + 1))
                hi, lo = m_hl[b % 2][:, :, 0:L.heads], m_hl[b % 2][:, :, L.heads:2 * L.heads]
                chain.step(nc.vector.tensor_copy(hi, m_max[:, :, 0:L.heads]))
                chain.settle()
                nc.vector.tensor_tensor(lo, m_max[:, :, 0:L.heads], hi, ALU.subtract).then_inc(L.m_ready, 1)

            def normalise(b):
                dve.wait_ge(L.sum_ready, b + 1)
                nc.vector.reciprocal(recip[:, :], sum_bank[:, :]).then_inc(L.recip_ready, 1)
                dve.wait_ge(L.recip_ready, b + 1)
                dve.wait_ge(L.ctx_ready, b + 1)
                nc.vector.tensor_tensor(att_t[b % 2][:, :], ctx_bank[:, :], recip[:, :], ALU.mult).then_inc(L.att_ready, 1)

            def residual(b):
                dve.wait_ge(L.out_psum, b + 1)
                if L.a == 0:
                    dve.wait_ge(bo_added, b + 1)
                span = slice(TPB * b, TPB * (b + 1))
                nc.vector.tensor_tensor(x_mid[:, span, :].rearrange("p j d -> p (j d)"), sum_bank[:, :],
                                        resid[:, span, :].rearrange("p j d -> p (j d)"),
                                        ALU.add).then_inc(L.resid_done, 1)
                dve.wait_ge(L.resid_done, b + 1)
                dve_stats(chain, x_mid, span)

            query(0)
            maximum(0)
            query(1)
            for b in range(B):
                if b + 1 < B:
                    maximum(b + 1)
                if b >= 1:
                    residual(b - 1)
                if b + 2 < B:
                    query(b + 2)
                normalise(b)
            residual(B - 1)

        def dve_stats(chain, x, span):
            for t in range(span.start, span.stop):
                chain.step(nc.vector.bn_stats(stats[:, t, :], x[:, t, :]))

        def dve_moments(dve, chain, n, span):
            me, mo = stats[:, span, 1], stats[:, span, 4]
            ve, vo = stats[:, span, 2], stats[:, span, 5]
            mu, r, a, v = mean[:, span], rstd[:, span], ln_a[:, span], ln_v[:, span]
            V = nc.vector
            chain.settle()
            chain.step(V.tensor_tensor(a, me, mo, ALU.subtract))
            chain.step(V.tensor_tensor(v, ve, vo, ALU.add))
            chain.step(V.tensor_tensor(mu, me, mo, ALU.add))
            chain.settle()
            chain.step(V.tensor_scalar(v, v, 1.0 / D, EPS, ALU.mult, ALU.add))
            chain.step(V.scalar_tensor_tensor(a, a, 0.25, a, ALU.mult, ALU.mult))
            chain.step(V.tensor_scalar(mu, mu, 0.5, None, ALU.mult))
            chain.settle()
            chain.step(V.tensor_tensor(v, v, a, ALU.add))
            chain.settle()
            chain.step(V.tensor_scalar(a.bitcast(I32), v.bitcast(I32), 1, None, ALU.logical_shift_right))
            chain.settle()
            chain.step(V.tensor_scalar(r.bitcast(I32), a.bitcast(I32), -1.0, RSQRT_MAGIC, ALU.mult, ALU.add))
            chain.settle()
            for i in range(3):
                chain.step(V.scalar_tensor_tensor(a, r, -0.5, r, ALU.mult, ALU.mult))
                chain.settle()
                chain.step(V.tensor_tensor(a, a, v, ALU.mult))
                chain.settle()
                newton = V.scalar_tensor_tensor(r, a, 1.5, r, ALU.add, ALU.mult)
                if i < 2:
                    chain.step(newton)
                    chain.settle()
                else:
                    newton.then_inc(stats_ready[n], 1)

        def normalise_tile(engine, x, t):
            return engine.tensor_scalar(xn[:, t, :], x[:, t, :], mean[:, t:t + 1], rstd[:, t:t + 1],
                                        ALU.subtract, ALU.mult)

        @block.gpsimd
        def _(pool):
            chain = Chain(pool, pool_step)
            P_ = nc.gpsimd
            chain.step(P_.memset(m_t[0][:, :], 0.0))
            chain.step(P_.memset(m_t[1][:, :], 0.0))
            for i in range(2):
                chain.settle()
                chain.step(P_.memset(hidden[i][BIAS_ROW:P, FT - 1, :], 1.0))
            chain.settle()
            P_.memset(zero[:, :], 0.0).then_inc(zeroed, 1)

            def keys(L):
                pool.wait_ge(L.k_rot_ready, 1)
                for b in range(1, B):
                    for dst in (k_bdr, k_bd):
                        spread_keys(P_, L, b, dst).then_inc(L.k_bd_pool, 1)

            def tokens(n, x, tiles, level):
                pool.wait_ge(stats_ready[n], level)
                for t in tiles:
                    normalise_tile(P_, x, t).then_inc(xn_pool[n], 1)

            pool.wait_ge(load["c32"], 16)
            pool.wait_ge(att[0].k_rot_ready, 1)
            for dst in (k_bdr, k_bd):
                spread_keys(P_, att[0], 1, dst).then_inc(att[0].k_bd_pool, 1)
            tokens(0, x_in, range(TPB * 2, TPB * 3), 2)
            for dst in (k_bdr, k_bd):
                spread_keys(P_, att[0], 2, dst).then_inc(att[0].k_bd_pool, 1)
            tokens(0, x_in, range(TPB * 3, TPB * 4), 2)
            for dst in (k_bdr, k_bd):
                spread_keys(P_, att[0], 3, dst).then_inc(att[0].k_bd_pool, 1)
            pool.wait_ge(load["b_row"], 16)
            for b in range(B):
                pool.wait_ge(load[f"x{b}"], 16)
                P_.tensor_tensor(x_add[:, TPB * b:TPB * (b + 1), :], x_in[:, TPB * b:TPB * (b + 1), :],
                                 b_row[:, 1:2, :].to_broadcast([P, TPB, D]), ALU.add).then_inc(bo_added, 1)

            tokens(1, x_mid, range(TILES // 2, TILES), 1)
            keys(att[1])

            def gather(e):
                if e == 0:
                    pool.wait_ge(slots_ready, 1)
                    for s in dispatched:
                        pool.wait_ge(s, 16)
                for h in range(HALVES):
                    c = h * EXPERTS + e
                    P_.indirect_dma_start(
                        rows[:, c, :], None, dispatch,
                        bass.IndirectOffsetOnAxis(ap=slot_token[:, c:c + 1].bitcast(U32), axis=0)).then_inc(gathered[e], 16)

            def add(e):
                pool.wait_ge(expert_ready, HALVES * (e + 1))
                if e < 2:
                    pool.wait_ge(y_init, 32)
                else:
                    pool.wait_ge(added[e % 2], 16 * HALVES * (e // 2))
                for h in range(HALVES):
                    c = h * EXPERTS + e
                    P_.indirect_dma_start(
                        y_odd if e % 2 else y_even,
                        bass.IndirectOffsetOnAxis(ap=slot_token[:, c:c + 1].bitcast(U32), axis=0),
                        expert_out[:, e, h, :], None, compute_op=ALU.add).then_inc(added[e % 2], 16)

            AHEAD = 4
            for e in range(AHEAD):
                gather(e)
            for e in range(EXPERTS):
                add(e)
                if e + AHEAD < EXPERTS:
                    gather(e + AHEAD)

            tokens(2, x_in, range(TPB * 2, TILES), 1)
            pool.wait_ge(c21_ready, GEMMS)
            for b in range(B):
                pool.wait_ge(att[1].resid_done, b + 1)
                for g in range(2 * b, 2 * b + 2):
                    P_.tensor_tensor(x_add[:, TPG * g:TPG * (g + 1), :], x_mid[:, TPG * g:TPG * (g + 1), :],
                                     c21[:, g:g + 1, :].to_broadcast([P, TPG, D]), ALU.add).then_inc(x3c_ready, 1)
            tokens(3, x_mid, range(TILES // 2, TILES), 1)

        @block.scalar
        def _(act):
            def get(dst, src, name):
                act.dma_start(dst, src).then_inc(load[name], 16)

            get(ctx_rows[:, :], ins["ctx"], "ctx")
            get(rope[0][:, :, :], ins["rope0"], "rope0")
            get(b_col[:, :], ins["b_col"], "b_col")

            act.wait_ge(att[0].ctx_psum, 1)
            nc.scalar.activation(
                ctx_t[:, :, :, :],
                score_bank[0][:, 0:P].rearrange("p (b k) -> p b k", b=B)[:, :, None, :].to_broadcast([P, B, 4, KV]),
                ACT.Copy).then_inc(att[0].ctx_t_ready, 1)
            nc.scalar.activation(ident_bf[:, :], k32("ident"), ACT.Copy).then_inc(ident_ready, 1)
            act.wait_ge(zeroed, 1)
            act_attention(act, att[0], 0)

            for b in range(B):
                act.wait_ge(xn_psum[1], b + 1)
                nc.scalar.activation(xn_t[:, TPB * b:TPB * (b + 1), :].rearrange("p j t -> p (j t)"), bank[b][:, :],
                                     ACT.Copy).then_inc(xn_t_ready[1], 1)
            act.wait_ge(load["router"], 32)
            act.wait_ge(router_psum, 1)
            nc.scalar.activation(logit_t[:, :], bank[4][:, :], ACT.Identity, bias=br[:, 0:1]).then_inc(logit_t_ready, 1)
            act.wait_ge(logit_ready, 1)
            nc.scalar.activation(l_exp[:, :, :], logit[:, :, :], ACT.Exp).then_inc(l_exp_ready, 1)

            act.wait_ge(c_psum, 1)
            nc.scalar.activation(c_raw[:, :], bank[7][:, 0:2 * D], ACT.Copy).then_inc(c_raw_ready, 1)
            for g in range(GEMMS):
                act.wait_ge(w21_psum, g + 1)
                nc.scalar.activation(w21[:, g, :], bank[2 + g % 2][:, 0:D], ACT.Copy).then_inc(w21_ready, 1)
            for e in range(EXPERTS):
                act.wait_ge(rows_psum, e + 1)
                if e >= 2:
                    act.wait_ge(up_psum, e - 1)
                nc.scalar.activation(rows_t[e % 2][:, :], bank[e % 2][:, 0:CAP], ACT.Copy).then_inc(rows_t_ready, 1)
                act.wait_ge(up_psum, e + 1)
                if e >= 2:
                    act.wait_ge(down_psum, e - 1)
                pair = bank[2 + 2 * (e % 2)], bank[3 + 2 * (e % 2)]
                for f in range(FT):
                    n = P if f < FT - 1 else F_LAST
                    last = nc.scalar.activation(hidden[e % 2][0:n, f, :], pair[f // 2][0:n, (f % 2) * CAP:(f % 2 + 1) * CAP],
                                                ACT.Silu, bias=b_up[0:n, e // 2, f:f + 1])
                    last.then_inc(hidden_ready, 1)

            act_attention(act, att[1], 2)
            for b in range(B):
                act.wait_ge(xn_psum[3], b + 1)
                nc.scalar.activation(xn_t[:, TPB * b:TPB * (b + 1), :].rearrange("p j t -> p (j t)"), bank[b][:, :],
                                     ACT.Copy).then_inc(xn_t_ready[3], 1)

        @block.vector
        def _(dve):
            chain = Chain(dve, dve_step)
            V = nc.vector

            dve.wait_ge(load["x0"], 16)
            dve_stats(chain, x_in, slice(0, TPB))
            dve_moments(dve, chain, 0, slice(0, TPB))
            dve.wait_ge(stats_ready[0], 1)
            for t in range(TPB):
                normalise_tile(V, x_in, t).then_inc(xn_dve[0], 1)
            dve.wait_ge(load["c32"], 16)
            dve_rotate_keys(dve, chain, att[0])
            dve_first_keys(dve, att[0])
            dve_values(dve, att[0])
            for b in range(1, B):
                dve.wait_ge(load[f"x{b}"], 16)
                dve_stats(chain, x_in, slice(TPB * b, TPB * (b + 1)))
            dve_moments(dve, chain, 0, slice(TPB, TILES))
            dve.wait_ge(stats_ready[0], 2)
            for t in range(TPB, 2 * TPB):
                normalise_tile(V, x_in, t).then_inc(xn_dve[0], 1)
            dve_attention(dve, chain, att[0], x_add)

            dve_moments(dve, chain, 1, slice(0, TILES))
            dve.wait_ge(stats_ready[1], 1)
            for t in range(TILES // 2):
                normalise_tile(V, x_mid, t).then_inc(xn_dve[1], 1)
            dve.wait_ge(logit_psum, 1)
            lp = bank[5][:, :].rearrange("p (j b e) -> p b j e", j=TPB, b=B)[:, :, :, 0:EXPERTS]
            lg = logit[:, :, :].rearrange("p (b j) e -> p b j e", b=B)
            chain.step(V.tensor_reduce(l_max[:, :].rearrange("p (b j) -> p b j", b=B), lp, X_AXIS, ALU.max))
            chain.settle()
            V.tensor_tensor(lg, lp, l_max[:, :].rearrange("p (b j) -> p b j", b=B)[:, :, :, None]
                            .to_broadcast([P, B, TPB, EXPERTS]), ALU.subtract).then_inc(logit_ready, 1)
            dve.wait_ge(l_exp_ready, 1)
            chain.step(V.tensor_reduce(l_sum[:, :], l_exp[:, :, :], X_AXIS, ALU.add))
            chain.settle()
            chain.step(V.reciprocal(l_sum[:, :], l_sum[:, :]))
            chain.settle()
            V.tensor_tensor(weight[:, :, :], l_exp[:, :, :], l_sum[:, :, None].to_broadcast([P, TILES, EXPERTS]),
                            ALU.mult).then_inc(weight_ready, 1)
            dve.wait_ge(weight_ready, 1)

            dve.wait_ge(load["kbits"], 16)
            def bias_diagonal():
                dve.wait_ge(c_raw_ready, 1)
                for g in range(GEMMS):
                    V.tensor_scalar(c_one[:, g, :], c_raw[:, (g // 4) * D:(g // 4 + 1) * D], k32("crow")[:, g:g + 1],
                                    None, ALU.mult).then_inc(c_one_ready, 1)

            def bias_sum(first):
                dve.wait_ge(load["b2b"], 16)
                for g in range(first, first + 4):
                    dve.wait_ge(cb_psum, g + 1)
                    V.tensor_tensor(c21[:, g, :], bank[2 + g % 2][:, 0:D], b2b[:, g, :], ALU.add).then_inc(c21_ready, 1)

            between = {1: lambda: dve_rotate_keys(dve, chain, att[1]), 2: lambda: dve_first_keys(dve, att[1]),
                       3: lambda: dve_values(dve, att[1]), 4: bias_diagonal,
                       7: lambda: bias_sum(0), 8: lambda: bias_sum(4)}
            for s in range(STEPS):
                base = hit[s % 2][:, :, 0:1]
                step_bits = kbits[:, s * 8:(s + 1) * 8][:, None, :].to_broadcast([P, EXPERTS, 8])
                if s == 0:
                    chain.step(V.tensor_copy(cand[:, :, :], step_bits))
                    chain.step(V.memset(base, 0.0))
                else:
                    chain.step(V.tensor_tensor(cand[:, :, :], base.bitcast(I32).to_broadcast([P, EXPERTS, 8]), step_bits,
                                               ALU.bitwise_or))
                chain.settle()
                cf = cand[:, :, 1:8].bitcast(F32).rearrange("p e k -> p k e")
                V.tensor_tensor(above[:, :, :, :],
                                weight[:, None, :, :].to_broadcast([P, CANDS, TILES, EXPERTS]),
                                cf[:, :, None, :].to_broadcast([P, CANDS, TILES, EXPERTS]),
                                ALU.is_ge).then_inc(above_ready, 1)
                if s in between:
                    between[s]()
                dve.wait_ge(counted, s + 1)
                cnt = bank[1][:, 0:CANDS * EXPERTS].rearrange("p (k e) -> p e k", k=CANDS)
                chain.step(V.scalar_tensor_tensor(hit[s % 2][:, :, 1:8], cnt, float(CAP), cand[:, :, 1:8].bitcast(F32),
                                                  ALU.is_ge, ALU.mult))
                chain.settle()
                chain.step(V.tensor_reduce(hit[(s + 1) % 2][:, :, 0:1], hit[s % 2][:, :, :], X_AXIS, ALU.max))
                chain.settle()

            limit = hit[STEPS % 2][:, :, 0:1].rearrange("p e o -> p o e").to_broadcast([P, TILES, EXPERTS])
            chain.step(V.tensor_tensor(picks[:, 0, :, :], weight[:, :, :], limit, ALU.is_gt))
            chain.step(V.tensor_tensor(picks[:, 1, :, :], weight[:, :, :], limit, ALU.is_equal))
            chain.settle()
            V.tensor_tensor(pos_b[:, :, :], picks[:, 0, :, :], picks[:, 1, :, :], ALU.add).then_inc(picks_ready, 1)
            dve.wait_ge(prefix_ready, 1)
            pre = bank[5][:, 0:2 * TILES * EXPERTS].rearrange("p (k t e) -> p k t e", k=2, t=TILES)
            chain.step(V.tensor_copy(n_above[:, 0:EXPERTS], bank[6][:, 0:EXPERTS]))
            chain.step(V.tensor_tensor(pos_a[:, :, :], pre[:, 0, :, :], picks[:, 0, :, :], ALU.mult))
            chain.settle()
            chain.step(V.scalar_tensor_tensor(pos_a[:, :, :], pos_b[:, :, :], -4096.0, pos_a[:, :, :], ALU.mult, ALU.add))
            chain.settle()
            chain.step(V.tensor_tensor(pos_b[:, :, :], pre[:, 1, :, :],
                                       n_above[:, 0:EXPERTS][:, None, :].to_broadcast([P, TILES, EXPERTS]), ALU.add))
            chain.settle()
            chain.step(V.tensor_tensor(pos_b[:, :, :], pos_b[:, :, :], picks[:, 1, :, :], ALU.mult))
            chain.settle()
            chain.step(V.scalar_tensor_tensor(pos_i[:, :, :], pos_a[:, :, :], 4096.0, pos_b[:, :, :], ALU.add, ALU.add))
            chain.settle()
            chain.step(V.tensor_scalar(pos_d[:, 0, :, :], pos_i[:, :, :], 4, None, ALU.logical_shift_right))
            chain.step(V.tensor_scalar(pos_d[:, 1, :, :], pos_i[:, :, :], SLOT_B - 1, None, ALU.bitwise_and))
            chain.settle()
            chain.step(V.tensor_copy(pos_h[:, :, :, :], pos_d[:, :, :, :]))
            chain.settle()
            dve.wait_ge(load["c16"], 16)
            digits = k16("iota").rearrange("p (a e) -> p a e", e=EXPERTS)[:, None, :, :].to_broadcast([P, TILES, 16, EXPERTS])
            token = k16("token").rearrange("p (t a e) -> p t a e", t=TILES, a=16)
            for h in range(2):
                for i, dst in enumerate((onehot_a, onehot_b)):
                    sp_ = slice(8 * h, 8 * h + 8)
                    ins_ = V.tensor_tensor(dst[:, sp_, :, :],
                                           pos_h[:, i, sp_, :][:, :, None, :].to_broadcast([P, 8, 16, EXPERTS]),
                                           digits[:, sp_, :, :], ALU.is_equal)
                    chain.step(ins_)
                chain.settle()
                V.tensor_tensor(onehot_b[:, sp_, :, :], onehot_b[:, sp_, :, :], token[:, sp_, :, :],
                                ALU.mult).then_inc(onehot_ready, 1)
            dve.wait_ge(ids_psum, 1)
            V.tensor_tensor(ids[:, :], bank[6][:, 0:P], k32("expert"), ALU.mult).then_inc(ids_ready, 1)
            dve.wait_ge(place_psum, 1)
            V.tensor_copy(slot_token[:, :], bank[7][:, 0:HALVES * EXPERTS]).then_inc(slots_ready, 1)

            for e in range(EXPERTS):
                dve.wait_ge(down_psum, e + 1)
                for h in range(HALVES):
                    V.tensor_scalar(expert_out[:, e, h, :], bank[6 + e % 2][:, h * D:(h + 1) * D],
                                    rows[:, h * EXPERTS + e, D + e:D + e + 1], None, ALU.mult).then_inc(expert_ready, 1)

            for b in range(B):
                span = slice(TPB * b, TPB * (b + 1))
                dve.wait_ge(y_loaded[b], 32)
                V.tensor_tensor(x_in[:, span, :], x_in[:, span, :], x_add[:, span, :], ALU.add).then_inc(x2_ready, 1)
                dve.wait_ge(x2_ready, b + 1)
                dve_stats(chain, x_in, span)
            dve_moments(dve, chain, 2, slice(0, TILES))
            dve.wait_ge(stats_ready[2], 1)
            for t in range(2 * TPB):
                normalise_tile(V, x_in, t).then_inc(xn_dve[2], 1)
            dve_attention(dve, chain, att[1], x_in)

            dve_moments(dve, chain, 3, slice(0, TILES))
            dve.wait_ge(stats_ready[3], 1)
            for t in range(TILES // 2):
                normalise_tile(V, x_mid, t).then_inc(xn_dve[3], 1)
            dve.wait_ge(x3c_ready, GEMMS)
            for b in range(B):
                span = slice(TPB * b, TPB * (b + 1))
                dve.wait_ge(fin_psum, b + 1)
                V.tensor_tensor(xn[:, span, :].rearrange("p j d -> p (j d)"), bank[4 + b][:, :],
                                x_add[:, span, :].rearrange("p j d -> p (j d)"), ALU.add).then_inc(fin_ready, 1)

        @block.tensor
        def _(pe):
            pe_prepare_kv(pe, att[0], True)
            pe.wait_ge(load["csm"], 16)
            pe.wait_ge(ident_ready, 1)
            pe.wait_ge(att[0].v_bd_ready, 1)

            def tokens0(b):
                if b < 2:
                    pe.wait_ge(xn_dve[0], TPB * (b + 1))
                else:
                    pe.wait_ge(xn_pool[0], TPB * (b - 1))

            pe_attention(pe, att[0], 0, tokens0)

            pe.wait_ge(att[0].resid_done, B)
            pe.wait_ge(load["router"], 32)
            for b in range(B):
                pe.wait_ge(xn_dve[1] if b < 2 else xn_pool[1], TPB * (b % 2 + 1))
                pe_transpose_tokens(pe, 1, b, bank[b])
            pe.wait_ge(xn_t_ready[1], B)
            for b in range(B):
                last = nc.tensor.matmul(bank[4][32 * b:32 * b + 32, :], wr[:, :],
                                        xn_t[:, TPB * b:TPB * (b + 1), :].rearrange("p j t -> p (j t)"),
                                        start=True, stop=True)
            last.then_inc(router_psum, 1)
            pe.wait_ge(logit_t_ready, 1)
            for j in range(TPB):
                last = nc.tensor.transpose(bank[5][:, j * P:(j + 1) * P], logit_t[:, j * P:(j + 1) * P], k32("ident"))
            last.then_inc(logit_psum, 1)

            def combined(g):
                if g == 0:
                    pe.wait_ge(load["w1"], 16)
                if g >= 2:
                    pe.wait_ge(w21_ready, g - 1)
                for k in range(OT):
                    last = nc.tensor.matmul(bank[2 + g % 2][:, 0:D], w1[:, g, k, :], w2t[:, g, k, :],
                                            start=(k == 0), stop=(k == OT - 1))
                last.then_inc(w21_psum, 1)

            def bias_rows():
                pe.wait_ge(load["b1c"], 16)
                pe.wait_ge(load["w2t"], 16)
                for half in range(2):
                    for k in range(OT):
                        for q in range(4):
                            g = 4 * half + q
                            last = nc.tensor.matmul(bank[7][32 * q:32 * q + 32, half * D:(half + 1) * D], b1c[:, k, :],
                                                    w2t[:, g, k, :], start=(k == 0), stop=(k == OT - 1),
                                                    skip_group_check=True)
                last.then_inc(c_psum, 1)

            def bias_everywhere(first):
                pe.wait_ge(w21_ready, GEMMS)
                for g in range(first, first + 4):
                    pe.wait_ge(c_one_ready, g + 1)
                    if g >= 2:
                        pe.wait_ge(c21_ready, g - 1)
                    nc.tensor.matmul(bank[2 + g % 2][:, 0:D], k32("ones"), c_one[:, g, :],
                                     start=True, stop=True).then_inc(cb_psum, 1)

            for s in range(STEPS):
                pe.wait_ge(above_ready, s + 1)
                for t in range(TILES):
                    last = nc.tensor.matmul(bank[1][:, 0:CANDS * EXPERTS], ksm("ones"), above[:, :, t, :],
                                            start=(t == 0), stop=(t == TILES - 1))
                last.then_inc(counted, 1)
                if s == 0:
                    pe_prepare_kv(pe, att[1], False)
                elif s == 1:
                    bias_rows()
                elif s < 6:
                    combined(2 * s - 4)
                    combined(2 * s - 3)
                elif s == 6:
                    bias_everywhere(0)
                elif s == 7:
                    bias_everywhere(4)

            pe.wait_ge(picks_ready, 1)
            pre = bank[5][:, 0:2 * TILES * EXPERTS].rearrange("p (k t e) -> p k t e", k=2, t=TILES)
            nc.tensor.matmul(pre, ksm("tri"), picks[:, :, :, :], start=True, stop=True)
            for t in range(TILES - 1):
                later = TILES - 1 - t
                nc.tensor.matmul(pre[:, :, t + 1:TILES, :], ksm("ones"),
                                 picks[:, :, t:t + 1, :].to_broadcast([P, 2, later, EXPERTS]),
                                 start=False, stop=True, skip_group_check=True)
            for t in range(TILES):
                last = nc.tensor.matmul(bank[6][:, 0:EXPERTS], ksm("ones"), picks[:, 0, t, :],
                                        start=(t == 0), stop=(t == TILES - 1))
            last.then_inc(prefix_ready, 1)
            for t in range(TILES):
                if t % 8 == 0:
                    pe.wait_ge(onehot_ready, t // 8 + 1)
                last = nc.tensor.matmul(bank[6][:, 0:P], onehot_b[:, t, :, :], onehot_a[:, t, :, :],
                                        start=(t == 0), stop=(t == TILES - 1))
            last.then_inc(ids_psum, 1)
            pe.wait_ge(ids_ready, 1)
            pe.wait_ge(c_raw_ready, 1)
            by_a = ids[:, :].rearrange("p (h l e) -> p l h e", h=HALVES, l=8)
            for l in range(8):
                last = nc.tensor.matmul(bank[7][:, 0:HALVES * EXPERTS].rearrange("p (h e) -> p h e", h=HALVES),
                                        k16("place")[:, l * P:(l + 1) * P], by_a[:, l, :, :],
                                        start=(l == 0), stop=(l == 7))
            last.then_inc(place_psum, 1)

            pe.wait_ge(load["w_up"], 32)
            pe.wait_ge(load["w_down"], 16)
            pe.wait_ge(c21_ready, GEMMS)

            def up(e):
                pe.wait_ge(gathered[e], 16 * HALVES)
                for h in range(HALVES):
                    last = nc.tensor.transpose(bank[e % 2][:, h * P:(h + 1) * P], rows[:, h * EXPERTS + e, 0:D],
                                               k32("ident"))
                last.then_inc(rows_psum, 1)
                pe.wait_ge(rows_t_ready, e + 1)
                if e >= 2:
                    pe.wait_ge(hidden_ready, FT * (e - 1))
                pair = bank[2 + 2 * (e % 2)], bank[3 + 2 * (e % 2)]
                for f in range(FT):
                    last = nc.tensor.matmul(pair[f // 2][:, (f % 2) * CAP:(f % 2 + 1) * CAP], w_up[:, e // 2, f, :],
                                            rows_t[e % 2][:, :], start=True, stop=True)
                last.then_inc(up_psum, 1)

            def down(e):
                if e >= 2:
                    pe.wait_ge(expert_ready, HALVES * (e - 1))
                pe.wait_ge(hidden_ready, FT * (e + 1))
                for h in range(HALVES):
                    for f in range(FT):
                        last = nc.tensor.matmul(bank[6 + e % 2][:, h * D:(h + 1) * D], hidden[e % 2][:, f, h * P:(h + 1) * P],
                                                w_down[:, e, f, :], start=(f == 0), stop=(f == FT - 1))
                last.then_inc(down_psum, 1)

            up(0)
            for e in range(EXPERTS):
                if e + 1 < EXPERTS:
                    up(e + 1)
                down(e)

            pe.wait_ge(expert_ready, HALVES * EXPERTS)

            def tokens2(b):
                if b < 2:
                    pe.wait_ge(xn_dve[2], TPB * (b + 1))
                else:
                    pe.wait_ge(xn_pool[2], TPB * (b - 1))

            pe_attention(pe, att[1], 2, tokens2)

            pe.wait_ge(att[1].resid_done, B)
            for b in range(B):
                pe.wait_ge(xn_dve[3] if b < 2 else xn_pool[3], TPB * (b % 2 + 1))
                pe_transpose_tokens(pe, 3, b, bank[b])
            for b in range(B):
                pe.wait_ge(xn_t_ready[3], b + 1)
                for j in range(TPB):
                    t = TPB * b + j
                    last = nc.tensor.matmul(bank[4 + b][:, j * D:(j + 1) * D], xn_t[:, t, :], w21[:, t // TPG, :],
                                            start=True, stop=True)
                last.then_inc(fin_psum, 1)


def _rope_table(heads, interleaved):
    f4 = np.float32
    hd = D // heads
    dim = hd // 2
    e = np.arange(D) % hd
    if interleaved:
        freq = np.exp(-np.arange(dim, dtype=f4) * f4(np.log(f4(10000.0))) / f4(dim)).astype(f4)
        which, sign = e // 2, np.where(e % 2, 1.0, -1.0)
    else:
        freq = (f4(1.0) / np.power(f4(10000.0), np.arange(0, hd, 2, dtype=f4) / f4(hd))).astype(f4)
        which, sign = e % dim, np.where(e < dim, -1.0, 1.0)
    ang = (np.arange(SEQ, dtype=f4)[None, :] * freq[which][:, None]).astype(f4)
    return np.stack([np.cos(ang), np.sin(ang) * sign[:, None]], axis=1).astype(f4)


def _swap(heads, interleaved):
    hd = D // heads
    c = np.arange(D)
    return c ^ 1 if interleaved else np.where(c % hd < hd // 2, c + hd // 2, c - hd // 2)


def _constants():
    p = np.arange(P)
    ke = np.arange(P)
    hd = [D // h for h in HEADS]
    c32 = np.zeros((P, C32_W), np.float32)

    def put(dst, table, name, value):
        dst[:, table[name][0]:table[name][1]] = value

    put(c32, C32, "ident", np.eye(P))
    for a in range(2):
        put(c32, C32, f"head{a}", p[:, None] // hd[a] == np.arange(HEADS[a])[None, :])
        put(c32, C32, f"vmask{a}", (ke[None, :] // hd[a]) % 4 == p[:, None] // KV)
    put(c32, C32, "expert", p[:, None] % EXPERTS == ke[None, :] % EXPERTS)
    gemm = np.arange(GEMMS)
    put(c32, C32, "crow", p[:, None] == (32 * (gemm % 4) + gemm)[None, :])
    put(c32, C32, "ones", 1.0)
    csm = np.zeros((P, CSM_W), np.float16)
    put(csm, CSM, "tri", p[:, None] < ke[None, :])
    put(csm, CSM, "ones", 1.0)
    for a in range(2):
        h = HEADS[a]
        col = np.arange(h * KV)
        put(csm, CSM, f"neg{a}", -1.0 * ((p[:, None] < 2 * h) & (p[:, None] % h == col[None, :] // KV)))
    c16 = np.zeros((P, C16_W), np.float16)
    put(c16, C16, "iota", np.repeat(np.arange(16), EXPERTS)[None, :])
    put(c16, C16, "token", (P * np.arange(TILES)[None, :, None] + p[:, None, None] + np.zeros((1, 1, P))).reshape(P, -1))
    place = np.zeros((P, 8, P))
    for l in range(8):
        place[:, l, :] = ke[None, :] == 16 * l + p[:, None] // EXPERTS
    put(c16, C16, "place", place.reshape(P, -1))
    shifts = BITS * (STEPS - 1 - np.arange(STEPS))
    bits = (np.arange(8)[None, :] << shifts[:, None]).reshape(1, -1).astype(np.int32)
    kbits = np.ascontiguousarray(np.broadcast_to(bits, (P, STEPS * 8)))
    return c32, csm, c16, kbits


def kernel(**inputs):
    import concourse.bacc as bacc
    from concourse.bass_utils import run_bass_kernel_spmd

    g = {k: np.asarray(v) for k, v in inputs.items()}
    c32, csm, c16, kbits = _constants()
    sw = [_swap(HEADS[0], True), _swap(HEADS[1], False)]

    def stack(ws):
        return np.ascontiguousarray(np.stack(ws, axis=1))

    wq, wk, wv, wo = (g[f"L0_xattn_w{n}"].T for n in "qkvo")
    wq1, wkv1, wo1 = g["L1_xattn_Wq"].T, g["L1_xattn_Wkv"].T, g["L1_xattn_Wout"].T
    bq, bk = g["L0_xattn_bq"], g["L0_xattn_bk"]
    pad_f = FT * P - F
    w_up = np.pad(g["L0_ffn_W_up"], ((0, 0), (0, 0), (0, pad_f))).reshape(GROUPS, D, FT, P).transpose(1, 0, 2, 3)
    b_up = np.pad(g["L0_ffn_b_up"], ((0, 0), (0, pad_f))).reshape(GROUPS, FT, P).transpose(2, 0, 1)
    w_down = np.pad(g["L0_ffn_W_down"], ((0, 0), (0, pad_f), (0, 0))).reshape(EXPERTS, FT, P, D).transpose(2, 0, 1, 3).copy()
    w_down[BIAS_ROW, :, FT - 1, :] = g["L0_ffn_b_down"]
    arrays = {
        "x": g["x"].reshape(N_TOK, D), "ctx": g["ctx_1024"].reshape(B * KV, D),
        "c32": c32, "csm": csm, "c16": c16, "kbits": kbits,
        "w_att0": stack([wq, wq[:, sw[0]], wk, wk[:, sw[0]], wv, wo]),
        "w_att1": stack([wq1, wq1[:, sw[1]], wkv1[:, :D], wkv1[:, :D][:, sw[1]], wkv1[:, D:], wo1]),
        "b_col": np.stack([bq, bq[sw[0]], bk, bk[sw[0]]], axis=1),
        "b_row": np.stack([g["L0_xattn_bv"], g["L0_xattn_bo"]]),
        "rope0": _rope_table(HEADS[0], True), "rope1": _rope_table(HEADS[1], False),
        "wr": np.pad(g["L0_ffn_Wr"], ((0, 0), (0, 32 - EXPERTS))),
        "br": np.tile(np.pad(g["L0_ffn_br"], (0, 32 - EXPERTS)), B).reshape(P, 1),
        "w_up": w_up, "b_up": b_up, "w_down": w_down,
        "w1": g["L1_ffn_W1"].reshape(GEMMS, OT, P, D).transpose(2, 0, 1, 3),
        "w2t": g["L1_ffn_W2"].transpose(0, 2, 1).reshape(GEMMS, OT, P, D).transpose(2, 0, 1, 3),
        "b1c": np.repeat(g["L1_ffn_b1"].reshape(GEMMS, OT, P).transpose(2, 1, 0), 1, axis=2),
        "b2": g["L1_ffn_b2"],
    }
    b1 = np.zeros((P, OT, 32), np.float32)
    b1[:, :, 0:GEMMS] = arrays["b1c"]
    arrays["b1c"] = b1

    nc = bacc.Bacc("TRN2", target_bir_lowering=False, num_devices=1)
    ins, feed = {}, {}
    for name, a in arrays.items():
        a = np.ascontiguousarray(a)
        feed[f"in_{name}"] = a
        ins[name] = nc.dram_tensor(f"in_{name}", a.shape, mybir.dt.from_np(a.dtype), kind="ExternalInput").ap()
    out = nc.dram_tensor("out", (N_TOK, D), F32, kind="ExternalOutput").ap()
    build(nc, ins, out)
    r = run_bass_kernel_spmd(nc, [feed], core_ids=[0])
    return r.results[0]["out"].reshape(B, SEQ, D)
```

```python
from contextlib import ExitStack

import numpy as np

import concourse.bass as bass
from concourse import mybir

B, SEQ, D = 4, 512, 128
KV = 32
P = 128
N_TOK = B * SEQ
TILES = N_TOK // P
TPB = SEQ // P
HEADS = (16, 8)
EXPERTS, GROUPS = 8, 4
CAP = N_TOK // EXPERTS
HALVES = CAP // P
F = int(D * 4 * (2.0 / 3.0))
FT = (F + P - 1) // P
BIAS_ROW = 96
F_LAST = BIAS_ROW
GEMMS, INTER = 8, 512
OT = INTER // P
TPG = TILES // GEMMS
BITS = 3
STEPS = 10
CANDS = (1 << BITS) - 1
ROW = D + EXPERTS
SLOT_B = 16
EPS = 1e-5
RSQRT_MAGIC = float(0x5F3759DF)

F32, F32R = mybir.dt.float32, mybir.dt.float32r
BF16, F16 = mybir.dt.bfloat16, mybir.dt.float16
I32, U32 = mybir.dt.int32, mybir.dt.uint32
ALU = mybir.AluOpType
ACT = mybir.ActivationFunctionType
X_AXIS = mybir.AxisListType.X


def columns(**widths):
    at, out = 0, {}
    for name, width in widths.items():
        out[name] = (at, at + width)
        at += width
    return out, at


C32, C32_W = columns(ident=P, head0=16, head1=8, vmask0=P, vmask1=P, expert=P, crow=8, ones=P)
CSM, CSM_W = columns(tri=P, ones=P, neg0=4 * P, neg1=2 * P)
C16, C16_W = columns(iota=P, token=TILES * P, place=8 * P)
W_Q, W_QS, W_K, W_KS, W_V, W_O = range(6)


class Chain:

    def __init__(self, engine, semaphore):
        self.engine, self.semaphore, self.count = engine, semaphore, 0

    def step(self, instruction):
        instruction.then_inc(self.semaphore, 1)
        self.count += 1

    def settle(self):
        self.engine.wait_ge(self.semaphore, self.count)


def build(nc, ins, out):
    with ExitStack() as ctx:
        def sb(name, shape, dt=F32):
            return ctx.enter_context(nc.sbuf_tensor(name, shape, dt))

        def sem(name):
            return ctx.enter_context(nc.semaphore(name))

        bank = [ctx.enter_context(nc.psum_tensor(f"bank{i}", [P, 512], F32)) for i in range(8)]
        TX = bank[0]
        ring = bank[1:4]
        score_bank = bank[4:6]
        fin_bank = ring + score_bank[1:2]
        ctx_bank, sum_bank = bank[6], bank[7]

        dispatch = nc.dram_tensor("dispatch_rows", [N_TOK, ROW], F32).ap()
        y_even = nc.dram_tensor("y_even", [N_TOK, D], F32).ap()
        y_odd = nc.dram_tensor("y_odd", [N_TOK, D], F32).ap()

        c32 = sb("c32", [P, C32_W])
        csm = sb("csm", [P, CSM_W], F16)
        ident_bf = sb("ident_bf", [P, P], BF16)
        c16 = sb("c16", [P, C16_W], F16)
        kbits = sb("kbits", [P, STEPS * 8], I32)

        def k32(name):
            return c32[:, C32[name][0]:C32[name][1]]

        def ksm(name):
            return csm[:, CSM[name][0]:CSM[name][1]]

        def k16(name):
            return c16[:, C16[name][0]:C16[name][1]]

        w_att = [sb(f"w_att{a}", [P, 6, D]) for a in range(2)]
        b_col = sb("b_col", [P, 4])
        b_row = sb("b_row", [P, 2, D])
        rope = [sb(f"rope{a}", [P, 2, SEQ]) for a in range(2)]
        ctx_rows = sb("ctx_rows", [P, D])
        ctx_t = sb("ctx_t", [P, B, 4, KV])
        wr = sb("wr", [P, 32])
        br = sb("br", [P, 1])
        w_up = sb("w_up", [P, GROUPS, FT, P])
        b_up = sb("b_up", [P, GROUPS, FT])
        w_down = sb("w_down", [P, EXPERTS, FT, D])
        w1 = sb("w1", [P, GEMMS, OT, D])
        w2t = sb("w2t", [P, GEMMS, OT, D])
        b1c = sb("b1c", [P, OT, 32])
        b2b = sb("b2b", [P, GEMMS, D])
        w21 = sb("w21", [P, GEMMS, D])
        c21 = sb("c21", [P, GEMMS, D])
        c_raw = sb("c_raw", [P, 2 * D])
        c_one = sb("c_one", [P, GEMMS, D])

        x_in = sb("x_in", [P, TILES, D])
        x_mid = sb("x_mid", [P, TILES, D])
        x_add = sb("x_add", [P, TILES, D])
        xn = sb("xn", [P, TILES, D])
        xn_t = sb("xn_t", [P, TILES, P])
        stats = sb("stats", [P, TILES, 6])
        moments = sb("moments", [P, TILES, 2])
        rstd = sb("rstd", [P, TILES])
        ln_a = sb("ln_a", [P, TILES])
        ln_v = sb("ln_v", [P, TILES])

        k_rot = sb("k_rot", [P, B, KV])
        k_a = sb("k_a", [P, B, KV])
        k_b = sb("k_b", [P, B, KV])
        k_bd = sb("k_bd", [P, B, 512])
        k_bdr = sb("k_bdr", [P, B, 512], F32R)
        v_raw = sb("v_raw", [P, B, D])
        v_bd = sb("v_bd", [P, B, D])
        q_a = sb("q_a", [P, SEQ])
        q_b = sb("q_b", [P, SEQ])
        q_t = [sb(f"q_t{i}", [P, SEQ]) for i in range(2)]
        q_tr = [sb(f"q_tr{i}", [P, SEQ], F32R) for i in range(2)]
        m_max = sb("m_max", [P, TPB, 16])
        m_hl = [sb(f"m_hl{i}", [P, TPB, 32], BF16) for i in range(2)]
        m_t = [sb(f"m_t{i}", [P, SEQ], BF16) for i in range(2)]
        probs_all = sb("probs", [P, 4, SEQ])
        probs = [probs_all[:, i, :] for i in range(4)]
        recip = sb("recip", [P, SEQ])
        att_t = [sb(f"att_t{i}", [P, SEQ]) for i in range(2)]

        logit_t = sb("logit_t", [P, SEQ])
        logit = sb("logit", [P, TILES, EXPERTS])
        l_max = sb("l_max", [P, TILES])
        l_exp = sb("l_exp", [P, TILES, EXPERTS])
        l_sum = sb("l_sum", [P, TILES])
        weight = sb("weight", [P, TILES, EXPERTS])
        cand = sb("cand", [P, EXPERTS, 8], I32)
        hit = [sb(f"hit{i}", [P, EXPERTS, 8]) for i in range(2)]
        above = sb("above", [P, CANDS, TILES, EXPERTS], BF16)
        picks = sb("picks", [P, 2, TILES, EXPERTS], BF16)
        n_above = sb("n_above", [P, TILES])
        pos_a = sb("pos_a", [P, TILES, EXPERTS])
        pos_b = sb("pos_b", [P, TILES, EXPERTS])
        pos_i = sb("pos_i", [P, TILES, EXPERTS], I32)
        pos_d = sb("pos_d", [P, 2, TILES, EXPERTS], I32)
        pos_h = sb("pos_h", [P, 2, TILES, EXPERTS], F16)
        onehot_a, onehot_b = (probs_all[:, 2 * i:2 * i + 2, :].rearrange("p a n -> p (a n)").bitcast(F16)
                              .rearrange("p (t a e) -> p t a e", t=TILES, a=16) for i in range(2))
        ids = sb("ids", [P, P], F16)
        slot_token = sb("slot_token", [P, HALVES * EXPERTS], I32)
        rows = (w1[:, :, :, :].rearrange("p g k d -> p (g k d)")[:, 0:EXPERTS * HALVES * ROW]
                .rearrange("p (c r) -> p c r", r=ROW))
        rows_t = [sb(f"rows_t{i}", [P, CAP]) for i in range(2)]
        hidden = [sb(f"hidden{i}", [P, FT, CAP]) for i in range(2)]
        expert_out = xn_t[:, :, :].rearrange("p (e h) d -> p e h d", h=HALVES)
        zero = sb("zero", [P, D])

        load = {n: sem(f"load_{n}") for n in (
            "x0", "x1", "x2", "x3", "c32", "csm", "c16", "kbits", "w_att0", "w_att1", "b_col", "b_row",
            "rope0", "rope1", "ctx", "router", "w_up", "w_down", "w1", "w2t", "b1c", "b2b")}
        dve_step = sem("dve_step")
        pool_step = sem("pool_step")
        zeroed = sem("zeroed")
        moments_ready = [sem(f"moments_ready{n}") for n in range(4)]
        xn_dve = [sem(f"xn_dve{n}") for n in range(4)]
        xn_pool = [sem(f"xn_pool{n}") for n in range(4)]
        xn_psum = [sem(f"xn_psum{n}") for n in range(4)]
        xn_t_ready = [sem(f"xn_t_ready{n}") for n in range(4)]

        class Attention:

            def __init__(self, a):
                self.a, self.heads = a, HEADS[a]
                self.hg = self.heads // 4
                self.cols = 4 * D // self.heads
                self.scale = float(D // self.heads) ** -0.5
                self.ctx_psum = sem(f"ctx_psum_{a}")
                self.ctx_t_ready = sem(f"ctx_t_ready_{a}")
                self.k_psum = sem(f"k_psum_{a}")
                self.k_rot_ready = sem(f"k_rot_ready_{a}")
                self.k_bd_dve = sem(f"k_bd_dve_{a}")
                self.k_bd_pool = sem(f"k_bd_pool_{a}")
                self.v_psum = sem(f"v_psum_{a}")
                self.v_raw_ready = sem(f"v_raw_ready_{a}")
                self.v_bd_ready = sem(f"v_bd_ready_{a}")
                self.ring_filled = sem(f"ring_filled_{a}")
                self.ring_read = sem(f"ring_read_{a}")
                self.q_ready = sem(f"q_ready_{a}")
                self.qr_ready = sem(f"qr_ready_{a}")
                self.m_ready = sem(f"m_ready_{a}")
                self.m_psum = sem(f"m_psum_{a}")
                self.m_t_ready = sem(f"m_t_ready_{a}")
                self.scores_ready = sem(f"scores_ready_{a}")
                self.probs_ready = sem(f"probs_ready_{a}")
                self.sum_ready = sem(f"sum_ready_{a}")
                self.ctx_ready = sem(f"ctx_ready_{a}")
                self.recip_ready = sem(f"recip_ready_{a}")
                self.att_ready = sem(f"att_ready_{a}")
                self.out_psum = sem(f"out_psum_{a}")
                self.resid_done = sem(f"resid_done_{a}")

        att = [Attention(0), Attention(1)]
        bo_added = sem("bo_added")
        ident_ready = sem("ident_ready")
        router_psum, logit_t_ready = sem("router_psum"), sem("logit_t_ready")
        logit_psum, logit_ready, l_exp_ready = sem("logit_psum"), sem("logit_ready"), sem("l_exp_ready")
        weight_ready = sem("weight_ready")
        above_ready, counted = sem("above_ready"), sem("counted")
        picks_ready, prefix_ready = sem("picks_ready"), sem("prefix_ready")
        onehot_ready, ids_psum, ids_ready, place_psum, slots_ready = (
            sem("onehot_ready"), sem("ids_psum"), sem("ids_ready"), sem("place_psum"), sem("slots_ready"))
        dispatched = [sem(f"dispatched{i}") for i in range(2)]
        y_init = sem("y_init")
        gathered = [sem(f"gathered{i}") for i in range(EXPERTS)]
        rows_psum, rows_t_ready = sem("rows_psum"), sem("rows_t_ready")
        up_psum, hidden_ready = sem("up_psum"), sem("hidden_ready")
        down_psum, expert_ready = sem("down_psum"), sem("expert_ready")
        added = [sem(f"added{i}") for i in range(2)]
        y_loaded = [sem(f"y_loaded{b}") for b in range(B)]
        x2_ready = sem("x2_ready")
        c_psum, c_raw_ready, c_one_ready, cb_psum, c21_ready = (
            sem("c_psum"), sem("c_raw_ready"), sem("c_one_ready"), sem("cb_psum"), sem("c21_ready"))
        w21_psum, w21_ready = sem("w21_psum"), sem("w21_ready")
        x3c_ready = sem("x3c_ready")
        fin_psum, fin_ready = sem("fin_psum"), sem("fin_ready")
        stored = sem("stored")

        def tok(ap):
            return ap.rearrange("(t p) d -> p t d", p=P)

        def wait_tokens_early(engine, n, b, j=TPB - 1):
            if b == 0:
                engine.wait_ge(xn_dve[n], j + 1)
            else:
                engine.wait_ge(xn_pool[n], b)

        def wait_tokens_late(engine, n, b, j=TPB - 1):
            if b == B - 1:
                engine.wait_ge(xn_dve[n], j + 1)
            else:
                engine.wait_ge(xn_pool[n], b + 1)

        block = ctx.enter_context(nc.Block())

        @block.sync
        def _(sp):
            def get(dst, src, name):
                sp.dma_start(dst, src).then_inc(load[name], 16)

            def get_x(b):
                get(x_in[:, TPB * b:TPB * (b + 1), :], tok(ins["x"])[:, TPB * b:TPB * (b + 1), :], f"x{b}")

            get_x(0)
            get(c32[:, :], ins["c32"], "c32")
            get(w_att[0][:, :, :], ins["w_att0"], "w_att0")
            for b in range(1, B):
                get_x(b)
            get(csm[:, :], ins["csm"], "csm")
            get(b_row[:, :, :], ins["b_row"][None, :, :].to_broadcast([P, 2, D]), "b_row")
            get(wr[:, :], ins["wr"], "router")
            get(br[:, :], ins["br"], "router")
            get(rope[1][:, :, :], ins["rope1"], "rope1")
            get(w_att[1][:, :, :], ins["w_att1"], "w_att1")
            get(kbits[:, :], ins["kbits"], "kbits")
            get(b1c[:, :, :], ins["b1c"], "b1c")
            get(w2t[:, :, :, :], ins["w2t"], "w2t")
            get(w1[:, :, :, :], ins["w1"], "w1")
            get(b2b[:, :, :], ins["b2"][None, :, :].to_broadcast([P, GEMMS, D]), "b2b")
            get(c16[:, :], ins["c16"], "c16")
            get(w_up[:, :, :, :], ins["w_up"], "w_up")
            get(b_up[:, :, :], ins["b_up"], "w_up")
            get(w_down[:, :, :, :], ins["w_down"], "w_down")

            sp.wait_ge(zeroed, 1)
            sp.dma_start(tok(y_odd), zero[:, None, :].to_broadcast([P, TILES, D])).then_inc(y_init, 16)
            for b in range(B):
                span = slice(TPB * b, TPB * (b + 1))
                wait_tokens_late(sp, 1, b)
                sp.dma_start(tok(dispatch)[:, span, 0:D], xn[:, span, :]).then_inc(dispatched[0], 16)
                sp.wait_ge(att[0].resid_done, b + 1)
                sp.dma_start(tok(y_even)[:, span, :], x_mid[:, span, :]).then_inc(y_init, 16)
            sp.wait_ge(weight_ready, 1)
            sp.dma_start(tok(dispatch)[:, :, D:ROW], weight[:, :, :]).then_inc(dispatched[1], 16)
            sp.wait_ge(added[0], 16 * HALVES * EXPERTS // 2)
            sp.wait_ge(added[1], 16 * HALVES * EXPERTS // 2)
            for b in range(B):
                span = slice(TPB * b, TPB * (b + 1))
                sp.dma_start(x_in[:, span, :], tok(y_even)[:, span, :]).then_inc(y_loaded[b], 16)
                sp.dma_start(x_add[:, span, :], tok(y_odd)[:, span, :]).then_inc(y_loaded[b], 16)
            for b in range(B):
                sp.wait_ge(fin_ready, b + 1 if b < B - 1 else B - 1 + TPB)
                sp.dma_start(tok(out)[:, TPB * b:TPB * (b + 1), :], xn[:, TPB * b:TPB * (b + 1), :]).then_inc(stored, 16)
            sp.wait_ge(stored, 16 * B)

        def pe_prepare_kv(pe, L, first):
            W = w_att[L.a]
            pe.wait_ge(load[f"w_att{L.a}"], 16)
            if first:
                pe.wait_ge(load["ctx"], 16)
                pe.wait_ge(load["c32"], 16)
                nc.tensor.transpose(score_bank[0][:, 0:P], ctx_rows[:, :], k32("ident")).then_inc(L.ctx_psum, 1)
                pe.wait_ge(L.ctx_t_ready, 1)
            keys = ctx_t[:, :, 0, :]
            nc.tensor.matmul(score_bank[1][:, 0:P], W[:, W_K, :], keys, start=True, stop=True)
            nc.tensor.matmul(score_bank[1][:, P:2 * P], W[:, W_KS, :], keys, start=True, stop=True).then_inc(L.k_psum, 1)
            for b in range(B):
                last = nc.tensor.matmul(ctx_bank[:, b * P:(b + 1) * P], ctx_t[:, b, :, :], W[:, W_V, :],
                                        start=True, stop=True)
            last.then_inc(L.v_psum, 1)

        def dve_rotate_keys(dve, chain, L):
            cos = rope[L.a][:, 0, 0:KV][:, None, :].to_broadcast([P, B, KV])
            sin = rope[L.a][:, 1, 0:KV][:, None, :].to_broadcast([P, B, KV])
            kp = score_bank[1][:, 0:P].rearrange("p (b k) -> p b k", b=B)
            ks = score_bank[1][:, P:2 * P].rearrange("p (b k) -> p b k", b=B)
            dve.wait_ge(load[f"rope{L.a}"], 16)
            if L.a == 0:
                dve.wait_ge(load["b_col"], 16)
            dve.wait_ge(L.k_psum, 1)
            if L.a == 0:
                chain.step(nc.vector.scalar_tensor_tensor(k_a[:, :, :], kp, b_col[:, 2:3], cos, ALU.add, ALU.mult))
                chain.step(nc.vector.scalar_tensor_tensor(k_b[:, :, :], ks, b_col[:, 3:4], sin, ALU.add, ALU.mult))
            else:
                chain.step(nc.vector.tensor_tensor(k_a[:, :, :], kp, cos, ALU.mult))
                chain.step(nc.vector.tensor_tensor(k_b[:, :, :], ks, sin, ALU.mult))
            chain.settle()
            nc.vector.tensor_tensor(k_rot[:, :, :], k_a[:, :, :], k_b[:, :, :], ALU.add).then_inc(L.k_rot_ready, 1)

        def dve_first_keys(dve, L):
            dve.wait_ge(L.k_rot_ready, 1)
            for dst in (k_bdr, k_bd):
                spread_keys(nc.vector, L, 0, dst).then_inc(L.k_bd_dve, 1)

        def dve_values(dve, L):
            dve.wait_ge(L.v_psum, 1)
            vp = ctx_bank[:, :].rearrange("p (b e) -> p b e", b=B)
            mask = k32(f"vmask{L.a}")[:, None, :].to_broadcast([P, B, D])
            if L.a == 0:
                dve.wait_ge(load["b_row"], 16)
                nc.vector.tensor_tensor(v_raw[:, :, :], vp, b_row[:, 0:1, :].to_broadcast([P, B, D]),
                                        ALU.add).then_inc(L.v_raw_ready, 1)
                dve.wait_ge(L.v_raw_ready, 1)
                nc.vector.tensor_tensor(v_bd[:, :, :], v_raw[:, :, :], mask, ALU.mult).then_inc(L.v_bd_ready, 1)
            else:
                nc.vector.tensor_tensor(v_bd[:, :, :], vp, mask, ALU.mult).then_inc(L.v_bd_ready, 1)

        def spread_keys(engine, L, b, dst):
            o = dst[:, b, 0:L.heads * KV].rearrange("p (h k) -> p h k", h=L.heads)
            return engine.tensor_tensor(o, k_rot[:, b:b + 1, :].to_broadcast([P, L.heads, KV]),
                                        k32(f"head{L.a}")[:, :, None].to_broadcast([P, L.heads, KV]), ALU.mult)

        def pe_transpose_tokens(pe, n, b, dst):
            for j in range(TPB):
                (wait_tokens_late if n % 2 else wait_tokens_early)(pe, n, b, j)
                last = nc.tensor.transpose(dst[:, j * P:(j + 1) * P], xn[:, TPB * b + j, :], k32("ident"))
            last.then_inc(xn_psum[n], 1)

        def uses(L):
            return 2 + L.hg

        def pe_fill(pe, L, u):
            if u >= 3:
                pe.wait_ge(L.ring_read, u - 2)
            return ring[u % 3]

        def pe_project_q(pe, L, n, b):
            W = w_att[L.a]
            pe_transpose_tokens(pe, n, b, TX)
            pe.wait_ge(xn_t_ready[n], b + 1)
            rhs = xn_t[:, TPB * b:TPB * (b + 1), :].rearrange("p j t -> p (j t)")
            for i, w in enumerate((W_Q, W_QS)):
                dst = pe_fill(pe, L, uses(L) * b + i)
                nc.tensor.matmul(dst[:, :], W[:, w, :], rhs, start=True, stop=True).then_inc(L.ring_filled, 1)

        def pe_max_scores(pe, L, b, i):
            width = L.heads * KV
            per = 512 // width
            dst = pe_fill(pe, L, uses(L) * b + 2 + i)
            pe.wait_ge(L.qr_ready, b + 1)
            for k in range(per):
                j = i * per + k
                last = nc.tensor.matmul(dst[:, k * width:(k + 1) * width], q_tr[b % 2][:, j * P:(j + 1) * P],
                                        k_bdr[:, b, 0:width], start=True, stop=True)
            last.then_inc(L.ring_filled, 1)

        def pe_transpose_maxima(pe, L, n, b):
            rows_m = 2 * L.heads
            if b == B - 1:
                pe.wait_ge(xn_t_ready[n + 1], 1)
            pe.wait_ge(L.m_ready, b + 1)
            mt = TX[:, :].bitcast(BF16)
            for j in range(TPB):
                last = nc.tensor.transpose(mt[0:rows_m, j * P:(j + 1) * P], m_hl[b % 2][:, j, 0:rows_m], ident_bf[:, :])
            last.then_inc(L.m_psum, 1)

        def pe_scores(pe, L, b, g):
            v = L.hg * b + g
            if g == 0:
                pe.wait_ge(L.q_ready, b + 1)
            if v >= 2:
                pe.wait_ge(L.probs_ready, v - 1)
            nc.tensor.matmul(score_bank[v % 2][:, :], k_bd[:, b, g * P:(g + 1) * P], q_t[b % 2][:, :],
                             start=True, stop=False)
            if g == 0:
                pe.wait_ge(L.m_t_ready, b + 1)
            nc.tensor.matmul(score_bank[v % 2][:, :], ksm(f"neg{L.a}")[:, g * P:(g + 1) * P], m_t[b % 2][:, :],
                             start=False, stop=True).then_inc(L.scores_ready, 1)

        def pe_values(pe, L, b):
            for dst in (ctx_bank, sum_bank):
                if b >= 1 and dst is ctx_bank:
                    pe.wait_ge(L.att_ready, b)
                if b >= 1 and dst is sum_bank:
                    pe.wait_ge(L.resid_done, b)
                for g in range(L.hg):
                    pe.wait_ge(L.probs_ready, L.hg * b + g + 1)
                    w = (k32(f"vmask{L.a}")[:, 0:L.cols] if dst is sum_bank
                         else v_bd[:, b, g * L.cols:(g + 1) * L.cols])
                    last = nc.tensor.matmul(dst[g * L.cols:(g + 1) * L.cols, :], w, probs[(L.hg * b + g) % 4][:, :],
                                            start=True, stop=True)
                last.then_inc(L.sum_ready if dst is sum_bank else L.ctx_ready, 1)

        def pe_project_out(pe, L, b):
            pe.wait_ge(L.att_ready, b + 1)
            for j in range(TPB):
                last = nc.tensor.matmul(sum_bank[:, j * P:(j + 1) * P], att_t[b % 2][:, j * P:(j + 1) * P],
                                        w_att[L.a][:, W_O, :], start=True, stop=True)
            last.then_inc(L.out_psum, 1)

        def pe_attention(pe, L, n, aside):
            def keys_ready(b):
                if b == 0:
                    pe.wait_ge(L.k_bd_dve, 2)
                else:
                    pe.wait_ge(L.k_bd_pool, 2 * b)

            pe_project_q(pe, L, n, 0)
            keys_ready(0)
            for i in range(L.hg):
                pe_max_scores(pe, L, 0, i)
            pe_project_q(pe, L, n, 1)
            for b in range(B):
                pe_transpose_maxima(pe, L, n, b)
                if b + 1 < B:
                    keys_ready(b + 1)
                for g in range(L.hg):
                    pe_scores(pe, L, b, g)
                    if b + 1 < B:
                        pe_max_scores(pe, L, b + 1, g)
                if b >= 1:
                    pe_project_out(pe, L, b - 1)
                if b + 2 < B:
                    pe_project_q(pe, L, n, b + 2)
                else:
                    pe_transpose_tokens(pe, n + 1, b - 2, TX)
                if b == 0:
                    pe.wait_ge(L.v_bd_ready, 1)
                pe_values(pe, L, b)
            pe.wait_ge(L.ring_read, uses(L) * B)
            aside()
            pe_project_out(pe, L, B - 1)

        def act_tokens(act, n, b, src):
            act.wait_ge(xn_psum[n], b + 1)
            nc.scalar.activation(xn_t[:, TPB * b:TPB * (b + 1), :].rearrange("p j t -> p (j t)"), src[:, :],
                                 ACT.Copy).then_inc(xn_t_ready[n], 1)

        def act_attention(act, L, n):
            def tokens(b):
                act_tokens(act, n, b, TX)

            def rounded_q(b):
                act.wait_ge(L.q_ready, b + 1)
                nc.scalar.activation(q_tr[b % 2][:, :], q_t[b % 2][:, :], ACT.Copy).then_inc(L.qr_ready, 1)

            tokens(0)
            rounded_q(0)
            tokens(1)
            rounded_q(1)
            for b in range(B):
                rows_m = 2 * L.heads
                act.wait_ge(L.m_psum, b + 1)
                nc.scalar.activation(m_t[b % 2][0:rows_m, :], TX[:, :].bitcast(BF16)[0:rows_m, 0:SEQ],
                                     ACT.Copy).then_inc(L.m_t_ready, 1)
                for g in range(L.hg):
                    v = L.hg * b + g
                    act.wait_ge(L.scores_ready, v + 1)
                    if v >= 4:
                        act.wait_ge(L.sum_ready, (v - 4) // L.hg + 1)
                    nc.scalar.activation(probs[v % 4][:, :], score_bank[v % 2][:, :], ACT.Exp,
                                         scale=L.scale).then_inc(L.probs_ready, 1)
                if b + 2 < B:
                    tokens(b + 2)
                    rounded_q(b + 2)
                else:
                    act_tokens(act, n + 1, b - 2, TX)

        def dve_attention(dve, chain, L, n, resid, aside):
            cos, sin = rope[L.a][:, 0, :], rope[L.a][:, 1, :]

            def query(b):
                u = uses(L) * b
                dve.wait_ge(L.ring_filled, u + 1)
                if L.a == 0:
                    nc.vector.scalar_tensor_tensor(q_a[:, :], ring[u % 3][:, :], b_col[:, 0:1], cos,
                                                   ALU.add, ALU.mult).then_inc(L.ring_read, 1)
                else:
                    nc.vector.tensor_tensor(q_a[:, :], ring[u % 3][:, :], cos, ALU.mult).then_inc(L.ring_read, 1)
                dve.wait_ge(L.ring_filled, u + 2)
                if L.a == 0:
                    nc.vector.scalar_tensor_tensor(q_b[:, :], ring[(u + 1) % 3][:, :], b_col[:, 1:2], sin,
                                                   ALU.add, ALU.mult).then_inc(L.ring_read, 1)
                else:
                    nc.vector.tensor_tensor(q_b[:, :], ring[(u + 1) % 3][:, :], sin, ALU.mult).then_inc(L.ring_read, 1)
                dve.wait_ge(L.ring_read, u + 2)
                nc.vector.tensor_tensor(q_t[b % 2][:, :], q_a[:, :], q_b[:, :], ALU.add).then_inc(L.q_ready, 1)

            def maximum(b):
                per = TPB // L.hg
                for i in range(L.hg):
                    u = uses(L) * b + 2 + i
                    dve.wait_ge(L.ring_filled, u + 1)
                    nc.vector.tensor_reduce(m_max[:, i * per:(i + 1) * per, 0:L.heads],
                                            ring[u % 3][:, :].rearrange("p (j h k) -> p j h k", j=per, h=L.heads),
                                            X_AXIS, ALU.max).then_inc(L.ring_read, 1)
                dve.wait_ge(L.ring_read, uses(L) * (b + 1))
                hi, lo = m_hl[b % 2][:, :, 0:L.heads], m_hl[b % 2][:, :, L.heads:2 * L.heads]
                chain.step(nc.vector.tensor_copy(hi, m_max[:, :, 0:L.heads]))
                chain.settle()
                nc.vector.tensor_tensor(lo, m_max[:, :, 0:L.heads], hi, ALU.subtract).then_inc(L.m_ready, 1)

            def normalise(b):
                dve.wait_ge(L.sum_ready, b + 1)
                nc.vector.reciprocal(recip[:, :], sum_bank[:, :]).then_inc(L.recip_ready, 1)
                dve.wait_ge(L.recip_ready, b + 1)
                dve.wait_ge(L.ctx_ready, b + 1)
                nc.vector.tensor_tensor(att_t[b % 2][:, :], ctx_bank[:, :], recip[:, :], ALU.mult).then_inc(L.att_ready, 1)

            def residual(b):
                dve.wait_ge(L.out_psum, b + 1)
                if L.a == 0:
                    dve.wait_ge(bo_added, b + 1)
                span = slice(TPB * b, TPB * (b + 1))
                nc.vector.tensor_tensor(x_mid[:, span, :].rearrange("p j d -> p (j d)"), sum_bank[:, :],
                                        resid[:, span, :].rearrange("p j d -> p (j d)"),
                                        ALU.add).then_inc(L.resid_done, 1)
                dve.wait_ge(L.resid_done, b + 1)
                dve_moments(chain, n + 1, x_mid, b)

            query(0)
            maximum(0)
            query(1)
            for b in range(B):
                if b + 1 < B:
                    maximum(b + 1)
                if b >= 1:
                    residual(b - 1)
                if b + 2 < B:
                    query(b + 2)
                normalise(b)
            aside()
            residual(B - 1)

        def dve_moments(chain, n, x, b):
            for t in range(TPB * b, TPB * (b + 1)):
                chain.step(nc.vector.bn_stats(stats[:, t, :], x[:, t, :]))
            chain.settle()
            for t in range(TPB * b, TPB * (b + 1)):
                last = nc.vector.bn_aggr(moments[:, t, :], stats[:, t, :])
            last.then_inc(moments_ready[n], 1)

        def first_guess(engine, ops, chain, n, b):
            span = slice(TPB * b, TPB * (b + 1))
            r, v = rstd[:, span], ln_v[:, span]
            engine.wait_ge(moments_ready[n], b + 1)
            chain.step(ops.tensor_scalar(v, moments[:, span, 1], EPS, None, ALU.add))
            chain.settle()
            chain.step(ops.tensor_scalar(r.bitcast(I32), v.bitcast(I32), -0.5, RSQRT_MAGIC, ALU.mult, ALU.add))
            chain.settle()
            return r, ln_a[:, span], v

        def inverse_deviation(dve, chain, n, b):
            r, a, v = first_guess(dve, nc.vector, chain, n, b)
            for _ in range(3):
                chain.step(nc.vector.scalar_tensor_tensor(a, r, -0.5, r, ALU.mult, ALU.mult))
                chain.settle()
                chain.step(nc.vector.tensor_tensor(a, a, v, ALU.mult))
                chain.settle()
                chain.step(nc.vector.scalar_tensor_tensor(r, a, 1.5, r, ALU.add, ALU.mult))
                chain.settle()

        def dve_normalise(x, n, t):
            nc.vector.tensor_scalar(xn[:, t, :], x[:, t, :], moments[:, t, 0:1], rstd[:, t:t + 1],
                                    ALU.subtract, ALU.mult).then_inc(xn_dve[n], 1)

        def pool_normalise(pool, chain, x, n, b):
            ops = nc.gpsimd
            span = slice(TPB * b, TPB * (b + 1))
            r, a, v = first_guess(pool, ops, chain, n, b)
            chain.step(ops.tensor_scalar(v, v, -0.5, None, ALU.mult))
            for _ in range(3):
                chain.step(ops.tensor_tensor(a, r, r, ALU.mult))
                chain.settle()
                chain.step(ops.tensor_tensor(a, a, v, ALU.mult))
                chain.settle()
                chain.step(ops.tensor_scalar(a, a, 1.5, None, ALU.add))
                chain.settle()
                chain.step(ops.tensor_tensor(r, r, a, ALU.mult))
                chain.settle()
            if n == 1 or n == 3:
                pool.wait_ge(xn_psum[n - 1], b + 1)
            chain.step(ops.tensor_tensor(xn[:, span, :], x[:, span, :],
                                         moments[:, span, 0:1].to_broadcast([P, TPB, D]), ALU.subtract))
            chain.settle()
            ops.tensor_tensor(xn[:, span, :], xn[:, span, :], rstd[:, span][:, :, None].to_broadcast([P, TPB, D]),
                              ALU.mult).then_inc(xn_pool[n], 1)

        @block.gpsimd
        def _(pool):
            chain = Chain(pool, pool_step)
            P_ = nc.gpsimd
            chain.step(P_.memset(m_t[0][:, :], 0.0))
            chain.step(P_.memset(m_t[1][:, :], 0.0))
            for i in range(2):
                chain.settle()
                chain.step(P_.memset(hidden[i][BIAS_ROW:P, FT - 1, :], 1.0))
            chain.settle()
            P_.memset(zero[:, :], 0.0).then_inc(zeroed, 1)

            def keys(L):
                pool.wait_ge(L.k_rot_ready, 1)
                for b in range(1, B):
                    for dst in (k_bdr, k_bd):
                        spread_keys(P_, L, b, dst).then_inc(L.k_bd_pool, 1)

            pool.wait_ge(load["c32"], 16)
            pool_normalise(pool, chain, x_in, 0, 1)
            pool.wait_ge(att[0].k_rot_ready, 1)
            for b in range(1, B):
                if b > 1:
                    pool_normalise(pool, chain, x_in, 0, b)
                for dst in (k_bdr, k_bd):
                    spread_keys(P_, att[0], b, dst).then_inc(att[0].k_bd_pool, 1)
            pool.wait_ge(load["b_row"], 16)
            for b in range(B):
                P_.tensor_tensor(x_add[:, TPB * b:TPB * (b + 1), :], x_in[:, TPB * b:TPB * (b + 1), :],
                                 b_row[:, 1:2, :].to_broadcast([P, TPB, D]), ALU.add).then_inc(bo_added, 1)

            for b in range(B - 1):
                pool_normalise(pool, chain, x_mid, 1, b)
            keys(att[1])

            def gather(e):
                if e == 0:
                    pool.wait_ge(slots_ready, 1)
                    pool.wait_ge(dispatched[0], 16 * B)
                    pool.wait_ge(dispatched[1], 16)
                for h in range(HALVES):
                    c = h * EXPERTS + e
                    P_.indirect_dma_start(
                        rows[:, c, :], None, dispatch,
                        bass.IndirectOffsetOnAxis(ap=slot_token[:, c:c + 1].bitcast(U32), axis=0)).then_inc(gathered[e], 16)

            def add(e):
                pool.wait_ge(expert_ready, HALVES * (e + 1))
                if e < 2:
                    pool.wait_ge(y_init, 16 * (B + 1))
                else:
                    pool.wait_ge(added[e % 2], 16 * HALVES * (e // 2))
                for h in range(HALVES):
                    c = h * EXPERTS + e
                    P_.indirect_dma_start(
                        y_odd if e % 2 else y_even,
                        bass.IndirectOffsetOnAxis(ap=slot_token[:, c:c + 1].bitcast(U32), axis=0),
                        expert_out[:, e, h, :], None, compute_op=ALU.add).then_inc(added[e % 2], 16)

            AHEAD = 4
            for e in range(AHEAD):
                gather(e)
            for e in range(EXPERTS):
                add(e)
                if e + AHEAD < EXPERTS:
                    gather(e + AHEAD)

            for b in range(1, B):
                pool_normalise(pool, chain, x_in, 2, b)
            pool.wait_ge(c21_ready, GEMMS)
            for b in range(B):
                if b < B - 1:
                    pool_normalise(pool, chain, x_mid, 3, b)
                else:
                    pool.wait_ge(att[1].resid_done, B)
                for g in range(2 * b, 2 * b + 2):
                    P_.tensor_tensor(x_add[:, TPG * g:TPG * (g + 1), :], x_mid[:, TPG * g:TPG * (g + 1), :],
                                     c21[:, g:g + 1, :].to_broadcast([P, TPG, D]), ALU.add).then_inc(x3c_ready, 1)

        @block.scalar
        def _(act):
            def get(dst, src, name):
                act.dma_start(dst, src).then_inc(load[name], 16)

            get(ctx_rows[:, :], ins["ctx"], "ctx")
            get(rope[0][:, :, :], ins["rope0"], "rope0")
            get(b_col[:, :], ins["b_col"], "b_col")

            act.wait_ge(att[0].ctx_psum, 1)
            nc.scalar.activation(
                ctx_t[:, :, :, :],
                score_bank[0][:, 0:P].rearrange("p (b k) -> p b k", b=B)[:, :, None, :].to_broadcast([P, B, 4, KV]),
                ACT.Copy).then_inc(att[0].ctx_t_ready, 1)
            nc.scalar.activation(ident_bf[:, :], k32("ident"), ACT.Copy).then_inc(ident_ready, 1)
            act.wait_ge(zeroed, 1)
            act_attention(act, att[0], 0)

            for b in (B - 2, B - 1):
                act_tokens(act, 1, b, bank[b])
            act.wait_ge(load["router"], 32)
            act.wait_ge(router_psum, 1)
            nc.scalar.activation(logit_t[:, :], bank[4][:, :], ACT.Identity, bias=br[:, 0:1]).then_inc(logit_t_ready, 1)
            act.wait_ge(logit_ready, 1)
            nc.scalar.activation(l_exp[:, :, :], logit[:, :, :], ACT.Exp).then_inc(l_exp_ready, 1)

            act.wait_ge(c_psum, 1)
            nc.scalar.activation(c_raw[:, :], bank[7][:, 0:2 * D], ACT.Copy).then_inc(c_raw_ready, 1)
            for g in range(GEMMS):
                act.wait_ge(w21_psum, g + 1)
                nc.scalar.activation(w21[:, g, :], bank[2 + g % 2][:, 0:D], ACT.Copy).then_inc(w21_ready, 1)
            for e in range(EXPERTS):
                act.wait_ge(rows_psum, e + 1)
                if e >= 2:
                    act.wait_ge(up_psum, e - 1)
                nc.scalar.activation(rows_t[e % 2][:, :], bank[e % 2][:, 0:CAP], ACT.Copy).then_inc(rows_t_ready, 1)
                act.wait_ge(up_psum, e + 1)
                if e >= 2:
                    act.wait_ge(down_psum, e - 1)
                pair = bank[2 + 2 * (e % 2)], bank[3 + 2 * (e % 2)]
                for f in range(FT):
                    n = P if f < FT - 1 else F_LAST
                    last = nc.scalar.activation(hidden[e % 2][0:n, f, :], pair[f // 2][0:n, (f % 2) * CAP:(f % 2 + 1) * CAP],
                                                ACT.Silu, bias=b_up[0:n, e // 2, f:f + 1])
                    last.then_inc(hidden_ready, 1)

            act_attention(act, att[1], 2)
            for b, src in ((B - 2, TX), (B - 1, score_bank[0])):
                act_tokens(act, 3, b, src)

        @block.vector
        def _(dve):
            chain = Chain(dve, dve_step)
            V = nc.vector

            dve.wait_ge(load["x0"], 16)
            dve_moments(chain, 0, x_in, 0)
            inverse_deviation(dve, chain, 0, 0)
            for t in range(TPB):
                dve_normalise(x_in, 0, t)
            dve.wait_ge(load["c32"], 16)
            dve_rotate_keys(dve, chain, att[0])
            dve_first_keys(dve, att[0])
            for b in range(1, B):
                dve.wait_ge(load[f"x{b}"], 16)
                dve_moments(chain, 0, x_in, b)
                if b == 1:
                    dve_values(dve, att[0])
            dve_attention(dve, chain, att[0], 0, x_add, lambda: None)

            inverse_deviation(dve, chain, 1, B - 1)
            for t in range(TILES - TPB, TILES):
                dve_normalise(x_mid, 1, t)
            dve.wait_ge(logit_psum, 1)
            lp = bank[5][:, :].rearrange("p (j b e) -> p b j e", j=TPB, b=B)[:, :, :, 0:EXPERTS]
            lg = logit[:, :, :].rearrange("p (b j) e -> p b j e", b=B)
            chain.step(V.tensor_reduce(l_max[:, :].rearrange("p (b j) -> p b j", b=B), lp, X_AXIS, ALU.max))
            chain.settle()
            V.tensor_tensor(lg, lp, l_max[:, :].rearrange("p (b j) -> p b j", b=B)[:, :, :, None]
                            .to_broadcast([P, B, TPB, EXPERTS]), ALU.subtract).then_inc(logit_ready, 1)
            dve.wait_ge(l_exp_ready, 1)
            chain.step(V.tensor_reduce(l_sum[:, :], l_exp[:, :, :], X_AXIS, ALU.add))
            chain.settle()
            chain.step(V.reciprocal(l_sum[:, :], l_sum[:, :]))
            chain.settle()
            V.tensor_tensor(weight[:, :, :], l_exp[:, :, :], l_sum[:, :, None].to_broadcast([P, TILES, EXPERTS]),
                            ALU.mult).then_inc(weight_ready, 1)
            dve.wait_ge(weight_ready, 1)

            dve.wait_ge(load["kbits"], 16)
            def bias_diagonal():
                dve.wait_ge(c_raw_ready, 1)
                for g in range(GEMMS):
                    V.tensor_scalar(c_one[:, g, :], c_raw[:, (g // 4) * D:(g // 4 + 1) * D], k32("crow")[:, g:g + 1],
                                    None, ALU.mult).then_inc(c_one_ready, 1)

            def bias_sum(first):
                dve.wait_ge(load["b2b"], 16)
                for g in range(first, first + 4):
                    dve.wait_ge(cb_psum, g + 1)
                    V.tensor_tensor(c21[:, g, :], bank[2 + g % 2][:, 0:D], b2b[:, g, :], ALU.add).then_inc(c21_ready, 1)

            between = {1: lambda: dve_rotate_keys(dve, chain, att[1]), 2: lambda: dve_first_keys(dve, att[1]),
                       3: lambda: dve_values(dve, att[1]), 4: bias_diagonal,
                       7: lambda: bias_sum(0), 8: lambda: bias_sum(4)}
            for s in range(STEPS):
                base = hit[s % 2][:, :, 0:1]
                step_bits = kbits[:, s * 8:(s + 1) * 8][:, None, :].to_broadcast([P, EXPERTS, 8])
                if s == 0:
                    chain.step(V.tensor_copy(cand[:, :, :], step_bits))
                    chain.step(V.memset(base, 0.0))
                else:
                    chain.step(V.tensor_tensor(cand[:, :, :], base.bitcast(I32).to_broadcast([P, EXPERTS, 8]), step_bits,
                                               ALU.bitwise_or))
                chain.settle()
                cf = cand[:, :, 1:8].bitcast(F32).rearrange("p e k -> p k e")
                V.tensor_tensor(above[:, :, :, :],
                                weight[:, None, :, :].to_broadcast([P, CANDS, TILES, EXPERTS]),
                                cf[:, :, None, :].to_broadcast([P, CANDS, TILES, EXPERTS]),
                                ALU.is_ge).then_inc(above_ready, 1)
                if s in between:
                    between[s]()
                dve.wait_ge(counted, s + 1)
                cnt = bank[1][:, 0:CANDS * EXPERTS].rearrange("p (k e) -> p e k", k=CANDS)
                chain.step(V.scalar_tensor_tensor(hit[s % 2][:, :, 1:8], cnt, float(CAP), cand[:, :, 1:8].bitcast(F32),
                                                  ALU.is_ge, ALU.mult))
                chain.settle()
                chain.step(V.tensor_reduce(hit[(s + 1) % 2][:, :, 0:1], hit[s % 2][:, :, :], X_AXIS, ALU.max))
                chain.settle()

            limit = hit[STEPS % 2][:, :, 0:1].rearrange("p e o -> p o e").to_broadcast([P, TILES, EXPERTS])
            chain.step(V.tensor_tensor(picks[:, 0, :, :], weight[:, :, :], limit, ALU.is_gt))
            chain.step(V.tensor_tensor(picks[:, 1, :, :], weight[:, :, :], limit, ALU.is_equal))
            chain.settle()
            V.tensor_tensor(pos_b[:, :, :], picks[:, 0, :, :], picks[:, 1, :, :], ALU.add).then_inc(picks_ready, 1)
            dve.wait_ge(prefix_ready, 1)
            pre = bank[5][:, 0:2 * TILES * EXPERTS].rearrange("p (k t e) -> p k t e", k=2, t=TILES)
            chain.step(V.tensor_copy(n_above[:, 0:EXPERTS], bank[6][:, 0:EXPERTS]))
            chain.step(V.tensor_tensor(pos_a[:, :, :], pre[:, 0, :, :], picks[:, 0, :, :], ALU.mult))
            chain.settle()
            chain.step(V.scalar_tensor_tensor(pos_a[:, :, :], pos_b[:, :, :], -4096.0, pos_a[:, :, :], ALU.mult, ALU.add))
            chain.settle()
            chain.step(V.tensor_tensor(pos_b[:, :, :], pre[:, 1, :, :],
                                       n_above[:, 0:EXPERTS][:, None, :].to_broadcast([P, TILES, EXPERTS]), ALU.add))
            chain.settle()
            chain.step(V.tensor_tensor(pos_b[:, :, :], pos_b[:, :, :], picks[:, 1, :, :], ALU.mult))
            chain.settle()
            chain.step(V.scalar_tensor_tensor(pos_i[:, :, :], pos_a[:, :, :], 4096.0, pos_b[:, :, :], ALU.add, ALU.add))
            chain.settle()
            chain.step(V.tensor_scalar(pos_d[:, 0, :, :], pos_i[:, :, :], 4, None, ALU.logical_shift_right))
            chain.step(V.tensor_scalar(pos_d[:, 1, :, :], pos_i[:, :, :], SLOT_B - 1, None, ALU.bitwise_and))
            chain.settle()
            chain.step(V.tensor_copy(pos_h[:, :, :, :], pos_d[:, :, :, :]))
            chain.settle()
            dve.wait_ge(load["c16"], 16)
            digits = k16("iota").rearrange("p (a e) -> p a e", e=EXPERTS)[:, None, :, :].to_broadcast([P, TILES, 16, EXPERTS])
            token = k16("token").rearrange("p (t a e) -> p t a e", t=TILES, a=16)
            for h in range(2):
                for i, dst in enumerate((onehot_a, onehot_b)):
                    sp_ = slice(8 * h, 8 * h + 8)
                    ins_ = V.tensor_tensor(dst[:, sp_, :, :],
                                           pos_h[:, i, sp_, :][:, :, None, :].to_broadcast([P, 8, 16, EXPERTS]),
                                           digits[:, sp_, :, :], ALU.is_equal)
                    chain.step(ins_)
                chain.settle()
                V.tensor_tensor(onehot_b[:, sp_, :, :], onehot_b[:, sp_, :, :], token[:, sp_, :, :],
                                ALU.mult).then_inc(onehot_ready, 1)
            dve.wait_ge(ids_psum, 1)
            V.tensor_tensor(ids[:, :], bank[6][:, 0:P], k32("expert"), ALU.mult).then_inc(ids_ready, 1)
            dve.wait_ge(place_psum, 1)
            V.tensor_copy(slot_token[:, :], bank[7][:, 0:HALVES * EXPERTS]).then_inc(slots_ready, 1)

            for e in range(EXPERTS):
                dve.wait_ge(down_psum, e + 1)
                for h in range(HALVES):
                    V.tensor_scalar(expert_out[:, e, h, :], bank[6 + e % 2][:, h * D:(h + 1) * D],
                                    rows[:, h * EXPERTS + e, D + e:D + e + 1], None, ALU.mult).then_inc(expert_ready, 1)

            for b in range(B):
                span = slice(TPB * b, TPB * (b + 1))
                dve.wait_ge(y_loaded[b], 32)
                V.tensor_tensor(x_in[:, span, :], x_in[:, span, :], x_add[:, span, :], ALU.add).then_inc(x2_ready, 1)
                dve.wait_ge(x2_ready, b + 1)
                dve_moments(chain, 2, x_in, b)
                if b == 0:
                    inverse_deviation(dve, chain, 2, 0)
                    for t in range(TPB):
                        dve_normalise(x_in, 2, t)

            def final(b):
                span = slice(TPB * b, TPB * (b + 1))
                dve.wait_ge(x3c_ready, 2 * (b + 1))
                dve.wait_ge(fin_psum, b + 1)
                V.tensor_tensor(xn[:, span, :].rearrange("p j d -> p (j d)"), fin_bank[b][:, :],
                                x_add[:, span, :].rearrange("p j d -> p (j d)"), ALU.add).then_inc(fin_ready, 1)

            def first_results():
                final(0)
                final(1)

            dve_attention(dve, chain, att[1], 2, x_in, first_results)

            dve.wait_ge(moments_ready[3], B)
            for t in range(TILES - TPB, TILES):
                V.tensor_scalar(xn[:, t, :], x_mid[:, t, :], moments[:, t, 0:1], None,
                                ALU.subtract).then_inc(xn_dve[3], 1)
            inverse_deviation(dve, chain, 3, B - 1)
            final(B - 2)
            dve.wait_ge(x3c_ready, 2 * B)
            dve.wait_ge(fin_psum, B)
            for j in range(TPB):
                t = TILES - TPB + j
                V.scalar_tensor_tensor(xn[:, t, :], fin_bank[B - 1][:, j * D:(j + 1) * D], rstd[:, t:t + 1], x_add[:, t, :],
                                       ALU.mult, ALU.add).then_inc(fin_ready, 1)

        @block.tensor
        def _(pe):
            pe_prepare_kv(pe, att[0], True)
            pe.wait_ge(load["csm"], 16)
            pe.wait_ge(ident_ready, 1)
            pe.wait_ge(att[0].v_bd_ready, 1)

            pe_attention(pe, att[0], 0, lambda: None)

            def route(b):
                pe.wait_ge(xn_t_ready[1], b + 1)
                return nc.tensor.matmul(bank[4][32 * b:32 * b + 32, :], wr[:, :],
                                        xn_t[:, TPB * b:TPB * (b + 1), :].rearrange("p j t -> p (j t)"),
                                        start=True, stop=True)

            pe.wait_ge(load["router"], 32)
            pe_transpose_tokens(pe, 1, B - 2, bank[B - 2])
            for b in range(B - 1):
                route(b)
            pe_transpose_tokens(pe, 1, B - 1, bank[B - 1])
            last = route(B - 1)
            last.then_inc(router_psum, 1)
            pe.wait_ge(logit_t_ready, 1)
            for j in range(TPB):
                last = nc.tensor.transpose(bank[5][:, j * P:(j + 1) * P], logit_t[:, j * P:(j + 1) * P], k32("ident"))
            last.then_inc(logit_psum, 1)

            def combined(g):
                if g == 0:
                    pe.wait_ge(load["w1"], 16)
                if g >= 2:
                    pe.wait_ge(w21_ready, g - 1)
                for k in range(OT):
                    last = nc.tensor.matmul(bank[2 + g % 2][:, 0:D], w1[:, g, k, :], w2t[:, g, k, :],
                                            start=(k == 0), stop=(k == OT - 1))
                last.then_inc(w21_psum, 1)

            def bias_rows():
                pe.wait_ge(load["b1c"], 16)
                pe.wait_ge(load["w2t"], 16)
                for half in range(2):
                    for k in range(OT):
                        for q in range(4):
                            g = 4 * half + q
                            last = nc.tensor.matmul(bank[7][32 * q:32 * q + 32, half * D:(half + 1) * D], b1c[:, k, :],
                                                    w2t[:, g, k, :], start=(k == 0), stop=(k == OT - 1),
                                                    skip_group_check=True)
                last.then_inc(c_psum, 1)

            def bias_everywhere(first):
                pe.wait_ge(w21_ready, GEMMS)
                for g in range(first, first + 4):
                    pe.wait_ge(c_one_ready, g + 1)
                    if g >= 2:
                        pe.wait_ge(c21_ready, g - 1)
                    nc.tensor.matmul(bank[2 + g % 2][:, 0:D], k32("ones"), c_one[:, g, :],
                                     start=True, stop=True).then_inc(cb_psum, 1)

            for s in range(STEPS):
                pe.wait_ge(above_ready, s + 1)
                for t in range(TILES):
                    last = nc.tensor.matmul(bank[1][:, 0:CANDS * EXPERTS], ksm("ones"), above[:, :, t, :],
                                            start=(t == 0), stop=(t == TILES - 1))
                last.then_inc(counted, 1)
                if s == 0:
                    pe_prepare_kv(pe, att[1], False)
                elif s == 1:
                    bias_rows()
                elif s < 6:
                    combined(2 * s - 4)
                    combined(2 * s - 3)
                elif s == 6:
                    bias_everywhere(0)
                elif s == 7:
                    bias_everywhere(4)

            pe.wait_ge(picks_ready, 1)
            pre = bank[5][:, 0:2 * TILES * EXPERTS].rearrange("p (k t e) -> p k t e", k=2, t=TILES)
            nc.tensor.matmul(pre, ksm("tri"), picks[:, :, :, :], start=True, stop=True)
            for t in range(TILES - 1):
                later = TILES - 1 - t
                nc.tensor.matmul(pre[:, :, t + 1:TILES, :], ksm("ones"),
                                 picks[:, :, t:t + 1, :].to_broadcast([P, 2, later, EXPERTS]),
                                 start=False, stop=True, skip_group_check=True)
            for t in range(TILES):
                last = nc.tensor.matmul(bank[6][:, 0:EXPERTS], ksm("ones"), picks[:, 0, t, :],
                                        start=(t == 0), stop=(t == TILES - 1))
            last.then_inc(prefix_ready, 1)
            for t in range(TILES):
                if t % 8 == 0:
                    pe.wait_ge(onehot_ready, t // 8 + 1)
                last = nc.tensor.matmul(bank[6][:, 0:P], onehot_b[:, t, :, :], onehot_a[:, t, :, :],
                                        start=(t == 0), stop=(t == TILES - 1))
            last.then_inc(ids_psum, 1)
            pe.wait_ge(ids_ready, 1)
            pe.wait_ge(c_raw_ready, 1)
            by_a = ids[:, :].rearrange("p (h l e) -> p l h e", h=HALVES, l=8)
            for l in range(8):
                last = nc.tensor.matmul(bank[7][:, 0:HALVES * EXPERTS].rearrange("p (h e) -> p h e", h=HALVES),
                                        k16("place")[:, l * P:(l + 1) * P], by_a[:, l, :, :],
                                        start=(l == 0), stop=(l == 7))
            last.then_inc(place_psum, 1)

            pe.wait_ge(load["w_up"], 32)
            pe.wait_ge(load["w_down"], 16)
            pe.wait_ge(c21_ready, GEMMS)

            def up(e):
                pe.wait_ge(gathered[e], 16 * HALVES)
                for h in range(HALVES):
                    last = nc.tensor.transpose(bank[e % 2][:, h * P:(h + 1) * P], rows[:, h * EXPERTS + e, 0:D],
                                               k32("ident"))
                last.then_inc(rows_psum, 1)
                pe.wait_ge(rows_t_ready, e + 1)
                if e >= 2:
                    pe.wait_ge(hidden_ready, FT * (e - 1))
                pair = bank[2 + 2 * (e % 2)], bank[3 + 2 * (e % 2)]
                for f in range(FT):
                    last = nc.tensor.matmul(pair[f // 2][:, (f % 2) * CAP:(f % 2 + 1) * CAP], w_up[:, e // 2, f, :],
                                            rows_t[e % 2][:, :], start=True, stop=True)
                last.then_inc(up_psum, 1)

            def down(e):
                if e >= 2:
                    pe.wait_ge(expert_ready, HALVES * (e - 1))
                pe.wait_ge(hidden_ready, FT * (e + 1))
                for h in range(HALVES):
                    for f in range(FT):
                        last = nc.tensor.matmul(bank[6 + e % 2][:, h * D:(h + 1) * D], hidden[e % 2][:, f, h * P:(h + 1) * P],
                                                w_down[:, e, f, :], start=(f == 0), stop=(f == FT - 1))
                last.then_inc(down_psum, 1)

            up(0)
            for e in range(EXPERTS):
                if e + 1 < EXPERTS:
                    up(e + 1)
                down(e)

            pe.wait_ge(expert_ready, HALVES * EXPERTS)

            def combined_ffn(b):
                pe.wait_ge(xn_t_ready[3], b + 1)
                for j in range(TPB):
                    t = TPB * b + j
                    last = nc.tensor.matmul(fin_bank[b][:, j * D:(j + 1) * D], xn_t[:, t, :], w21[:, t // TPG, :],
                                            start=True, stop=True)
                last.then_inc(fin_psum, 1)

            def first_products():
                combined_ffn(0)
                combined_ffn(1)

            pe_attention(pe, att[1], 2, first_products)
            pe_transpose_tokens(pe, 3, B - 2, TX)
            combined_ffn(B - 2)
            pe_transpose_tokens(pe, 3, B - 1, score_bank[0])
            combined_ffn(B - 1)


def _rope_table(heads, interleaved):
    f4 = np.float32
    hd = D // heads
    dim = hd // 2
    e = np.arange(D) % hd
    if interleaved:
        freq = np.exp(-np.arange(dim, dtype=f4) * f4(np.log(f4(10000.0))) / f4(dim)).astype(f4)
        which, sign = e // 2, np.where(e % 2, 1.0, -1.0)
    else:
        freq = (f4(1.0) / np.power(f4(10000.0), np.arange(0, hd, 2, dtype=f4) / f4(hd))).astype(f4)
        which, sign = e % dim, np.where(e < dim, -1.0, 1.0)
    ang = (np.arange(SEQ, dtype=f4)[None, :] * freq[which][:, None]).astype(f4)
    return np.stack([np.cos(ang), np.sin(ang) * sign[:, None]], axis=1).astype(f4)


def _swap(heads, interleaved):
    hd = D // heads
    c = np.arange(D)
    return c ^ 1 if interleaved else np.where(c % hd < hd // 2, c + hd // 2, c - hd // 2)


def _constants():
    p = np.arange(P)
    ke = np.arange(P)
    hd = [D // h for h in HEADS]
    c32 = np.zeros((P, C32_W), np.float32)

    def put(dst, table, name, value):
        dst[:, table[name][0]:table[name][1]] = value

    put(c32, C32, "ident", np.eye(P))
    for a in range(2):
        put(c32, C32, f"head{a}", p[:, None] // hd[a] == np.arange(HEADS[a])[None, :])
        put(c32, C32, f"vmask{a}", (ke[None, :] // hd[a]) % 4 == p[:, None] // KV)
    put(c32, C32, "expert", p[:, None] % EXPERTS == ke[None, :] % EXPERTS)
    gemm = np.arange(GEMMS)
    put(c32, C32, "crow", p[:, None] == (32 * (gemm % 4) + gemm)[None, :])
    put(c32, C32, "ones", 1.0)
    csm = np.zeros((P, CSM_W), np.float16)
    put(csm, CSM, "tri", p[:, None] < ke[None, :])
    put(csm, CSM, "ones", 1.0)
    for a in range(2):
        h = HEADS[a]
        col = np.arange(h * KV)
        put(csm, CSM, f"neg{a}", -1.0 * ((p[:, None] < 2 * h) & (p[:, None] % h == col[None, :] // KV)))
    c16 = np.zeros((P, C16_W), np.float16)
    put(c16, C16, "iota", np.repeat(np.arange(16), EXPERTS)[None, :])
    put(c16, C16, "token", (P * np.arange(TILES)[None, :, None] + p[:, None, None] + np.zeros((1, 1, P))).reshape(P, -1))
    place = np.zeros((P, 8, P))
    for l in range(8):
        place[:, l, :] = ke[None, :] == 16 * l + p[:, None] // EXPERTS
    put(c16, C16, "place", place.reshape(P, -1))
    shifts = BITS * (STEPS - 1 - np.arange(STEPS))
    bits = (np.arange(8)[None, :] << shifts[:, None]).reshape(1, -1).astype(np.int32)
    kbits = np.ascontiguousarray(np.broadcast_to(bits, (P, STEPS * 8)))
    return c32, csm, c16, kbits


def kernel(**inputs):
    import concourse.bacc as bacc
    from concourse.bass_utils import run_bass_kernel_spmd

    g = {k: np.asarray(v) for k, v in inputs.items()}
    c32, csm, c16, kbits = _constants()
    sw = [_swap(HEADS[0], True), _swap(HEADS[1], False)]

    def stack(ws):
        return np.ascontiguousarray(np.stack(ws, axis=1))

    wq, wk, wv, wo = (g[f"L0_xattn_w{n}"].T for n in "qkvo")
    wq1, wkv1, wo1 = g["L1_xattn_Wq"].T, g["L1_xattn_Wkv"].T, g["L1_xattn_Wout"].T
    bq, bk = g["L0_xattn_bq"], g["L0_xattn_bk"]
    pad_f = FT * P - F
    w_up = np.pad(g["L0_ffn_W_up"], ((0, 0), (0, 0), (0, pad_f))).reshape(GROUPS, D, FT, P).transpose(1, 0, 2, 3)
    b_up = np.pad(g["L0_ffn_b_up"], ((0, 0), (0, pad_f))).reshape(GROUPS, FT, P).transpose(2, 0, 1)
    w_down = np.pad(g["L0_ffn_W_down"], ((0, 0), (0, pad_f), (0, 0))).reshape(EXPERTS, FT, P, D).transpose(2, 0, 1, 3).copy()
    w_down[BIAS_ROW, :, FT - 1, :] = g["L0_ffn_b_down"]
    arrays = {
        "x": g["x"].reshape(N_TOK, D), "ctx": g["ctx_1024"].reshape(B * KV, D),
        "c32": c32, "csm": csm, "c16": c16, "kbits": kbits,
        "w_att0": stack([wq, wq[:, sw[0]], wk, wk[:, sw[0]], wv, wo]),
        "w_att1": stack([wq1, wq1[:, sw[1]], wkv1[:, :D], wkv1[:, :D][:, sw[1]], wkv1[:, D:], wo1]),
        "b_col": np.stack([bq, bq[sw[0]], bk, bk[sw[0]]], axis=1),
        "b_row": np.stack([g["L0_xattn_bv"], g["L0_xattn_bo"]]),
        "rope0": _rope_table(HEADS[0], True), "rope1": _rope_table(HEADS[1], False),
        "wr": np.pad(g["L0_ffn_Wr"], ((0, 0), (0, 32 - EXPERTS))),
        "br": np.tile(np.pad(g["L0_ffn_br"], (0, 32 - EXPERTS)), B).reshape(P, 1),
        "w_up": w_up, "b_up": b_up, "w_down": w_down,
        "w1": g["L1_ffn_W1"].reshape(GEMMS, OT, P, D).transpose(2, 0, 1, 3),
        "w2t": g["L1_ffn_W2"].transpose(0, 2, 1).reshape(GEMMS, OT, P, D).transpose(2, 0, 1, 3),
        "b1c": np.repeat(g["L1_ffn_b1"].reshape(GEMMS, OT, P).transpose(2, 1, 0), 1, axis=2),
        "b2": g["L1_ffn_b2"],
    }
    b1 = np.zeros((P, OT, 32), np.float32)
    b1[:, :, 0:GEMMS] = arrays["b1c"]
    arrays["b1c"] = b1

    nc = bacc.Bacc("TRN2", target_bir_lowering=False, num_devices=1)
    ins, feed = {}, {}
    for name, a in arrays.items():
        a = np.ascontiguousarray(a)
        feed[f"in_{name}"] = a
        ins[name] = nc.dram_tensor(f"in_{name}", a.shape, mybir.dt.from_np(a.dtype), kind="ExternalInput").ap()
    out = nc.dram_tensor("out", (N_TOK, D), F32, kind="ExternalOutput").ap()
    build(nc, ins, out)
    r = run_bass_kernel_spmd(nc, [feed], core_ids=[0])
    return r.results[0]["out"].reshape(B, SEQ, D)
```

```python
from contextlib import ExitStack

import numpy as np

import concourse.bass as bass
from concourse import mybir

B, SEQ, D = 4, 512, 128
KV = 32
P = 128
N_TOK = B * SEQ
TILES = N_TOK // P
TPB = SEQ // P
HEADS = (16, 8)
EXPERTS, GROUPS = 8, 4
CAP = N_TOK // EXPERTS
HALVES = CAP // P
F = int(D * 4 * (2.0 / 3.0))
FT = (F + P - 1) // P
BIAS_ROW = 96
F_LAST = BIAS_ROW
GEMMS, INTER = 8, 512
OT = INTER // P
TPG = TILES // GEMMS
BITS = 3
STEPS = 10
CANDS = (1 << BITS) - 1
ROW = D + EXPERTS
SLOT_B = 16
EPS = 1e-5
WARM0, WARM2 = 10, 13
WHILE_LN = 7
RSQRT_MAGIC = float(0x5F3759DF)

F32, F32R = mybir.dt.float32, mybir.dt.float32r
BF16, F16 = mybir.dt.bfloat16, mybir.dt.float16
I32, U32 = mybir.dt.int32, mybir.dt.uint32
ALU = mybir.AluOpType
ACT = mybir.ActivationFunctionType
X_AXIS = mybir.AxisListType.X


def columns(**widths):
    at, out = 0, {}
    for name, width in widths.items():
        out[name] = (at, at + width)
        at += width
    return out, at


C32, C32_W = columns(ident=P, head0=16, head1=8, vmask0=P, vmask1=P, expert=P, crow=8, ones=P)
CSM, CSM_W = columns(tri=P, ones=P, neg0=4 * P, neg1=2 * P)
C16, C16_W = columns(iota=P, token=TILES * P, place=8 * P)
W_Q, W_QS, W_K, W_KS, W_V, W_O = range(6)


class Chain:

    def __init__(self, engine, semaphore):
        self.engine, self.semaphore, self.count = engine, semaphore, 0

    def step(self, instruction):
        instruction.then_inc(self.semaphore, 1)
        self.count += 1

    def settle(self):
        self.engine.wait_ge(self.semaphore, self.count)


def build(nc, ins, out):
    with ExitStack() as ctx:
        def sb(name, shape, dt=F32):
            return ctx.enter_context(nc.sbuf_tensor(name, shape, dt))

        def sem(name):
            return ctx.enter_context(nc.semaphore(name))

        bank = [ctx.enter_context(nc.psum_tensor(f"bank{i}", [P, 512], F32)) for i in range(8)]
        TX = bank[0]
        ring = bank[1:4]
        score_bank = bank[4:6]
        ctx_bank, sum_bank = bank[6], bank[7]
        last_ctx, last_sum = ring[0], ring[1]
        w21_bank = TX, ring[2]
        fin_bank = ring[2], ctx_bank, score_bank[0], ring[0]

        dispatch = nc.dram_tensor("dispatch_rows", [N_TOK, ROW], F32).ap()
        y_even = nc.dram_tensor("y_even", [N_TOK, D], F32).ap()
        y_odd = nc.dram_tensor("y_odd", [N_TOK, D], F32).ap()

        c32 = sb("c32", [P, C32_W])
        csm = sb("csm", [P, CSM_W], F16)
        ident_bf = sb("ident_bf", [P, P], BF16)
        c16 = sb("c16", [P, C16_W], F16)
        kbits = sb("kbits", [P, STEPS * 8], I32)

        def k32(name):
            return c32[:, C32[name][0]:C32[name][1]]

        def ksm(name):
            return csm[:, CSM[name][0]:CSM[name][1]]

        def k16(name):
            return c16[:, C16[name][0]:C16[name][1]]

        w_att = [sb(f"w_att{a}", [P, 6, D]) for a in range(2)]
        b_col = sb("b_col", [P, 4])
        b_row = sb("b_row", [P, 2, D])
        rope = [sb(f"rope{a}", [P, 2, SEQ]) for a in range(2)]
        ctx_rows = sb("ctx_rows", [P, D])
        ctx_t = sb("ctx_t", [P, B, 4, KV])
        wr = sb("wr", [P, 32])
        br = sb("br", [P, 1])
        w_up = sb("w_up", [P, GROUPS, FT, P])
        b_up = sb("b_up", [P, GROUPS, FT])
        w_down = sb("w_down", [P, EXPERTS, FT, D])
        w1 = sb("w1", [P, GEMMS, OT, D])
        w2t = sb("w2t", [P, GEMMS, OT, D])
        b1c = sb("b1c", [P, OT, 32])
        b2b = sb("b2b", [P, GEMMS, D])
        w21 = sb("w21", [P, GEMMS, D])
        c21 = sb("c21", [P, GEMMS, D])
        c_raw = sb("c_raw", [P, 2 * D])
        c_one = sb("c_one", [P, GEMMS, D])

        x_in = sb("x_in", [P, TILES, D])
        x_mid = sb("x_mid", [P, TILES, D])
        x_add = sb("x_add", [P, TILES, D])
        xn = sb("xn", [P, TILES, D])
        xn_t = sb("xn_t", [P, TILES, P])
        stats = sb("stats", [P, TILES, 6])
        moments = sb("moments", [P, TILES, 2])
        rstd = sb("rstd", [P, TILES])
        ln_a = sb("ln_a", [P, TILES])
        ln_v = sb("ln_v", [P, TILES])

        k_rot = sb("k_rot", [P, B, KV])
        k_a = sb("k_a", [P, B, KV])
        k_b = sb("k_b", [P, B, KV])
        k_bd = sb("k_bd", [P, B, 512])
        k_bdr = sb("k_bdr", [P, B, 512], F32R)
        v_raw = sb("v_raw", [P, B, D])
        v_bd = sb("v_bd", [P, B, D])
        q_a = sb("q_a", [P, SEQ])
        q_b = sb("q_b", [P, SEQ])
        q_t = [sb(f"q_t{i}", [P, SEQ]) for i in range(2)]
        q_tr = [sb(f"q_tr{i}", [P, SEQ], F32R) for i in range(2)]
        m_max = sb("m_max", [P, TPB, 16])
        m_hl = [sb(f"m_hl{i}", [P, TPB, 32], BF16) for i in range(2)]
        m_t = [sb(f"m_t{i}", [P, SEQ], BF16) for i in range(2)]
        probs_all = sb("probs", [P, 4, SEQ])
        probs = [probs_all[:, i, :] for i in range(4)]
        recip = sb("recip", [P, SEQ])
        att_t = [sb(f"att_t{i}", [P, SEQ]) for i in range(2)]

        logit_t = sb("logit_t", [P, SEQ])
        logit = sb("logit", [P, TILES, EXPERTS])
        l_max = sb("l_max", [P, TILES])
        l_exp = sb("l_exp", [P, TILES, EXPERTS])
        l_sum = sb("l_sum", [P, TILES])
        weight = sb("weight", [P, TILES, EXPERTS])
        cand = sb("cand", [P, EXPERTS, 8], I32)
        hit = [sb(f"hit{i}", [P, EXPERTS, 8]) for i in range(2)]
        above = sb("above", [P, CANDS, TILES, EXPERTS], BF16)
        picks = sb("picks", [P, 2, TILES, EXPERTS], BF16)
        n_above = sb("n_above", [P, TILES])
        pos_a = sb("pos_a", [P, TILES, EXPERTS])
        pos_b = sb("pos_b", [P, TILES, EXPERTS])
        pos_i = sb("pos_i", [P, TILES, EXPERTS], I32)
        pos_d = sb("pos_d", [P, 2, TILES, EXPERTS], I32)
        pos_h = sb("pos_h", [P, 2, TILES, EXPERTS], F16)
        onehot_a, onehot_b = (probs_all[:, 2 * i:2 * i + 2, :].rearrange("p a n -> p (a n)").bitcast(F16)
                              .rearrange("p (t a e) -> p t a e", t=TILES, a=16) for i in range(2))
        ids = sb("ids", [P, P], F16)
        slot_token = sb("slot_token", [P, HALVES * EXPERTS], I32)
        rows = (w1[:, :, :, :].rearrange("p g k d -> p (g k d)")[:, 0:EXPERTS * HALVES * ROW]
                .rearrange("p (c r) -> p c r", r=ROW))
        rows_t = [sb(f"rows_t{i}", [P, CAP]) for i in range(2)]
        hidden = [sb(f"hidden{i}", [P, FT, CAP]) for i in range(2)]
        expert_out = xn_t[:, :, :].rearrange("p (e h) d -> p e h d", h=HALVES)
        zero = sb("zero", [P, D])
        table_probe = sb("table_probe", [P, 1])

        load = {n: sem(f"load_{n}") for n in (
            "x0", "x1", "x2", "x3", "c32", "csm", "c16", "kbits", "w_att0", "w_att1", "b_col", "b_row",
            "rope0", "rope1", "ctx", "router", "w_up", "w_down", "w1", "w2t", "b1c", "b2b")}
        dve_step = sem("dve_step")
        pool_step = sem("pool_step")
        zeroed = sem("zeroed")
        moments_ready = [sem(f"moments_ready{n}") for n in range(4)]
        xn_dve = [sem(f"xn_dve{n}") for n in range(4)]
        xn_pool = [sem(f"xn_pool{n}") for n in range(4)]
        xn_psum = [sem(f"xn_psum{n}") for n in range(4)]
        xn_t_ready = [sem(f"xn_t_ready{n}") for n in range(4)]

        class Attention:

            def __init__(self, a):
                self.a, self.heads = a, HEADS[a]
                self.hg = self.heads // 4
                self.cols = 4 * D // self.heads
                self.k_bank = score_bank[1 - a]
                self.scale = float(D // self.heads) ** -0.5
                self.ctx_psum = sem(f"ctx_psum_{a}")
                self.ctx_t_ready = sem(f"ctx_t_ready_{a}")
                self.k_psum = sem(f"k_psum_{a}")
                self.k_rot_ready = sem(f"k_rot_ready_{a}")
                self.k_bd_dve = sem(f"k_bd_dve_{a}")
                self.k_bd_pool = sem(f"k_bd_pool_{a}")
                self.v_psum = sem(f"v_psum_{a}")
                self.v_raw_ready = sem(f"v_raw_ready_{a}")
                self.v_bd_ready = sem(f"v_bd_ready_{a}")
                self.ring_filled = sem(f"ring_filled_{a}")
                self.ring_read = sem(f"ring_read_{a}")
                self.q_ready = sem(f"q_ready_{a}")
                self.qr_ready = sem(f"qr_ready_{a}")
                self.m_ready = sem(f"m_ready_{a}")
                self.m_psum = sem(f"m_psum_{a}")
                self.m_t_ready = sem(f"m_t_ready_{a}")
                self.scores_ready = sem(f"scores_ready_{a}")
                self.probs_ready = sem(f"probs_ready_{a}")
                self.sum_ready = sem(f"sum_ready_{a}")
                self.ctx_ready = sem(f"ctx_ready_{a}")
                self.recip_ready = sem(f"recip_ready_{a}")
                self.att_ready = sem(f"att_ready_{a}")
                self.out_psum = sem(f"out_psum_{a}")
                self.resid_done = sem(f"resid_done_{a}")

        att = [Attention(0), Attention(1)]
        bo_added = sem("bo_added")
        ident_ready = sem("ident_ready")
        router_psum, logit_t_ready = sem("router_psum"), sem("logit_t_ready")
        logit_psum, logit_ready, l_exp_ready = sem("logit_psum"), sem("logit_ready"), sem("l_exp_ready")
        weight_ready = sem("weight_ready")
        above_ready, counted = sem("above_ready"), sem("counted")
        picks_ready, prefix_ready = sem("picks_ready"), sem("prefix_ready")
        onehot_ready, ids_psum, ids_ready, place_psum, slots_ready = (
            sem("onehot_ready"), sem("ids_psum"), sem("ids_ready"), sem("place_psum"), sem("slots_ready"))
        dispatched = [sem(f"dispatched{i}") for i in range(2)]
        y_init = sem("y_init")
        gathered = [sem(f"gathered{i}") for i in range(EXPERTS)]
        rows_psum, rows_t_ready = sem("rows_psum"), sem("rows_t_ready")
        up_psum, hidden_ready = sem("up_psum"), sem("hidden_ready")
        down_psum, expert_ready = sem("down_psum"), sem("expert_ready")
        added = [sem(f"added{i}") for i in range(2)]
        y_loaded = [sem(f"y_loaded{b}") for b in range(B)]
        x2_ready = sem("x2_ready")
        c_psum, c_raw_ready, c_one_ready, cb_psum, c21_ready = (
            sem("c_psum"), sem("c_raw_ready"), sem("c_one_ready"), sem("cb_psum"), sem("c21_ready"))
        w21_psum, w21_ready = sem("w21_psum"), sem("w21_ready")
        x3c_ready = sem("x3c_ready")
        fin_psum, fin_copied, fin_pool, fin_ready = (
            sem("fin_psum"), sem("fin_copied"), sem("fin_pool"), sem("fin_ready"))
        stored = sem("stored")

        def tok(ap):
            return ap.rearrange("(t p) d -> p t d", p=P)

        def wait_tokens_early(engine, n, b, j=TPB - 1):
            if b < 2:
                engine.wait_ge(xn_dve[n], TPB * b + j + 1)
            else:
                engine.wait_ge(xn_pool[n], b - 1)

        def wait_tokens_late(engine, n, b, j=TPB - 1):
            if b == B - 1:
                engine.wait_ge(xn_dve[n], j + 1)
            else:
                engine.wait_ge(xn_pool[n], b + 1)

        block = ctx.enter_context(nc.Block())

        @block.sync
        def _(sp):
            def get(dst, src, name):
                sp.dma_start(dst, src).then_inc(load[name], 16)

            def get_x(b):
                get(x_in[:, TPB * b:TPB * (b + 1), :], tok(ins["x"])[:, TPB * b:TPB * (b + 1), :], f"x{b}")

            get_x(0)
            get_x(1)
            get(c32[:, :], ins["c32"], "c32")
            get(w_att[0][:, :, :], ins["w_att0"], "w_att0")
            for b in range(2, B):
                get_x(b)
            get(csm[:, :], ins["csm"], "csm")
            get(b_row[:, :, :], ins["b_row"][None, :, :].to_broadcast([P, 2, D]), "b_row")
            get(wr[:, :], ins["wr"], "router")
            get(br[:, :], ins["br"], "router")
            get(rope[1][:, :, :], ins["rope1"], "rope1")
            get(w_att[1][:, :, :], ins["w_att1"], "w_att1")
            get(kbits[:, :], ins["kbits"], "kbits")
            get(b1c[:, :, :], ins["b1c"], "b1c")
            get(w2t[:, :, :, :], ins["w2t"], "w2t")
            get(w1[:, :, :, :], ins["w1"], "w1")
            get(b2b[:, :, :], ins["b2"][None, :, :].to_broadcast([P, GEMMS, D]), "b2b")
            get(c16[:, :], ins["c16"], "c16")
            get(w_up[:, :, :, :], ins["w_up"], "w_up")
            get(b_up[:, :, :], ins["b_up"], "w_up")
            get(w_down[:, :, :, :], ins["w_down"], "w_down")

            sp.wait_ge(zeroed, 1)
            sp.dma_start(tok(y_odd), zero[:, None, :].to_broadcast([P, TILES, D])).then_inc(y_init, 16)
            for b in range(B):
                span = slice(TPB * b, TPB * (b + 1))
                wait_tokens_late(sp, 1, b)
                sp.dma_start(tok(dispatch)[:, span, 0:D], xn[:, span, :]).then_inc(dispatched[0], 16)
                sp.wait_ge(att[0].resid_done, b + 1)
                sp.dma_start(tok(y_even)[:, span, :], x_mid[:, span, :]).then_inc(y_init, 16)
            sp.wait_ge(weight_ready, 1)
            sp.dma_start(tok(dispatch)[:, :, D:ROW], weight[:, :, :]).then_inc(dispatched[1], 16)
            sp.wait_ge(added[0], 16 * HALVES * EXPERTS // 2)
            sp.wait_ge(added[1], 16 * HALVES * EXPERTS // 2)
            for b in range(B):
                span = slice(TPB * b, TPB * (b + 1))
                sp.dma_start(x_in[:, span, :], tok(y_even)[:, span, :]).then_inc(y_loaded[b], 16)
                sp.dma_start(x_add[:, span, :], tok(y_odd)[:, span, :]).then_inc(y_loaded[b], 16)
            for b in range(B):
                if b < 2:
                    sp.wait_ge(fin_pool, b + 1)
                else:
                    sp.wait_ge(fin_ready, TPB * (b - 1))
                sp.dma_start(tok(out)[:, TPB * b:TPB * (b + 1), :], xn[:, TPB * b:TPB * (b + 1), :]).then_inc(stored, 16)
            sp.wait_ge(stored, 16 * B)

        def pe_prepare_kv(pe, L, first):
            W = w_att[L.a]
            pe.wait_ge(load[f"w_att{L.a}"], 16)
            if first:
                pe.wait_ge(load["ctx"], 16)
                pe.wait_ge(load["c32"], 16)
                nc.tensor.transpose(score_bank[0][:, 0:P], ctx_rows[:, :], k32("ident")).then_inc(L.ctx_psum, 1)
                pe.wait_ge(L.ctx_t_ready, 1)
            keys = ctx_t[:, :, 0, :]
            nc.tensor.matmul(L.k_bank[:, 0:P], W[:, W_K, :], keys, start=True, stop=True)
            nc.tensor.matmul(L.k_bank[:, P:2 * P], W[:, W_KS, :], keys, start=True, stop=True).then_inc(L.k_psum, 1)
            for b in range(B):
                last = nc.tensor.matmul(ctx_bank[:, b * P:(b + 1) * P], ctx_t[:, b, :, :], W[:, W_V, :],
                                        start=True, stop=True)
            last.then_inc(L.v_psum, 1)

        def dve_rotate_keys(dve, chain, L):
            cos = rope[L.a][:, 0, 0:KV][:, None, :].to_broadcast([P, B, KV])
            sin = rope[L.a][:, 1, 0:KV][:, None, :].to_broadcast([P, B, KV])
            kp = L.k_bank[:, 0:P].rearrange("p (b k) -> p b k", b=B)
            ks = L.k_bank[:, P:2 * P].rearrange("p (b k) -> p b k", b=B)
            dve.wait_ge(load[f"rope{L.a}"], 16)
            if L.a == 0:
                dve.wait_ge(load["b_col"], 16)
            dve.wait_ge(L.k_psum, 1)
            if L.a == 0:
                chain.step(nc.vector.scalar_tensor_tensor(k_a[:, :, :], kp, b_col[:, 2:3], cos, ALU.add, ALU.mult))
                chain.step(nc.vector.scalar_tensor_tensor(k_b[:, :, :], ks, b_col[:, 3:4], sin, ALU.add, ALU.mult))
            else:
                chain.step(nc.vector.tensor_tensor(k_a[:, :, :], kp, cos, ALU.mult))
                chain.step(nc.vector.tensor_tensor(k_b[:, :, :], ks, sin, ALU.mult))
            chain.settle()
            nc.vector.tensor_tensor(k_rot[:, :, :], k_a[:, :, :], k_b[:, :, :], ALU.add).then_inc(L.k_rot_ready, 1)

        def dve_first_keys(dve, L):
            dve.wait_ge(L.k_rot_ready, 1)
            for dst in (k_bdr, k_bd):
                spread_keys(nc.vector, L, 0, dst).then_inc(L.k_bd_dve, 1)

        def dve_values(dve, L):
            dve.wait_ge(L.v_psum, 1)
            vp = ctx_bank[:, :].rearrange("p (b e) -> p b e", b=B)
            mask = k32(f"vmask{L.a}")[:, None, :].to_broadcast([P, B, D])
            if L.a == 0:
                dve.wait_ge(load["b_row"], 16)
                nc.vector.tensor_tensor(v_raw[:, :, :], vp, b_row[:, 0:1, :].to_broadcast([P, B, D]),
                                        ALU.add).then_inc(L.v_raw_ready, 1)
                dve.wait_ge(L.v_raw_ready, 1)
                nc.vector.tensor_tensor(v_bd[:, :, :], v_raw[:, :, :], mask, ALU.mult).then_inc(L.v_bd_ready, 1)
            else:
                nc.vector.tensor_tensor(v_bd[:, :, :], vp, mask, ALU.mult).then_inc(L.v_bd_ready, 1)

        def spread_keys(engine, L, b, dst):
            o = dst[:, b, 0:L.heads * KV].rearrange("p (h k) -> p h k", h=L.heads)
            return engine.tensor_tensor(o, k_rot[:, b:b + 1, :].to_broadcast([P, L.heads, KV]),
                                        k32(f"head{L.a}")[:, :, None].to_broadcast([P, L.heads, KV]), ALU.mult)

        def pe_transpose_tokens(pe, n, b, dst):
            for j in range(TPB):
                (wait_tokens_late if n % 2 else wait_tokens_early)(pe, n, b, j)
                last = nc.tensor.transpose(dst[:, j * P:(j + 1) * P], xn[:, TPB * b + j, :], k32("ident"))
            last.then_inc(xn_psum[n], 1)

        def uses(L):
            return 2 + L.hg

        def use_q(L, b):
            return 2 if b == 1 else uses(L) * b

        def use_max(L, b):
            return 4 if b == 0 else uses(L) * b + 2

        def pe_fill(pe, L, u):
            if u >= 3:
                pe.wait_ge(L.ring_read, u - 2)
            return ring[u % 3]

        def pe_project_q(pe, L, n, b):
            W = w_att[L.a]
            pe_transpose_tokens(pe, n, b, TX)
            pe.wait_ge(xn_t_ready[n], b + 1)
            rhs = xn_t[:, TPB * b:TPB * (b + 1), :].rearrange("p j t -> p (j t)")
            for i, w in enumerate((W_Q, W_QS)):
                dst = pe_fill(pe, L, use_q(L, b) + i)
                nc.tensor.matmul(dst[:, :], W[:, w, :], rhs, start=True, stop=True).then_inc(L.ring_filled, 1)

        def pe_max_scores(pe, L, b, i):
            width = L.heads * KV
            per = 512 // width
            dst = pe_fill(pe, L, use_max(L, b) + i)
            pe.wait_ge(L.qr_ready, b + 1)
            for k in range(per):
                j = i * per + k
                last = nc.tensor.matmul(dst[:, k * width:(k + 1) * width], q_tr[b % 2][:, j * P:(j + 1) * P],
                                        k_bdr[:, b, 0:width], start=True, stop=True)
            last.then_inc(L.ring_filled, 1)

        def pe_transpose_maxima(pe, L, n, b):
            rows_m = 2 * L.heads
            if b == B - 1:
                pe.wait_ge(xn_t_ready[n + 1], 1)
            pe.wait_ge(L.m_ready, b + 1)
            mt = TX[:, :].bitcast(BF16)
            for j in range(TPB):
                last = nc.tensor.transpose(mt[0:rows_m, j * P:(j + 1) * P], m_hl[b % 2][:, j, 0:rows_m], ident_bf[:, :])
            last.then_inc(L.m_psum, 1)

        def pe_scores(pe, L, b, g):
            v = L.hg * b + g
            if g == 0:
                pe.wait_ge(L.q_ready, b + 1)
            if v >= 2:
                pe.wait_ge(L.probs_ready, v - 1)
            nc.tensor.matmul(score_bank[v % 2][:, :], k_bd[:, b, g * P:(g + 1) * P], q_t[b % 2][:, :],
                             start=True, stop=False)

        def pe_subtract_maxima(pe, L, b, g):
            if g == 0:
                pe.wait_ge(L.m_t_ready, b + 1)
            nc.tensor.matmul(score_bank[(L.hg * b + g) % 2][:, :], ksm(f"neg{L.a}")[:, g * P:(g + 1) * P], m_t[b % 2][:, :],
                             start=False, stop=True).then_inc(L.scores_ready, 1)

        def pe_values(pe, L, b):
            last_batch = b == B - 1
            if last_batch:
                pe.wait_ge(L.ring_read, uses(L) * B)
            for summing in (False, True):
                if summing:
                    dst = last_sum if last_batch else sum_bank
                    if 1 <= b < B - 1:
                        pe.wait_ge(L.resid_done, b)
                else:
                    dst = last_ctx if last_batch else ctx_bank
                    if 1 <= b < B - 1:
                        pe.wait_ge(L.att_ready, b)
                for g in range(L.hg):
                    pe.wait_ge(L.probs_ready, L.hg * b + g + 1)
                    w = (k32(f"vmask{L.a}")[:, 0:L.cols] if summing
                         else v_bd[:, b, g * L.cols:(g + 1) * L.cols])
                    last = nc.tensor.matmul(dst[g * L.cols:(g + 1) * L.cols, :], w, probs[(L.hg * b + g) % 4][:, :],
                                            start=True, stop=True)
                last.then_inc(L.sum_ready if summing else L.ctx_ready, 1)

        def pe_project_out(pe, L, b):
            pe.wait_ge(L.att_ready, b + 1)
            if b == B - 1:
                pe.wait_ge(L.resid_done, b)
            for j in range(TPB):
                last = nc.tensor.matmul(sum_bank[:, j * P:(j + 1) * P], att_t[b % 2][:, j * P:(j + 1) * P],
                                        w_att[L.a][:, W_O, :], start=True, stop=True)
            last.then_inc(L.out_psum, 1)

        def pe_attention(pe, L, n, aside):
            def keys_ready(b):
                if L.a == 0 and b == 0:
                    pe.wait_ge(L.k_bd_dve, 2)
                else:
                    pe.wait_ge(L.k_bd_pool, 2 * b if L.a == 0 else 2 * (b + 1))

            pe_project_q(pe, L, n, 0)
            pe_project_q(pe, L, n, 1)
            keys_ready(0)
            for i in range(L.hg):
                pe_max_scores(pe, L, 0, i)
            for g in range(2):
                pe_scores(pe, L, 0, g)
            pe.wait_ge(load["csm"], 16)
            pe.wait_ge(ident_ready, 1)
            for b in range(B):
                pe_transpose_maxima(pe, L, n, b)
                if b + 1 < B:
                    keys_ready(b + 1)
                for g in range(L.hg):
                    if b > 0 or g >= 2:
                        pe_scores(pe, L, b, g)
                    pe_subtract_maxima(pe, L, b, g)
                    if b + 1 < B:
                        pe_max_scores(pe, L, b + 1, g)
                if b == B - 1:
                    break
                if b >= 1:
                    pe_project_out(pe, L, b - 1)
                if b + 2 < B:
                    pe_project_q(pe, L, n, b + 2)
                else:
                    pe_transpose_tokens(pe, n + 1, b - 2, TX)
                if b == 0:
                    pe.wait_ge(L.v_bd_ready, 1)
                pe_values(pe, L, b)
            pe_values(pe, L, B - 1)
            pe_project_out(pe, L, B - 2)
            pe_transpose_tokens(pe, n + 1, 1, TX)
            aside()
            pe_project_out(pe, L, B - 1)

        def act_tokens(act, n, b, src):
            act.wait_ge(xn_psum[n], b + 1)
            nc.scalar.activation(xn_t[:, TPB * b:TPB * (b + 1), :].rearrange("p j t -> p (j t)"), src[:, :],
                                 ACT.Copy).then_inc(xn_t_ready[n], 1)

        def act_attention(act, L, n):
            def tokens(b):
                act_tokens(act, n, b, TX)

            def rounded_q(b):
                act.wait_ge(L.q_ready, b + 1)
                nc.scalar.activation(q_tr[b % 2][:, :], q_t[b % 2][:, :], ACT.Copy).then_inc(L.qr_ready, 1)

            tokens(0)
            tokens(1)
            rounded_q(0)
            rounded_q(1)
            for b in range(B):
                rows_m = 2 * L.heads
                act.wait_ge(L.m_psum, b + 1)
                nc.scalar.activation(m_t[b % 2][0:rows_m, :], TX[:, :].bitcast(BF16)[0:rows_m, 0:SEQ],
                                     ACT.Copy).then_inc(L.m_t_ready, 1)
                for g in range(L.hg):
                    v = L.hg * b + g
                    act.wait_ge(L.scores_ready, v + 1)
                    if v >= 4:
                        act.wait_ge(L.sum_ready, (v - 4) // L.hg + 1)
                    nc.scalar.activation(probs[v % 4][:, :], score_bank[v % 2][:, :], ACT.Exp,
                                         scale=L.scale).then_inc(L.probs_ready, 1)
                if b + 2 < B:
                    tokens(b + 2)
                    rounded_q(b + 2)
                else:
                    act_tokens(act, n + 1, b - 2, TX)

        def dve_attention(dve, chain, L, n, resid, early):
            cos, sin = rope[L.a][:, 0, :], rope[L.a][:, 1, :]

            def query(b):
                if b >= 1:
                    dve.wait_ge(L.q_ready, b)
                u = use_q(L, b)
                dve.wait_ge(L.ring_filled, u + 1)
                if L.a == 0:
                    nc.vector.scalar_tensor_tensor(q_a[:, :], ring[u % 3][:, :], b_col[:, 0:1], cos,
                                                   ALU.add, ALU.mult).then_inc(L.ring_read, 1)
                else:
                    nc.vector.tensor_tensor(q_a[:, :], ring[u % 3][:, :], cos, ALU.mult).then_inc(L.ring_read, 1)
                dve.wait_ge(L.ring_filled, u + 2)
                if L.a == 0:
                    nc.vector.scalar_tensor_tensor(q_b[:, :], ring[(u + 1) % 3][:, :], b_col[:, 1:2], sin,
                                                   ALU.add, ALU.mult).then_inc(L.ring_read, 1)
                else:
                    nc.vector.tensor_tensor(q_b[:, :], ring[(u + 1) % 3][:, :], sin, ALU.mult).then_inc(L.ring_read, 1)
                dve.wait_ge(L.ring_read, u + 2)
                nc.vector.tensor_tensor(q_t[b % 2][:, :], q_a[:, :], q_b[:, :], ALU.add).then_inc(L.q_ready, 1)

            def maximum(b):
                per = TPB // L.hg
                for i in range(L.hg):
                    u = use_max(L, b) + i
                    dve.wait_ge(L.ring_filled, u + 1)
                    nc.vector.tensor_reduce(m_max[:, i * per:(i + 1) * per, 0:L.heads],
                                            ring[u % 3][:, :].rearrange("p (j h k) -> p j h k", j=per, h=L.heads),
                                            X_AXIS, ALU.max).then_inc(L.ring_read, 1)
                dve.wait_ge(L.ring_read, use_max(L, b) + L.hg)
                hi, lo = m_hl[b % 2][:, :, 0:L.heads], m_hl[b % 2][:, :, L.heads:2 * L.heads]
                chain.step(nc.vector.tensor_copy(hi, m_max[:, :, 0:L.heads]))
                chain.settle()
                nc.vector.tensor_tensor(lo, m_max[:, :, 0:L.heads], hi, ALU.subtract).then_inc(L.m_ready, 1)

            def normalise(b):
                if b >= 1:
                    dve.wait_ge(L.att_ready, b)
                dve.wait_ge(L.sum_ready, b + 1)
                nc.vector.reciprocal(recip[:, :], (last_sum if b == B - 1 else sum_bank)[:, :]).then_inc(L.recip_ready, 1)
                dve.wait_ge(L.recip_ready, b + 1)
                dve.wait_ge(L.ctx_ready, b + 1)
                nc.vector.tensor_tensor(att_t[b % 2][:, :], (last_ctx if b == B - 1 else ctx_bank)[:, :], recip[:, :], ALU.mult).then_inc(L.att_ready, 1)

            def residual(b):
                dve.wait_ge(L.out_psum, b + 1)
                if L.a == 0:
                    dve.wait_ge(bo_added, b + 1)
                span = slice(TPB * b, TPB * (b + 1))
                nc.vector.tensor_tensor(x_mid[:, span, :].rearrange("p j d -> p (j d)"), sum_bank[:, :],
                                        resid[:, span, :].rearrange("p j d -> p (j d)"),
                                        ALU.add).then_inc(L.resid_done, 1)
                dve.wait_ge(L.resid_done, b + 1)
                dve_moments(chain, n + 1, x_mid, b)

            early(0)
            query(0)
            early(1)
            query(1)
            early(2)
            maximum(0)
            early(3)
            for b in range(B):
                if b + 1 < B:
                    maximum(b + 1)
                if 1 <= b < B - 1:
                    residual(b - 1)
                if b + 2 < B:
                    query(b + 2)
                normalise(b)
            residual(B - 2)
            residual(B - 1)

        def dve_moments(chain, n, x, b):
            for t in range(TPB * b, TPB * (b + 1)):
                chain.step(nc.vector.bn_stats(stats[:, t, :], x[:, t, :]))
            chain.settle()
            for t in range(TPB * b, TPB * (b + 1)):
                last = nc.vector.bn_aggr(moments[:, t, :], stats[:, t, :])
            last.then_inc(moments_ready[n], 1)

        def first_guess(engine, ops, chain, n, b, batches=1):
            span = slice(TPB * b, TPB * (b + batches))
            r, v = rstd[:, span], ln_v[:, span]
            engine.wait_ge(moments_ready[n], b + batches)
            chain.step(ops.tensor_scalar(v, moments[:, span, 1], EPS, None, ALU.add))
            chain.settle()
            chain.step(ops.tensor_scalar(r.bitcast(I32), v.bitcast(I32), -0.5, RSQRT_MAGIC, ALU.mult, ALU.add))
            chain.settle()
            return r, ln_a[:, span], v

        def inverse_deviation(dve, chain, n, b, batches=1):
            r, a, v = first_guess(dve, nc.vector, chain, n, b, batches)
            for _ in range(3):
                chain.step(nc.vector.scalar_tensor_tensor(a, r, -0.5, r, ALU.mult, ALU.mult))
                chain.settle()
                chain.step(nc.vector.tensor_tensor(a, a, v, ALU.mult))
                chain.settle()
                chain.step(nc.vector.scalar_tensor_tensor(r, a, 1.5, r, ALU.add, ALU.mult))
                chain.settle()

        def dve_normalise(x, n, t):
            nc.vector.tensor_scalar(xn[:, t, :], x[:, t, :], moments[:, t, 0:1], rstd[:, t:t + 1],
                                    ALU.subtract, ALU.mult).then_inc(xn_dve[n], 1)

        def pool_normalise(pool, chain, x, n, b):
            ops = nc.gpsimd
            span = slice(TPB * b, TPB * (b + 1))
            r, a, v = first_guess(pool, ops, chain, n, b)
            chain.step(ops.tensor_scalar(v, v, -0.5, None, ALU.mult))
            for _ in range(3):
                chain.step(ops.tensor_tensor(a, r, r, ALU.mult))
                chain.settle()
                chain.step(ops.tensor_tensor(a, a, v, ALU.mult))
                chain.settle()
                chain.step(ops.tensor_scalar(a, a, 1.5, None, ALU.add))
                chain.settle()
                chain.step(ops.tensor_tensor(r, r, a, ALU.mult))
                chain.settle()
            if n == 1 or n == 3:
                pool.wait_ge(xn_psum[n - 1], b + 1)
            chain.step(ops.tensor_tensor(xn[:, span, :], x[:, span, :],
                                         moments[:, span, 0:1].to_broadcast([P, TPB, D]), ALU.subtract))
            chain.settle()
            ops.tensor_tensor(xn[:, span, :], xn[:, span, :], rstd[:, span][:, :, None].to_broadcast([P, TPB, D]),
                              ALU.mult).then_inc(xn_pool[n], 1)

        @block.gpsimd
        def _(pool):
            chain = Chain(pool, pool_step)
            P_ = nc.gpsimd
            chain.step(P_.memset(m_t[0][:, :], 0.0))
            chain.step(P_.memset(m_t[1][:, :], 0.0))
            for i in range(2):
                chain.settle()
                chain.step(P_.memset(hidden[i][BIAS_ROW:P, FT - 1, :], 1.0))
            chain.settle()
            P_.memset(zero[:, :], 0.0).then_inc(zeroed, 1)

            def keys(L):
                pool.wait_ge(L.k_rot_ready, 1)
                for b in range(B):
                    for dst in (k_bdr, k_bd):
                        spread_keys(P_, L, b, dst).then_inc(L.k_bd_pool, 1)

            def bias_diagonal():
                pool.wait_ge(c_raw_ready, 1)
                for half in range(2):
                    P_.tensor_tensor(c_one[:, 4 * half:4 * half + 4, :],
                                     c_raw[:, half * D:(half + 1) * D][:, None, :].to_broadcast([P, 4, D]),
                                     k32("crow")[:, 4 * half:4 * half + 4][:, :, None].to_broadcast([P, 4, D]),
                                     ALU.mult).then_inc(c_one_ready, 1)

            pool.wait_ge(load["c32"], 16)
            pool.wait_ge(att[0].k_rot_ready, 1)
            for b in range(1, B):
                if b > 1:
                    pool_normalise(pool, chain, x_in, 0, b)
                for dst in (k_bdr, k_bd):
                    spread_keys(P_, att[0], b, dst).then_inc(att[0].k_bd_pool, 1)
            pool.wait_ge(load["b_row"], 16)
            for b in range(B):
                P_.tensor_tensor(x_add[:, TPB * b:TPB * (b + 1), :], x_in[:, TPB * b:TPB * (b + 1), :],
                                 b_row[:, 1:2, :].to_broadcast([P, TPB, D]), ALU.add).then_inc(bo_added, 1)

            for b in range(B - 1):
                pool_normalise(pool, chain, x_mid, 1, b)
            keys(att[1])
            bias_diagonal()

            def gather(e):
                if e == 0:
                    pool.wait_ge(slots_ready, 1)
                    pool.wait_ge(dispatched[0], 16 * B)
                    pool.wait_ge(dispatched[1], 16)
                for h in range(HALVES):
                    c = h * EXPERTS + e
                    P_.indirect_dma_start(
                        rows[:, c, :], None, dispatch,
                        bass.IndirectOffsetOnAxis(ap=slot_token[:, c:c + 1].bitcast(U32), axis=0)).then_inc(gathered[e], 16)

            def add(e):
                pool.wait_ge(expert_ready, HALVES * (e + 1))
                if e < 2:
                    pool.wait_ge(y_init, 16 * (B + 1))
                else:
                    pool.wait_ge(added[e % 2], 16 * HALVES * (e // 2))
                for h in range(HALVES):
                    c = h * EXPERTS + e
                    P_.indirect_dma_start(
                        y_odd if e % 2 else y_even,
                        bass.IndirectOffsetOnAxis(ap=slot_token[:, c:c + 1].bitcast(U32), axis=0),
                        expert_out[:, e, h, :], None, compute_op=ALU.add).then_inc(added[e % 2], 16)

            AHEAD = 6
            for e in range(AHEAD):
                gather(e)
            for e in range(EXPERTS):
                add(e)
                if e + AHEAD < EXPERTS:
                    gather(e + AHEAD)

            for b in range(2, B):
                pool_normalise(pool, chain, x_in, 2, b)
            def add_bias(b):
                P_.tensor_tensor(x_add[:, TPB * b:TPB * (b + 1), :].rearrange("p (g t) d -> p g t d", t=TPG),
                                 x_mid[:, TPB * b:TPB * (b + 1), :].rearrange("p (g t) d -> p g t d", t=TPG),
                                 c21[:, 2 * b:2 * b + 2, :][:, :, None, :].to_broadcast([P, 2, TPG, D]),
                                 ALU.add).then_inc(x3c_ready, 1)

            def final(b):
                span = slice(TPB * b, TPB * (b + 1))
                pool.wait_ge(fin_copied, b + 1)
                pool.wait_ge(x3c_ready, b + 1)
                P_.tensor_tensor(xn[:, span, :], xn[:, span, :], x_add[:, span, :], ALU.add).then_inc(fin_pool, 1)

            pool.wait_ge(c21_ready, 2)
            for b in range(2):
                pool_normalise(pool, chain, x_mid, 3, b)
                add_bias(b)
            pool.wait_ge(moments_ready[3], B - 1)
            pool.wait_ge(xn_psum[2], B - 1)
            span = slice(TPB * (B - 2), TPB * (B - 1))
            P_.tensor_tensor(xn[:, span, :], x_mid[:, span, :], moments[:, span, 0:1].to_broadcast([P, TPB, D]),
                             ALU.subtract).then_inc(xn_pool[3], 1)
            add_bias(B - 2)
            final(0)
            pool.wait_ge(att[1].resid_done, B)
            add_bias(B - 1)
            final(1)

        @block.scalar
        def _(act):
            def get(dst, src, name):
                act.dma_start(dst, src).then_inc(load[name], 16)

            def load_table(function):
                nc.scalar.activation(table_probe[:, :], zero[:, 0:1], function)

            get(ctx_rows[:, :], ins["ctx"], "ctx")
            get(rope[0][:, :, :], ins["rope0"], "rope0")
            get(b_col[:, :], ins["b_col"], "b_col")

            act.wait_ge(att[0].ctx_psum, 1)
            nc.scalar.activation(
                ctx_t[:, :, :, :],
                score_bank[0][:, 0:P].rearrange("p (b k) -> p b k", b=B)[:, :, None, :].to_broadcast([P, B, 4, KV]),
                ACT.Copy).then_inc(att[0].ctx_t_ready, 1)
            nc.scalar.activation(ident_bf[:, :], k32("ident"), ACT.Copy).then_inc(ident_ready, 1)
            act.wait_ge(zeroed, 1)
            load_table(ACT.Exp)
            act_attention(act, att[0], 0)

            def combined(g):
                act.wait_ge(w21_psum, g + 1)
                nc.scalar.activation(w21[:, g, :], w21_bank[g % 2][:, 0:D], ACT.Copy).then_inc(w21_ready, 1)

            for g in range(WHILE_LN):
                combined(g)
            act_tokens(act, 1, B - 2, ring[1])
            act_tokens(act, 1, B - 1, ring[0])
            act.wait_ge(load["router"], 32)
            act.wait_ge(router_psum, 1)
            nc.scalar.activation(logit_t[:, :], bank[4][:, :], ACT.Identity, bias=br[:, 0:1]).then_inc(logit_t_ready, 1)
            act.wait_ge(logit_ready, 1)
            nc.scalar.activation(l_exp[:, :, :], logit[:, :, :], ACT.Exp).then_inc(l_exp_ready, 1)

            act.wait_ge(c_psum, 2)
            nc.scalar.activation(c_raw[:, :], bank[7][:, 0:2 * D], ACT.Copy).then_inc(c_raw_ready, 1)
            for g in range(WHILE_LN, GEMMS):
                combined(g)
            load_table(ACT.Silu)
            for e in range(EXPERTS):
                act.wait_ge(rows_psum, e + 1)
                if e >= 2:
                    act.wait_ge(up_psum, e - 1)
                nc.scalar.activation(rows_t[e % 2][:, :], bank[e % 2][:, 0:CAP], ACT.Copy).then_inc(rows_t_ready, 1)
                act.wait_ge(up_psum, e + 1)
                if e >= 2:
                    act.wait_ge(down_psum, e - 1)
                pair = bank[2 + 2 * (e % 2)], bank[3 + 2 * (e % 2)]
                for f in range(FT):
                    n = P if f < FT - 1 else F_LAST
                    last = nc.scalar.activation(hidden[e % 2][0:n, f, :], pair[f // 2][0:n, (f % 2) * CAP:(f % 2 + 1) * CAP],
                                                ACT.Silu, bias=b_up[0:n, e // 2, f:f + 1])
                    last.then_inc(hidden_ready, 1)

            load_table(ACT.Exp)
            act_attention(act, att[1], 2)
            for b in range(2):
                act.wait_ge(fin_psum, b + 1)
                nc.scalar.activation(xn[:, TPB * b:TPB * (b + 1), :].rearrange("p j d -> p (j d)"), fin_bank[b][:, :],
                                     ACT.Copy).then_inc(fin_copied, 1)
            for b, src in ((B - 2, TX), (B - 1, score_bank[1])):
                act_tokens(act, 3, b, src)

        @block.vector
        def _(dve):
            chain = Chain(dve, dve_step)
            V = nc.vector

            dve.wait_ge(load["x0"], 16)
            dve_moments(chain, 0, x_in, 0)
            dve.wait_ge(load["x1"], 16)
            dve_moments(chain, 0, x_in, 1)
            inverse_deviation(dve, chain, 0, 0, 2)
            for t in range(2 * TPB):
                dve_normalise(x_in, 0, t)
            dve.wait_ge(load["c32"], 16)
            dve_rotate_keys(dve, chain, att[0])

            def early0(step):
                if step == 0:
                    dve_first_keys(dve, att[0])
                elif step == 1:
                    dve.wait_ge(load["x2"], 16)
                    dve_moments(chain, 0, x_in, 2)
                elif step == 2:
                    dve_values(dve, att[0])
                else:
                    dve.wait_ge(load["x3"], 16)
                    dve_moments(chain, 0, x_in, 3)

            dve_attention(dve, chain, att[0], 0, x_add, early0)

            inverse_deviation(dve, chain, 1, B - 1)
            for t in range(TILES - TPB, TILES):
                dve_normalise(x_mid, 1, t)
            dve.wait_ge(logit_psum, 1)
            lp = bank[5][:, :].rearrange("p (j b e) -> p b j e", j=TPB, b=B)[:, :, :, 0:EXPERTS]
            lg = logit[:, :, :].rearrange("p (b j) e -> p b j e", b=B)
            chain.step(V.tensor_reduce(l_max[:, :].rearrange("p (b j) -> p b j", b=B), lp, X_AXIS, ALU.max))
            chain.settle()
            V.tensor_tensor(lg, lp, l_max[:, :].rearrange("p (b j) -> p b j", b=B)[:, :, :, None]
                            .to_broadcast([P, B, TPB, EXPERTS]), ALU.subtract).then_inc(logit_ready, 1)
            dve.wait_ge(l_exp_ready, 1)
            chain.step(V.tensor_reduce(l_sum[:, :], l_exp[:, :, :], X_AXIS, ALU.add))
            chain.settle()
            chain.step(V.reciprocal(l_sum[:, :], l_sum[:, :]))
            chain.settle()
            V.tensor_tensor(weight[:, :, :], l_exp[:, :, :], l_sum[:, :, None].to_broadcast([P, TILES, EXPERTS]),
                            ALU.mult).then_inc(weight_ready, 1)
            dve.wait_ge(weight_ready, 1)

            dve.wait_ge(load["kbits"], 16)
            def bias_sum(half):
                dve.wait_ge(load["b2b"], 16)
                dve.wait_ge(cb_psum, half + 1)
                V.tensor_tensor(c21[:, 4 * half:4 * half + 4, :].rearrange("p g d -> p (g d)"), bank[half][:, :],
                                b2b[:, 4 * half:4 * half + 4, :].rearrange("p g d -> p (g d)"),
                                ALU.add).then_inc(c21_ready, 1)

            between = {0: lambda: dve_rotate_keys(dve, chain, att[1]), 1: lambda: dve_values(dve, att[1]),
                       STEPS - 1: lambda: bias_sum(0)}
            for s in range(STEPS):
                base = hit[s % 2][:, :, 0:1]
                step_bits = kbits[:, s * 8:(s + 1) * 8][:, None, :].to_broadcast([P, EXPERTS, 8])
                if s == 0:
                    chain.step(V.tensor_copy(cand[:, :, :], step_bits))
                    chain.step(V.memset(base, 0.0))
                else:
                    chain.step(V.tensor_tensor(cand[:, :, :], base.bitcast(I32).to_broadcast([P, EXPERTS, 8]), step_bits,
                                               ALU.bitwise_or))
                chain.settle()
                cf = cand[:, :, 1:8].bitcast(F32).rearrange("p e k -> p k e")
                for h in range(2):
                    half = slice(h * TILES // 2, (h + 1) * TILES // 2)
                    V.tensor_tensor(above[:, :, half, :],
                                    weight[:, None, half, :].to_broadcast([P, CANDS, TILES // 2, EXPERTS]),
                                    cf[:, :, None, :].to_broadcast([P, CANDS, TILES // 2, EXPERTS]),
                                    ALU.is_ge).then_inc(above_ready, 1)
                if s in between:
                    between[s]()
                dve.wait_ge(counted, s + 1)
                cnt = bank[2][:, 0:CANDS * EXPERTS].rearrange("p (k e) -> p e k", k=CANDS)
                chain.step(V.scalar_tensor_tensor(hit[s % 2][:, :, 1:8], cnt, float(CAP), cand[:, :, 1:8].bitcast(F32),
                                                  ALU.is_ge, ALU.mult))
                chain.settle()
                chain.step(V.tensor_reduce(hit[(s + 1) % 2][:, :, 0:1], hit[s % 2][:, :, :], X_AXIS, ALU.max))
                chain.settle()

            limit = hit[STEPS % 2][:, :, 0:1].rearrange("p e o -> p o e").to_broadcast([P, TILES, EXPERTS])
            chain.step(V.tensor_tensor(picks[:, 0, :, :], weight[:, :, :], limit, ALU.is_gt))
            chain.step(V.tensor_tensor(picks[:, 1, :, :], weight[:, :, :], limit, ALU.is_equal))
            chain.settle()
            V.tensor_tensor(pos_b[:, :, :], picks[:, 0, :, :], picks[:, 1, :, :], ALU.add).then_inc(picks_ready, 1)
            bias_sum(1)
            dve.wait_ge(prefix_ready, 1)
            pre = bank[5][:, 0:2 * TILES * EXPERTS].rearrange("p (k t e) -> p k t e", k=2, t=TILES)
            chain.step(V.tensor_copy(n_above[:, 0:EXPERTS], bank[6][:, 0:EXPERTS]))
            chain.step(V.tensor_tensor(pos_a[:, :, :], pre[:, 0, :, :], picks[:, 0, :, :], ALU.mult))
            chain.settle()
            chain.step(V.scalar_tensor_tensor(pos_a[:, :, :], pos_b[:, :, :], -4096.0, pos_a[:, :, :], ALU.mult, ALU.add))
            chain.settle()
            chain.step(V.tensor_tensor(pos_b[:, :, :], pre[:, 1, :, :],
                                       n_above[:, 0:EXPERTS][:, None, :].to_broadcast([P, TILES, EXPERTS]), ALU.add))
            chain.settle()
            chain.step(V.tensor_tensor(pos_b[:, :, :], pos_b[:, :, :], picks[:, 1, :, :], ALU.mult))
            chain.settle()
            chain.step(V.scalar_tensor_tensor(pos_i[:, :, :], pos_a[:, :, :], 4096.0, pos_b[:, :, :], ALU.add, ALU.add))
            chain.settle()
            chain.step(V.tensor_scalar(pos_d[:, 0, :, :], pos_i[:, :, :], 4, None, ALU.logical_shift_right))
            chain.step(V.tensor_scalar(pos_d[:, 1, :, :], pos_i[:, :, :], SLOT_B - 1, None, ALU.bitwise_and))
            chain.settle()
            chain.step(V.tensor_copy(pos_h[:, :, :, :], pos_d[:, :, :, :]))
            chain.settle()
            dve.wait_ge(load["c16"], 16)
            digits = k16("iota").rearrange("p (a e) -> p a e", e=EXPERTS)[:, None, :, :].to_broadcast([P, TILES, 16, EXPERTS])
            token = k16("token").rearrange("p (t a e) -> p t a e", t=TILES, a=16)
            for h in range(2):
                for i, dst in enumerate((onehot_a, onehot_b)):
                    sp_ = slice(8 * h, 8 * h + 8)
                    ins_ = V.tensor_tensor(dst[:, sp_, :, :],
                                           pos_h[:, i, sp_, :][:, :, None, :].to_broadcast([P, 8, 16, EXPERTS]),
                                           digits[:, sp_, :, :], ALU.is_equal)
                    chain.step(ins_)
                chain.settle()
                V.tensor_tensor(onehot_b[:, sp_, :, :], onehot_b[:, sp_, :, :], token[:, sp_, :, :],
                                ALU.mult).then_inc(onehot_ready, 1)
            dve.wait_ge(ids_psum, 1)
            V.tensor_tensor(ids[:, :], bank[6][:, 0:P], k32("expert"), ALU.mult).then_inc(ids_ready, 1)
            dve.wait_ge(place_psum, 1)
            V.tensor_copy(slot_token[:, :], bank[7][:, 0:HALVES * EXPERTS]).then_inc(slots_ready, 1)

            for e in range(EXPERTS):
                dve.wait_ge(down_psum, e + 1)
                for h in range(HALVES):
                    V.tensor_scalar(expert_out[:, e, h, :], bank[6 + e % 2][:, h * D:(h + 1) * D],
                                    rows[:, h * EXPERTS + e, D + e:D + e + 1], None, ALU.mult).then_inc(expert_ready, 1)

            def sum_up(b):
                span = slice(TPB * b, TPB * (b + 1))
                dve.wait_ge(y_loaded[b], 32)
                V.tensor_tensor(x_in[:, span, :], x_in[:, span, :], x_add[:, span, :], ALU.add).then_inc(x2_ready, 1)
                dve.wait_ge(x2_ready, b + 1)
                dve_moments(chain, 2, x_in, b)

            sum_up(0)
            sum_up(1)
            inverse_deviation(dve, chain, 2, 0, 2)
            for t in range(2 * TPB):
                dve_normalise(x_in, 2, t)

            def early2(step):
                if step == 0:
                    sum_up(2)
                elif step == 3:
                    sum_up(3)

            dve_attention(dve, chain, att[1], 2, x_in, early2)

            dve.wait_ge(moments_ready[3], B)
            for t in range(TILES - TPB, TILES):
                V.tensor_scalar(xn[:, t, :], x_mid[:, t, :], moments[:, t, 0:1], None,
                                ALU.subtract).then_inc(xn_dve[3], 1)
            inverse_deviation(dve, chain, 3, B - 2, 2)
            for b in (B - 2, B - 1):
                dve.wait_ge(x3c_ready, b + 1)
                dve.wait_ge(fin_psum, b + 1)
                for j in range(TPB):
                    t = TPB * b + j
                    V.scalar_tensor_tensor(xn[:, t, :], fin_bank[b][:, j * D:(j + 1) * D], rstd[:, t:t + 1],
                                           x_add[:, t, :], ALU.mult, ALU.add).then_inc(fin_ready, 1)

        @block.tensor
        def _(pe):
            def raise_clock(n):
                for _ in range(n):
                    nc.tensor.matmul(TX[:, 0:P], zero[:, :], zero[:, :], start=True, stop=True)

            pe.wait_ge(zeroed, 1)
            raise_clock(WARM0)
            pe_prepare_kv(pe, att[0], True)
            def combined(g):
                if g == 0:
                    pe.wait_ge(load["w1"], 16)
                    pe.wait_ge(load["w2t"], 16)
                    pe.wait_ge(xn_t_ready[1], 2)
                if g >= 2:
                    pe.wait_ge(w21_ready, g - 1)
                for k in range(OT):
                    last = nc.tensor.matmul(w21_bank[g % 2][:, 0:D], w1[:, g, k, :], w2t[:, g, k, :],
                                            start=(k == 0), stop=(k == OT - 1))
                last.then_inc(w21_psum, 1)

            pe_attention(pe, att[0], 0, lambda: combined(0))
            for g in range(1, WHILE_LN):
                combined(g)

            def route(b):
                pe.wait_ge(xn_t_ready[1], b + 1)
                return nc.tensor.matmul(bank[4][32 * b:32 * b + 32, :], wr[:, :],
                                        xn_t[:, TPB * b:TPB * (b + 1), :].rearrange("p j t -> p (j t)"),
                                        start=True, stop=True)

            pe.wait_ge(load["router"], 32)
            pe_transpose_tokens(pe, 1, B - 2, ring[1])
            for b in range(B - 1):
                route(b)
            pe_transpose_tokens(pe, 1, B - 1, ring[0])
            last = route(B - 1)
            last.then_inc(router_psum, 1)
            pe.wait_ge(logit_t_ready, 1)
            for j in range(TPB):
                last = nc.tensor.transpose(bank[5][:, j * P:(j + 1) * P], logit_t[:, j * P:(j + 1) * P], k32("ident"))
            last.then_inc(logit_psum, 1)
            pe_prepare_kv(pe, att[1], False)

            def bias_rows(half):
                pe.wait_ge(load["b1c"], 16)
                for k in range(OT):
                    for q in range(4):
                        g = 4 * half + q
                        last = nc.tensor.matmul(bank[7][32 * q:32 * q + 32, half * D:(half + 1) * D], b1c[:, k, :],
                                                w2t[:, g, k, :], start=(k == 0), stop=(k == OT - 1),
                                                skip_group_check=True)
                last.then_inc(c_psum, 1)

            def bias_everywhere(half):
                pe.wait_ge(w21_ready, GEMMS)
                pe.wait_ge(c_one_ready, half + 1)
                nc.tensor.matmul(bank[half][:, :], k32("ones"),
                                 c_one[:, 4 * half:4 * half + 4, :].rearrange("p g d -> p (g d)"),
                                 start=True, stop=True).then_inc(cb_psum, 1)

            for s in range(STEPS):
                for t in range(TILES):
                    if t % (TILES // 2) == 0:
                        pe.wait_ge(above_ready, 2 * s + 1 + t // (TILES // 2))
                    last = nc.tensor.matmul(bank[2][:, 0:CANDS * EXPERTS], ksm("ones"), above[:, :, t, :],
                                            start=(t == 0), stop=(t == TILES - 1))
                last.then_inc(counted, 1)
                if s < 2:
                    bias_rows(s)
                elif s < 2 + GEMMS - WHILE_LN:
                    combined(s - 2 + WHILE_LN)
                elif s >= STEPS - 2:
                    bias_everywhere(s - (STEPS - 2))

            pe.wait_ge(picks_ready, 1)
            pre = bank[5][:, 0:2 * TILES * EXPERTS].rearrange("p (k t e) -> p k t e", k=2, t=TILES)
            nc.tensor.matmul(pre, ksm("tri"), picks[:, :, :, :], start=True, stop=True)
            for t in range(TILES - 1):
                later = TILES - 1 - t
                nc.tensor.matmul(pre[:, :, t + 1:TILES, :], ksm("ones"),
                                 picks[:, :, t:t + 1, :].to_broadcast([P, 2, later, EXPERTS]),
                                 start=False, stop=True, skip_group_check=True)
            for t in range(TILES):
                last = nc.tensor.matmul(bank[6][:, 0:EXPERTS], ksm("ones"), picks[:, 0, t, :],
                                        start=(t == 0), stop=(t == TILES - 1))
            last.then_inc(prefix_ready, 1)
            for t in range(TILES):
                if t % 8 == 0:
                    pe.wait_ge(onehot_ready, t // 8 + 1)
                last = nc.tensor.matmul(bank[6][:, 0:P], onehot_b[:, t, :, :], onehot_a[:, t, :, :],
                                        start=(t == 0), stop=(t == TILES - 1))
            last.then_inc(ids_psum, 1)
            pe.wait_ge(ids_ready, 1)
            pe.wait_ge(c_raw_ready, 1)
            by_a = ids[:, :].rearrange("p (h l e) -> p l h e", h=HALVES, l=8)
            for l in range(8):
                last = nc.tensor.matmul(bank[7][:, 0:HALVES * EXPERTS].rearrange("p (h e) -> p h e", h=HALVES),
                                        k16("place")[:, l * P:(l + 1) * P], by_a[:, l, :, :],
                                        start=(l == 0), stop=(l == 7))
            last.then_inc(place_psum, 1)

            pe.wait_ge(load["w_up"], 32)
            pe.wait_ge(load["w_down"], 16)
            pe.wait_ge(c21_ready, 2)

            def up(e):
                pe.wait_ge(gathered[e], 16 * HALVES)
                for h in range(HALVES):
                    last = nc.tensor.transpose(bank[e % 2][:, h * P:(h + 1) * P], rows[:, h * EXPERTS + e, 0:D],
                                               k32("ident"))
                last.then_inc(rows_psum, 1)
                pe.wait_ge(rows_t_ready, e + 1)
                if e >= 2:
                    pe.wait_ge(hidden_ready, FT * (e - 1))
                pair = bank[2 + 2 * (e % 2)], bank[3 + 2 * (e % 2)]
                for f in range(FT):
                    last = nc.tensor.matmul(pair[f // 2][:, (f % 2) * CAP:(f % 2 + 1) * CAP], w_up[:, e // 2, f, :],
                                            rows_t[e % 2][:, :], start=True, stop=True)
                last.then_inc(up_psum, 1)

            def down(e):
                if e >= 2:
                    pe.wait_ge(expert_ready, HALVES * (e - 1))
                pe.wait_ge(hidden_ready, FT * (e + 1))
                for h in range(HALVES):
                    for f in range(FT):
                        last = nc.tensor.matmul(bank[6 + e % 2][:, h * D:(h + 1) * D], hidden[e % 2][:, f, h * P:(h + 1) * P],
                                                w_down[:, e, f, :], start=(f == 0), stop=(f == FT - 1))
                last.then_inc(down_psum, 1)

            up(0)
            for e in range(EXPERTS):
                if e + 1 < EXPERTS:
                    up(e + 1)
                down(e)

            pe.wait_ge(expert_ready, HALVES * EXPERTS)
            pe.wait_ge(moments_ready[2], 1)
            raise_clock(WARM2)

            def combined_ffn(b):
                pe.wait_ge(xn_t_ready[3], b + 1)
                if b == 1:
                    pe.wait_ge(att[1].att_ready, B - 1)
                for j in range(TPB):
                    t = TPB * b + j
                    last = nc.tensor.matmul(fin_bank[b][:, j * D:(j + 1) * D], xn_t[:, t, :], w21[:, t // TPG, :],
                                            start=True, stop=True)
                last.then_inc(fin_psum, 1)

            pe_attention(pe, att[1], 2, lambda: combined_ffn(0))
            combined_ffn(1)
            pe_transpose_tokens(pe, 3, B - 2, TX)
            combined_ffn(B - 2)
            pe_transpose_tokens(pe, 3, B - 1, score_bank[1])
            combined_ffn(B - 1)


def _rope_table(heads, interleaved):
    f4 = np.float32
    hd = D // heads
    dim = hd // 2
    e = np.arange(D) % hd
    if interleaved:
        freq = np.exp(-np.arange(dim, dtype=f4) * f4(np.log(f4(10000.0))) / f4(dim)).astype(f4)
        which, sign = e // 2, np.where(e % 2, 1.0, -1.0)
    else:
        freq = (f4(1.0) / np.power(f4(10000.0), np.arange(0, hd, 2, dtype=f4) / f4(hd))).astype(f4)
        which, sign = e % dim, np.where(e < dim, -1.0, 1.0)
    ang = (np.arange(SEQ, dtype=f4)[None, :] * freq[which][:, None]).astype(f4)
    return np.stack([np.cos(ang), np.sin(ang) * sign[:, None]], axis=1).astype(f4)


def _swap(heads, interleaved):
    hd = D // heads
    c = np.arange(D)
    return c ^ 1 if interleaved else np.where(c % hd < hd // 2, c + hd // 2, c - hd // 2)


def _constants():
    p = np.arange(P)
    ke = np.arange(P)
    hd = [D // h for h in HEADS]
    c32 = np.zeros((P, C32_W), np.float32)

    def put(dst, table, name, value):
        dst[:, table[name][0]:table[name][1]] = value

    put(c32, C32, "ident", np.eye(P))
    for a in range(2):
        put(c32, C32, f"head{a}", p[:, None] // hd[a] == np.arange(HEADS[a])[None, :])
        put(c32, C32, f"vmask{a}", (ke[None, :] // hd[a]) % 4 == p[:, None] // KV)
    put(c32, C32, "expert", p[:, None] % EXPERTS == ke[None, :] % EXPERTS)
    gemm = np.arange(GEMMS)
    put(c32, C32, "crow", p[:, None] == (32 * (gemm % 4) + gemm)[None, :])
    put(c32, C32, "ones", 1.0)
    csm = np.zeros((P, CSM_W), np.float16)
    put(csm, CSM, "tri", p[:, None] < ke[None, :])
    put(csm, CSM, "ones", 1.0)
    for a in range(2):
        h = HEADS[a]
        col = np.arange(h * KV)
        put(csm, CSM, f"neg{a}", -1.0 * ((p[:, None] < 2 * h) & (p[:, None] % h == col[None, :] // KV)))
    c16 = np.zeros((P, C16_W), np.float16)
    put(c16, C16, "iota", np.repeat(np.arange(16), EXPERTS)[None, :])
    put(c16, C16, "token", (P * np.arange(TILES)[None, :, None] + p[:, None, None] + np.zeros((1, 1, P))).reshape(P, -1))
    place = np.zeros((P, 8, P))
    for l in range(8):
        place[:, l, :] = ke[None, :] == 16 * l + p[:, None] // EXPERTS
    put(c16, C16, "place", place.reshape(P, -1))
    shifts = BITS * (STEPS - 1 - np.arange(STEPS))
    bits = (np.arange(8)[None, :] << shifts[:, None]).reshape(1, -1).astype(np.int32)
    kbits = np.ascontiguousarray(np.broadcast_to(bits, (P, STEPS * 8)))
    return c32, csm, c16, kbits


def kernel(**inputs):
    import concourse.bacc as bacc
    from concourse.bass_utils import run_bass_kernel_spmd

    g = {k: np.asarray(v) for k, v in inputs.items()}
    c32, csm, c16, kbits = _constants()
    sw = [_swap(HEADS[0], True), _swap(HEADS[1], False)]

    def stack(ws):
        return np.ascontiguousarray(np.stack(ws, axis=1))

    wq, wk, wv, wo = (g[f"L0_xattn_w{n}"].T for n in "qkvo")
    wq1, wkv1, wo1 = g["L1_xattn_Wq"].T, g["L1_xattn_Wkv"].T, g["L1_xattn_Wout"].T
    bq, bk = g["L0_xattn_bq"], g["L0_xattn_bk"]
    pad_f = FT * P - F
    w_up = np.pad(g["L0_ffn_W_up"], ((0, 0), (0, 0), (0, pad_f))).reshape(GROUPS, D, FT, P).transpose(1, 0, 2, 3)
    b_up = np.pad(g["L0_ffn_b_up"], ((0, 0), (0, pad_f))).reshape(GROUPS, FT, P).transpose(2, 0, 1)
    w_down = np.pad(g["L0_ffn_W_down"], ((0, 0), (0, pad_f), (0, 0))).reshape(EXPERTS, FT, P, D).transpose(2, 0, 1, 3).copy()
    w_down[BIAS_ROW, :, FT - 1, :] = g["L0_ffn_b_down"]
    arrays = {
        "x": g["x"].reshape(N_TOK, D), "ctx": g["ctx_1024"].reshape(B * KV, D),
        "c32": c32, "csm": csm, "c16": c16, "kbits": kbits,
        "w_att0": stack([wq, wq[:, sw[0]], wk, wk[:, sw[0]], wv, wo]),
        "w_att1": stack([wq1, wq1[:, sw[1]], wkv1[:, :D], wkv1[:, :D][:, sw[1]], wkv1[:, D:], wo1]),
        "b_col": np.stack([bq, bq[sw[0]], bk, bk[sw[0]]], axis=1),
        "b_row": np.stack([g["L0_xattn_bv"], g["L0_xattn_bo"]]),
        "rope0": _rope_table(HEADS[0], True), "rope1": _rope_table(HEADS[1], False),
        "wr": np.pad(g["L0_ffn_Wr"], ((0, 0), (0, 32 - EXPERTS))),
        "br": np.tile(np.pad(g["L0_ffn_br"], (0, 32 - EXPERTS)), B).reshape(P, 1),
        "w_up": w_up, "b_up": b_up, "w_down": w_down,
        "w1": g["L1_ffn_W1"].reshape(GEMMS, OT, P, D).transpose(2, 0, 1, 3),
        "w2t": g["L1_ffn_W2"].transpose(0, 2, 1).reshape(GEMMS, OT, P, D).transpose(2, 0, 1, 3),
        "b1c": np.repeat(g["L1_ffn_b1"].reshape(GEMMS, OT, P).transpose(2, 1, 0), 1, axis=2),
        "b2": g["L1_ffn_b2"],
    }
    b1 = np.zeros((P, OT, 32), np.float32)
    b1[:, :, 0:GEMMS] = arrays["b1c"]
    arrays["b1c"] = b1

    nc = bacc.Bacc("TRN2", target_bir_lowering=False, num_devices=1)
    ins, feed = {}, {}
    for name, a in arrays.items():
        a = np.ascontiguousarray(a)
        feed[f"in_{name}"] = a
        ins[name] = nc.dram_tensor(f"in_{name}", a.shape, mybir.dt.from_np(a.dtype), kind="ExternalInput").ap()
    out = nc.dram_tensor("out", (N_TOK, D), F32, kind="ExternalOutput").ap()
    build(nc, ins, out)
    r = run_bass_kernel_spmd(nc, [feed], core_ids=[0])
    return r.results[0]["out"].reshape(B, SEQ, D)
```
